# Optimizing a Trainium2 kernel written in Bass

```python
import numpy as np
import jax
import jax.numpy as jnp

def _softmax(x, axis=-1):
    return jax.nn.softmax(x, axis=axis)

def _gelu(x):
    return jax.nn.gelu(x, approximate=True)

def _silu(x):
    return jax.nn.silu(x)

def _sigmoid(x):
    return jax.nn.sigmoid(x)

def _layernorm(x, axis=-1, eps=1e-05):
    m = jnp.mean(x, axis=axis, keepdims=True)
    v = jnp.var(x, axis=axis, keepdims=True)
    return (x - m) / jnp.sqrt(v + eps)

def _scatter_add(tgt, idx, src, axis=0):
    return tgt.at[idx].add(src)

def _segment_sum(src, seg, n):
    return jax.ops.segment_sum(src, seg, n)
kernel_name = 'mk_sandwich_d2_jaxref_r8_1348fc'

def setup_inputs(seed: int=0):
    np.random.seed(seed)
    _w = jnp.asarray

    def _L0_attn_setup():
        import jax, jax.numpy as jnp
        import numpy as np
        DILATION_RATE = 4
        SEGMENT_SIZE = 64
        key = jax.random.key(seed)
        x = jax.random.normal(key, (4, 1024, 128), dtype=jnp.float32)
        return {'x': x}
    _L0_attn_in = _L0_attn_setup()

    def _L0_ffn_setup():
        import jax, jax.numpy as jnp
        import numpy as np
        IN_FEATURES = 128
        ACT_BITS = 4

        def _hadamard(size: int) -> np.ndarray:
            h = np.array([[1.0]], dtype=np.float64)
            while h.shape[0] < size:
                h = np.block([[h, h], [h, -h]])
            return (h / np.sqrt(size)).astype(np.float32)

        def _quantize_activations(x, bits=ACT_BITS):
            pos = 2 ** (bits - 1) - 1
            neg = 2 ** (bits - 1)
            scale = jnp.clip(jnp.max(jnp.abs(jax.lax.stop_gradient(x)), axis=-1, keepdims=True), 1e-05) / pos
            q = jnp.clip(jnp.round(x / scale), -neg, pos) * scale
            return x + jax.lax.stop_gradient(q - x)

        def _ternary_quantize_ste(w):
            scale = jnp.clip(jnp.mean(jnp.abs(jax.lax.stop_gradient(w)), axis=1, keepdims=True), 1e-05)
            n = w / scale
            tern = jnp.where(n > 0.5, 1.0, jnp.where(n < -0.5, -1.0, 0.0))
            q = tern * scale
            return w + jax.lax.stop_gradient(q - w)
        key = jax.random.key(seed)
        k1, k2 = jax.random.split(key)
        x = jax.random.normal(k1, (8, 1024, IN_FEATURES), dtype=jnp.float32)
        bound = 1.0 / np.sqrt(IN_FEATURES)
        weight = jax.random.uniform(k2, (128, IN_FEATURES), dtype=jnp.float32, minval=-bound, maxval=bound)
        return {'x': x, 'weight': weight}
    _L0_ffn_in = _L0_ffn_setup()

    def _L1_attn_setup():
        import jax, jax.numpy as jnp
        import numpy as np
        B, N, DIM = (4, 128, 128)
        HEADS, DH = (16, 64)
        INNER = HEADS * DH
        PROJ_H = max(16, DH // 8)
        TOP_K = 32
        TEMP = 1.0
        SCALE = DH ** (-0.5)
        LN_EPS = 1e-05

        def _soma_gate(token_feat, ln_g, ln_b, w1, b1, w2, b2):
            mu = token_feat.mean(axis=-1, keepdims=True)
            var = token_feat.var(axis=-1, keepdims=True)
            H = (token_feat - mu) * jax.lax.rsqrt(var + LN_EPS) * ln_g + ln_b
            h = jax.nn.gelu(H @ w1.T + b1, approximate=False)
            scores = (h @ w2.T + b2)[..., 0]
            scores = scores / (TEMP + 1e-12)
            topk_vals, topk_idx = jax.lax.top_k(scores, TOP_K)
            b_idx = jnp.arange(scores.shape[0])[:, None]
            scores = jnp.full_like(scores, -1000000000.0).at[b_idx, topk_idx].set(topk_vals)
            return jax.nn.sigmoid(scores)
        key = jax.random.key(seed)
        ks = jax.random.split(key, 9)
        s = 0.02
        return {'x': jax.random.normal(ks[0], (B, N, DIM), dtype=jnp.float32), 'w_qkv': jax.random.normal(ks[1], (3 * INNER, DIM), dtype=jnp.float32) * s, 'w_out': jax.random.normal(ks[2], (DIM, INNER), dtype=jnp.float32) * s, 'b_out': jnp.zeros((DIM,), dtype=jnp.float32), 'ln_g': jnp.ones((DH,), dtype=jnp.float32), 'ln_b': jnp.zeros((DH,), dtype=jnp.float32), 'w1': jax.random.normal(ks[3], (PROJ_H, DH), dtype=jnp.float32) * s, 'b1': jnp.zeros((PROJ_H,), dtype=jnp.float32), 'w2': jax.random.normal(ks[4], (1, PROJ_H), dtype=jnp.float32) * s, 'b2': jnp.zeros((1,), dtype=jnp.float32)}
    _L1_attn_in = _L1_attn_setup()

    def _L1_ffn_setup():
        import jax, jax.numpy as jnp
        import numpy as np
        N_HEADS = 16
        N_KV_HEADS = 4
        N_EMBD = 128
        HEAD_DIM = N_EMBD // N_HEADS
        N_EXPERTS = 8
        TOP_K = 2
        EPS = 1e-06

        def _rmsnorm(x, w):
            xf = x.astype(jnp.float32)
            n = xf * jax.lax.rsqrt(jnp.mean(xf * xf, axis=-1, keepdims=True) + EPS)
            return n.astype(x.dtype) * w

        def _gqa(x, wq, wk, wv, wo):
            B, S, C = x.shape
            n_rep = N_HEADS // N_KV_HEADS
            q = (x @ wq.T).reshape(B, S, N_HEADS, HEAD_DIM)
            k = (x @ wk.T).reshape(B, S, N_KV_HEADS, HEAD_DIM)
            v = (x @ wv.T).reshape(B, S, N_KV_HEADS, HEAD_DIM)
            k = jnp.repeat(k, n_rep, axis=2)
            v = jnp.repeat(v, n_rep, axis=2)
            scale = 1.0 / np.sqrt(HEAD_DIM).astype(np.float32)
            attn = jnp.einsum('bqhd,bkhd->bhqk', q, k) * scale
            causal = jnp.tril(jnp.ones((S, S), dtype=bool))
            attn = jnp.where(causal, attn, jnp.float32(-jnp.inf))
            attn = jax.nn.softmax(attn, axis=-1)
            out = jnp.einsum('bhqk,bkhd->bqhd', attn, v).reshape(B, S, C)
            return out @ wo.T

        def _moe(x, gate_w, expert_w):
            B, S, C = x.shape
            t = x.reshape(B * S, C)
            logits = t @ gate_w.T
            w, sel = jax.lax.top_k(logits, TOP_K)
            w = jax.nn.softmax(w.astype(jnp.float32), axis=1).astype(t.dtype)
            comb = jnp.sum(w[..., None] * jax.nn.one_hot(sel, N_EXPERTS, dtype=t.dtype), axis=1)
            out = jnp.zeros_like(t)
            for e in range(N_EXPERTS):
                out = out + comb[:, e, None] * (t @ expert_w[e].T)
            return out.reshape(B, S, C)
        key = jax.random.key(seed)
        ks = jax.random.split(key, 10)
        B, S, C = (4, 256, N_EMBD)
        s = 0.02
        return {'x': jax.random.normal(ks[0], (B, S, C), dtype=jnp.float32), 'attn_norm_w': jnp.ones((C,), dtype=jnp.float32), 'ffn_norm_w': jnp.ones((C,), dtype=jnp.float32), 'wq': jax.random.normal(ks[1], (C, C), dtype=jnp.float32) * s, 'wk': jax.random.normal(ks[2], (N_KV_HEADS * HEAD_DIM, C), dtype=jnp.float32) * s, 'wv': jax.random.normal(ks[3], (N_KV_HEADS * HEAD_DIM, C), dtype=jnp.float32) * s, 'wo': jax.random.normal(ks[4], (C, C), dtype=jnp.float32) * s, 'gate_w': jax.random.normal(ks[5], (N_EXPERTS, C), dtype=jnp.float32) * s, 'expert_w': jax.random.normal(ks[6], (N_EXPERTS, C, C), dtype=jnp.float32) * s}
    _L1_ffn_in = _L1_ffn_setup()
    _d = {'L0_attn_x': _L0_attn_in['x'], 'L0_ffn_weight': _L0_ffn_in['weight'], 'L1_attn_w_qkv': _L1_attn_in['w_qkv'], 'L1_attn_w_out': _L1_attn_in['w_out'], 'L1_attn_b_out': _L1_attn_in['b_out'], 'L1_attn_ln_g': _L1_attn_in['ln_g'], 'L1_attn_ln_b': _L1_attn_in['ln_b'], 'L1_attn_w1': _L1_attn_in['w1'], 'L1_attn_b1': _L1_attn_in['b1'], 'L1_attn_w2': _L1_attn_in['w2'], 'L1_attn_b2': _L1_attn_in['b2'], 'L1_ffn_attn_norm_w': _L1_ffn_in['attn_norm_w'], 'L1_ffn_ffn_norm_w': _L1_ffn_in['ffn_norm_w'], 'L1_ffn_wq': _L1_ffn_in['wq'], 'L1_ffn_wk': _L1_ffn_in['wk'], 'L1_ffn_wv': _L1_ffn_in['wv'], 'L1_ffn_wo': _L1_ffn_in['wo'], 'L1_ffn_gate_w': _L1_ffn_in['gate_w'], 'L1_ffn_expert_w': _L1_ffn_in['expert_w']}
    _x0 = _d['L0_attn_x']
    _d['L0_attn_x'] = jax.random.normal(jax.random.fold_in(jax.random.key(seed), 1), (8, 512, 128), dtype=_x0.dtype)
    del _x0
    return _d

def reference(L0_attn_x, L0_ffn_weight, L1_attn_w_qkv, L1_attn_w_out, L1_attn_b_out, L1_attn_ln_g, L1_attn_ln_b, L1_attn_w1, L1_attn_b1, L1_attn_w2, L1_attn_b2, L1_ffn_attn_norm_w, L1_ffn_ffn_norm_w, L1_ffn_wq, L1_ffn_wk, L1_ffn_wv, L1_ffn_wo, L1_ffn_gate_w, L1_ffn_expert_w):

    def _L0_attn_ref(x):
        import jax, jax.numpy as jnp
        import numpy as np
        DILATION_RATE = 4
        SEGMENT_SIZE = 64
        'LongNet-style dilated attention.\n\n            For each offset in range(dilation_rate): take the strided slice\n            x[:, offset::r, :], split it into segments of length `segment_size`,\n            run full softmax(q k^T / sqrt(d)) v attention inside each segment\n            (q=k=v=the slice; attention dim is the full d_model, matching how the\n            original feeds [B, n_seg, seg, d_model] to FlashAttention), scatter the\n            result back to the strided positions, and average the dilation heads\n            (softmax over uniform logits == 1/r weights).\n\n            Since seq_len % (r * segment_size) == 0, the r strided slices tile the\n            sequence exactly, so we vectorize over offsets with a single reshape:\n            position p = i*r + offset  ->  xr[:, i, offset, :].\n            '
        r, seg = (DILATION_RATE, SEGMENT_SIZE)
        B, S, D = x.shape
        n = S // r
        g = n // seg
        scale = 1.0 / jnp.sqrt(jnp.asarray(D, dtype=x.dtype))
        xs = x.reshape(B, g, seg, r, D)
        scores = jnp.einsum('bgqrd,bgkrd->brgqk', xs, xs) * scale
        probs = jax.nn.softmax(scores, axis=-1)
        out = jnp.einsum('brgqk,bgkrd->bgqrd', probs, xs)
        return out.reshape(B, S, D) / r

    def _L0_ffn_ref(x, weight):
        import jax, jax.numpy as jnp
        import numpy as np
        IN_FEATURES = 128
        ACT_BITS = 4

        def _hadamard(size: int) -> np.ndarray:
            h = np.array([[1.0]], dtype=np.float64)
            while h.shape[0] < size:
                h = np.block([[h, h], [h, -h]])
            return (h / np.sqrt(size)).astype(np.float32)

        def _quantize_activations(x, bits=ACT_BITS):
            pos = 2 ** (bits - 1) - 1
            neg = 2 ** (bits - 1)
            scale = jnp.clip(jnp.max(jnp.abs(jax.lax.stop_gradient(x)), axis=-1, keepdims=True), 1e-05) / pos
            q = jnp.clip(jnp.round(x / scale), -neg, pos) * scale
            return x + jax.lax.stop_gradient(q - x)

        def _ternary_quantize_ste(w):
            scale = jnp.clip(jnp.mean(jnp.abs(jax.lax.stop_gradient(w)), axis=1, keepdims=True), 1e-05)
            n = w / scale
            tern = jnp.where(n > 0.5, 1.0, jnp.where(n < -0.5, -1.0, 0.0))
            q = tern * scale
            return w + jax.lax.stop_gradient(q - w)
        H = jnp.asarray(_hadamard(IN_FEATURES))
        xh = x @ H
        xq = _quantize_activations(xh)
        wq = _ternary_quantize_ste(weight)
        return jnp.einsum('bsi,oi->bso', xq, wq)

    def _L1_attn_ref(x, w_qkv, w_out, b_out, ln_g, ln_b, w1, b1, w2, b2):
        import jax, jax.numpy as jnp
        import numpy as np
        B, N, DIM = (4, 128, 128)
        HEADS, DH = (16, 64)
        INNER = HEADS * DH
        PROJ_H = max(16, DH // 8)
        TOP_K = 32
        TEMP = 1.0
        SCALE = DH ** (-0.5)
        LN_EPS = 1e-05

        def _soma_gate(token_feat, ln_g, ln_b, w1, b1, w2, b2):
            mu = token_feat.mean(axis=-1, keepdims=True)
            var = token_feat.var(axis=-1, keepdims=True)
            H = (token_feat - mu) * jax.lax.rsqrt(var + LN_EPS) * ln_g + ln_b
            h = jax.nn.gelu(H @ w1.T + b1, approximate=False)
            scores = (h @ w2.T + b2)[..., 0]
            scores = scores / (TEMP + 1e-12)
            topk_vals, topk_idx = jax.lax.top_k(scores, TOP_K)
            b_idx = jnp.arange(scores.shape[0])[:, None]
            scores = jnp.full_like(scores, -1000000000.0).at[b_idx, topk_idx].set(topk_vals)
            return jax.nn.sigmoid(scores)
        Bx, Nx, _ = x.shape
        qkv = x @ w_qkv.T
        q, k, v = jnp.split(qkv, 3, axis=-1)
        to_heads = lambda t: t.reshape(Bx, Nx, HEADS, DH).transpose(0, 2, 1, 3)
        q, k, v = (to_heads(q), to_heads(k), to_heads(v))
        dots = jnp.einsum('bhid,bhjd->bhij', q, k) * SCALE
        q_mean = q.mean(axis=1)
        gate = _soma_gate(q_mean, ln_g, ln_b, w1, b1, w2, b2)
        dots = dots * (gate[:, None, :, None] * gate[:, None, None, :])
        attn = jax.nn.softmax(dots, axis=-1)
        out = jnp.einsum('bhij,bhjd->bhid', attn, v)
        out = out.transpose(0, 2, 1, 3).reshape(Bx, Nx, INNER)
        return out @ w_out.T + b_out

    def _L1_ffn_ref(x, attn_norm_w, ffn_norm_w, wq, wk, wv, wo, gate_w, expert_w):
        import jax, jax.numpy as jnp
        import numpy as np
        N_HEADS = 16
        N_KV_HEADS = 4
        N_EMBD = 128
        HEAD_DIM = N_EMBD // N_HEADS
        N_EXPERTS = 8
        TOP_K = 2
        EPS = 1e-06

        def _rmsnorm(x, w):
            xf = x.astype(jnp.float32)
            n = xf * jax.lax.rsqrt(jnp.mean(xf * xf, axis=-1, keepdims=True) + EPS)
            return n.astype(x.dtype) * w

        def _gqa(x, wq, wk, wv, wo):
            B, S, C = x.shape
            n_rep = N_HEADS // N_KV_HEADS
            q = (x @ wq.T).reshape(B, S, N_HEADS, HEAD_DIM)
            k = (x @ wk.T).reshape(B, S, N_KV_HEADS, HEAD_DIM)
            v = (x @ wv.T).reshape(B, S, N_KV_HEADS, HEAD_DIM)
            k = jnp.repeat(k, n_rep, axis=2)
            v = jnp.repeat(v, n_rep, axis=2)
            scale = 1.0 / np.sqrt(HEAD_DIM).astype(np.float32)
            attn = jnp.einsum('bqhd,bkhd->bhqk', q, k) * scale
            causal = jnp.tril(jnp.ones((S, S), dtype=bool))
            attn = jnp.where(causal, attn, jnp.float32(-jnp.inf))
            attn = jax.nn.softmax(attn, axis=-1)
            out = jnp.einsum('bhqk,bkhd->bqhd', attn, v).reshape(B, S, C)
            return out @ wo.T

        def _moe(x, gate_w, expert_w):
            B, S, C = x.shape
            t = x.reshape(B * S, C)
            logits = t @ gate_w.T
            w, sel = jax.lax.top_k(logits, TOP_K)
            w = jax.nn.softmax(w.astype(jnp.float32), axis=1).astype(t.dtype)
            comb = jnp.sum(w[..., None] * jax.nn.one_hot(sel, N_EXPERTS, dtype=t.dtype), axis=1)
            out = jnp.zeros_like(t)
            for e in range(N_EXPERTS):
                out = out + comb[:, e, None] * (t @ expert_w[e].T)
            return out.reshape(B, S, C)
        h = x + _gqa(_rmsnorm(x, attn_norm_w), wq, wk, wv, wo)
        out = h + _moe(_rmsnorm(h, ffn_norm_w), gate_w, expert_w)
        return out
    x = L0_attn_x
    x = x + _layernorm(_L0_attn_ref(_layernorm(x, axis=-1)), axis=-1)
    x = x + _layernorm(_L0_ffn_ref(_layernorm(x, axis=-1), L0_ffn_weight), axis=-1)
    x = x + _layernorm(_L1_attn_ref(_layernorm(x, axis=-1), L1_attn_w_qkv, L1_attn_w_out, L1_attn_b_out, L1_attn_ln_g, L1_attn_ln_b, L1_attn_w1, L1_attn_b1, L1_attn_w2, L1_attn_b2), axis=-1)
    x = x + _layernorm(_L1_ffn_ref(_layernorm(x, axis=-1), L1_ffn_attn_norm_w, L1_ffn_ffn_norm_w, L1_ffn_wq, L1_ffn_wk, L1_ffn_wv, L1_ffn_wo, L1_ffn_gate_w, L1_ffn_expert_w), axis=-1)
    return x

_drawn_inputs = setup_inputs


def setup_inputs(seed=0):
    import zlib

    import numpy as np

    out = dict(_drawn_inputs(seed))
    spreads = {'L1_attn_b_out': (0.0, 0.1),
     'L1_attn_ln_g': (1.0, 0.6),
     'L1_attn_ln_b': (0.0, 0.8),
     'L1_attn_b1': (0.0, 0.8),
     'L1_ffn_attn_norm_w': (1.0, 0.6),
     'L1_ffn_ffn_norm_w': (1.0, 0.6)}
    factors = {'L1_attn_w1': 8.0,
     'L1_attn_w2': 8.0,
     'L1_ffn_wq': 8.0,
     'L1_ffn_wk': 8.0,
     'L1_ffn_wv': 5.644,
     'L1_ffn_wo': 4.654}
    for name, (base, spread) in spreads.items():
        noise = np.random.default_rng([zlib.crc32(name.encode()), seed]).standard_normal(out[name].shape)
        drawn = base * np.exp(spread * noise) if base else spread * noise
        out[name] = jnp.asarray(drawn.astype(out[name].dtype))
    for name, factor in factors.items():
        out[name] = (out[name] * factor).astype(out[name].dtype)
    return out
```

```python
import concourse.bass as bass
from concourse import mybir
from contextlib import ExitStack

FP32 = mybir.dt.float32
BF16 = mybir.dt.bfloat16
ALU = mybir.AluOpType
ACT = mybir.ActivationFunctionType
AX = mybir.AxisListType

B, S, D = 8, 512, 128
R = 4
SEG = 64
TILES = B * R
CT = 8
CHUNKS = TILES // CT
DH, HEADS = 64, 16
PROJ = 16
TOP_K = 32
NSEL = 2 * TOP_K + 2
LOWEST = -3e38
HD4, KV4, NE = 8, 4, 8
KVD = KV4 * HD4
VW = 32
QT = S // 128
SLOTS = 6
PAIRS = ((0, 3, 0, 0), (3, 2, 0, 1), (5, 1, 0, 2))
PAIRW = 512 + 384 + 256 + 128
S_HEADS = (range(0, 3), range(3, 6), range(6, 9), range(9, 12), range(12, 15), range(15, 16), (), ())
S_DONE = 5
RMS_EPS = 1e-6
LN_EPS = 1e-5
ROUND = 12582912.0
POS = 7.0
NEG = -8.0


def wait_alone(eng, sem, count, unit=1):
    if not isinstance(count, int):
        count = eng.to_reg(count)
        eng.wait_ge(sem, unit)
    eng.wait_ge(sem, count)


class Phase:

    def __init__(self, nc, ctx, tag=""):
        self.nc, self.ctx, self.tag, self.all_sems = nc, ctx, tag, []

    def sb(self, name, shape, dt=FP32):
        return self.ctx.enter_context(self.nc.sbuf_tensor(self.tag + name, shape, dt))

    def ps(self, name, shape, dt=FP32):
        return self.ctx.enter_context(self.nc.psum_tensor(self.tag + name, shape, dt))

    def sem(self, name):
        self.all_sems.append(self.nc.alloc_semaphore(name=self.tag + name))
        return self.all_sems[-1]

    def close(self):
        self.nc.clear_and_free_semaphores(self.all_sems)
        self.nc.all_engine_barrier()

    def sems(self, names):
        return {n: self.sem(n) for n in names.split()}


def setup_phase(nc, top, dram):
    with ExitStack() as ctx:
        ph = Phase(nc, ctx, "su_")
        sm = ph.sems("loaded ident_bf tern_abs tern_scale tern_steps tern_low tern_full part1 rest1 part2 "
                     "rest2 parts parts_psum parts_out mean_w mean_w_out gate_w eps1 zeroed")
        w = ph.sb("w", [128, D])
        pos = ph.sb("pos", [128, D])
        low = ph.sb("low", [128, D])
        rest = ph.sb("rest", [128, 2, D])
        part = ph.sb("part", [128, 3, D], BF16)
        absum = ph.sb("absum", [128, 1])
        scale = ph.sb("scale", [128, 1])
        lim = ph.sb("lim", [128, 2])
        pt = ph.ps("pt", [128, 3, D], BF16)
        with nc.Block() as block:

            @block.sync
            def _(sp):
                sp.dma_start(w[:, :], dram["ffn_weight"]).then_inc(sm["loaded"], 16)
                sp.dma_start(top.ident[:, :], dram["ident"]).then_inc(sm["loaded"], 16)
                sp.dma_start(top.hadamard[:, :], dram["hadamard"]).then_inc(sm["loaded"], 16)
                sp.dma_start(top.w_qkvT[:, :], dram["w_qkvT"]).then_inc(sm["loaded"], 16)
                sp.dma_start(top.ln_gb[:, :], dram["ln_gb"]).then_inc(sm["loaded"], 16)
                sp.dma_start(top.w1T[:, :], dram["w1T"]).then_inc(sm["loaded"], 16)
                sp.dma_start(top.b1[:, :], dram["b1"]).then_inc(sm["loaded"], 16)
                sp.dma_start(top.w2T[:, :], dram["w2T"]).then_inc(sm["loaded"], 16)
                sp.dma_start(top.b2[:, :], dram["b2"]).then_inc(sm["loaded"], 16)
                for t, name in ((top.w_outT, "w_outT"), (top.qkv4T, "qkv4T"), (top.wo4T, "wo4T"),
                                (top.gate_expT, "gate_expT"), (top.norm_w, "norm_w"), (top.b_out, "b_out"),
                                (top.iota, "iota"), (top.iota_col, "iota_col"), (top.batch_rows, "batch_rows"),
                                (top.first_row, "first_row"), (top.lower_f, "lower"), (top.mask_f, "mask")):
                    sp.dma_start(t[:], dram[name]).then_inc(sm["loaded"], 16)

            @block.gpsimd
            def _(pool):
                nc.gpsimd.memset(top.ones_bf[:, :], 1.0)
                nc.gpsimd.memset(top.eps_rms[:, :], RMS_EPS)
                nc.gpsimd.memset(top.eps[:, :], LN_EPS).then_inc(sm["zeroed"], 1)
                for c in range(2):
                    nc.gpsimd.memset(top.expS[c][:, :, :], 0.0).then_inc(sm["zeroed"], 1)

            @block.vector
            def _(dve):
                dve.wait_ge(sm["loaded"], 16 * 21)
                nc.vector.tensor_copy(top.ident_bf[:, :], top.ident[:, :]).then_inc(sm["ident_bf"], 1)
                nc.vector.tensor_reduce(absum[:, :], w[:, :], AX.X, ALU.add, apply_absolute_value=True)\
                    .then_inc(sm["tern_abs"], 1)
                dve.wait_ge(sm["tern_abs"], 1)
                nc.vector.tensor_scalar(scale[:, :], absum[:, :], 1.0 / D, LN_EPS, ALU.mult, ALU.max)\
                    .then_inc(sm["tern_scale"], 1)
                dve.wait_ge(sm["tern_scale"], 1)
                nc.vector.tensor_scalar(lim[:, 0:1], scale[:, :], 0.5, None, ALU.mult)
                nc.vector.tensor_scalar(lim[:, 1:2], scale[:, :], -0.5, None, ALU.mult)\
                    .then_inc(sm["tern_steps"], 1)
                dve.wait_ge(sm["tern_steps"], 1)
                nc.vector.tensor_scalar(pos[:, :], w[:, :], lim[:, 0:1], scale[:, :], ALU.is_gt, ALU.mult)
                nc.vector.tensor_scalar(low[:, :], w[:, :], lim[:, 1:2], scale[:, :], ALU.is_lt, ALU.mult)\
                    .then_inc(sm["tern_low"], 1)
                dve.wait_ge(sm["tern_low"], 1)
                nc.vector.tensor_tensor(w[:, :], pos[:, :], low[:, :], ALU.subtract).then_inc(sm["tern_full"], 1)
                dve.wait_ge(sm["tern_full"], 1)
                nc.vector.tensor_copy(part[:, 0, :], w[:, :]).then_inc(sm["part1"], 1)
                dve.wait_ge(sm["part1"], 1)
                nc.vector.tensor_tensor(rest[:, 0, :], w[:, :], part[:, 0, :], ALU.subtract).then_inc(sm["rest1"], 1)
                dve.wait_ge(sm["rest1"], 1)
                nc.vector.tensor_copy(part[:, 1, :], rest[:, 0, :]).then_inc(sm["part2"], 1)
                dve.wait_ge(sm["part2"], 1)
                nc.vector.tensor_tensor(part[:, 2, :], rest[:, 0, :], part[:, 1, :], ALU.subtract)\
                    .then_inc(sm["parts"], 1)
                nc.vector.tensor_copy(top.lower[:, :], top.lower_f[:, :])
                nc.vector.tensor_copy(top.mask_bf[:, :], top.mask_f[:, :])
                nc.vector.tensor_copy(top.batch_rows_bf[:, :, :], top.batch_rows[:, :, :])
                nc.vector.tensor_scalar(top.qkv4T[:, :], top.qkv4T[:, :], top.norm_w[:, 0:1], None, ALU.mult)
                nc.vector.tensor_scalar(top.gate_expT[:, :], top.gate_expT[:, :], top.norm_w[:, 1:2], None, ALU.mult)
                nc.vector.tensor_reduce(
                    top.w_qmeanT[:, :], top.w_qkvT[:, 0:HEADS * DH].rearrange("p (h d) -> p d h", h=HEADS),
                    AX.X, ALU.add).then_inc(sm["mean_w"], 1)
                dve.wait_ge(sm["mean_w"], 1)
                nc.vector.tensor_scalar(top.w_qmeanT[:, :], top.w_qmeanT[:, :], 1.0 / HEADS, None, ALU.mult)
                dve.wait_ge(sm["parts_psum"], 1)
                nc.vector.tensor_copy(top.ternT[:, :, :], pt[:, :, :]).then_inc(sm["parts_out"], 1)

            @block.tensor
            def _(pe):
                pe.wait_ge(sm["ident_bf"], 1)
                pe.wait_ge(sm["parts"], 1)
                for j in range(3):
                    last = nc.tensor.transpose(pt[:, j, :], part[:, j, :], top.ident_bf[:, :])
                last.then_inc(sm["parts_psum"], 1)
        ph.close()


def dilated_and_ternary_phase(nc, top, dram):
    with ExitStack() as ctx:
        ph = Phase(nc, ctx, "a_")
        sm = ph.sems(
            "s1_std s1_ostd s1_orstd s2_std s2_ostd s3_std s3_qstd s1_stats s1_mv s1_rstd s1_norm s1_n s1_nT_psum s1_nT s1_scores s1_E s1_sum s1_O s1_ostats s1_omv "
            "s1_sq s1_var s1_onorm s1_y s1_x "
            "s2_stats s2_mv s2_rstd s2_norm s2_n s2_nT_psum s2_nT s2_xh s2_absmax s2_scale s2_rscale s2_ratio s2_q "
            "s2_qT_psum s2_qT s2_O s2_ostats s2_omv s2_sq s2_var s2_ors s2_ors2 s2_onorm s2_y s2_x s2_rounded "
            "s3_stats s3_mv s3_rstd s3_norm s3_n s3_nT_psum s3_nT s3_qm s3_qstats s3_qmv s3_qrstd s3_qnorm s3_z "
            "s3_zT_psum s3_H s3_pre s3_hidden s3_score_psum s3_score")
        x_in = [ph.sem(f"x_in{c}") for c in range(2)]
        n3_kept = [ph.sem(f"n3_kept{c}") for c in range(2)]
        score_kept = [ph.sem(f"score_kept{c}") for c in range(2)]
        two = range(2)
        n = [ph.sb(f"n{c}", [128, CT, D]) for c in two]
        nT = [ph.sb(f"nT{c}", [128, CT, D]) for c in two]
        y = [ph.sb(f"y{c}", [128, CT, D]) for c in two]
        ratio = y
        q = [ph.sb(f"q{c}", [128, CT, D], BF16) for c in two]
        qT = [ph.sb(f"qT{c}", [128, CT, D], BF16) for c in two]
        z = [ph.sb(f"z{c}", [128, CT, DH]) for c in two]
        HT = [ph.sb(f"HT{c}", [DH, CT * D]) for c in two]
        u = [ph.sb(f"u{c}", [PROJ, CT * D]) for c in two]
        score = [ph.sb(f"score{c}", [1, 2, D, R]) for c in two]
        st = [ph.sb(f"st{c}", [128, CT, 6]) for c in two]
        mv = [ph.sb(f"mv{c}", [128, CT, 2]) for c in two]
        rs = [ph.sb(f"rs{c}", [128, CT]) for c in two]
        nb = [ph.sb(f"nb{c}", [128, CT]) for c in two]
        den = [ph.sb(f"den{c}", [128, CT]) for c in two]
        std = [ph.sb(f"std{c}", [128, CT]) for c in two]
        tmp = [ph.sb(f"tmp{c}", [128, CT]) for c in two]
        sc = [ph.sb(f"sc{c}", [128, CT]) for c in two]
        PA = [ph.ps(f"PA{c}", [128, CT, D]) for c in two]
        PB = [ph.ps(f"PB{c}", [128, CT, D]) for c in two]
        X, N3 = top.X, top.N3
        expS = top.expS
        n_iter = CHUNKS // 2

        def chunk(i, c):
            return bass.ds((2 * i + c) * CT, CT)

        def counts(eng, i):
            return [2 * i + 1 + c for c in two]

        def rows(tile, k):
            return tile[:, k, :]

        with nc.Block() as block:

            @block.sync
            def _(sp):
                with sp.Fori(0, n_iter) as i:
                    for c in two:
                        sp.dma_start(X[:, chunk(i, c), :], dram["x"][:, chunk(i, c), :]).then_inc(x_in[c], 16)
                    done = counts(sp, i)
                    for c in two:
                        wait_alone(sp, sm["s3_n"], done[c])
                        sp.dma_start(N3[:, chunk(i, c), :], n[c][:, :, :]).then_inc(n3_kept[c], 16)
                    for c in two:
                        sp.wait_ge(sm["s3_score"], done[c])
                        sp.dma_start(dram["scores"][:, bass.ds((2 * i + c) * 2 * S, 2 * S)],
                                     score[c][:, :, :, :].rearrange("a b p r -> a (b p r)"))\
                            .then_inc(score_kept[c], 16)
                for c in two:
                    sp.wait_ge(n3_kept[c], 16 * n_iter)
                    sp.wait_ge(score_kept[c], 16 * n_iter)

            @block.vector
            def _(dve):
                def stats(src, c, k, s, width=D):
                    for t in range(CT):
                        last = nc.vector.bn_stats(st[c][:, t, :], src(t))
                    last.then_inc(sm[s + "stats"], 1)
                    wait_alone(dve, sm[s + "stats"], k)
                    for t in range(CT):
                        last = nc.vector.bn_aggr(mv[c][:, t, :], st[c][:, t, :])
                    last.then_inc(sm[s + "mv"], 1)
                    wait_alone(dve, sm[s + "mv"], k)

                def norm_scalars(c, k, s):
                    dve.wait_ge(sm[s + "std"], k)
                    nc.vector.reciprocal(rs[c][:, :], std[c][:, :]).then_inc(sm[s + "rstd"], 1)
                    dve.wait_ge(sm[s + "rstd"], k)
                    nc.vector.scalar_tensor_tensor(out=nb[c][:, :], in0=mv[c][:, :, 0], scalar=-1.0,
                                                   in1=rs[c][:, :], op0=ALU.mult, op1=ALU.mult)\
                        .then_inc(sm[s + "norm"], 1)

                with dve.Fori(0, n_iter) as i:
                    done = counts(dve, i)
                    for c in two:
                        wait_alone(dve, x_in[c], 16 * i + 16, 16)
                        stats(lambda t: X[:, (2 * i + c) * CT + t, :], c, done[c], "s1_")
                    for c in two:
                        norm_scalars(c, done[c], "s1_")
                    for c in two:
                        dve.wait_ge(sm["s1_nT_psum"], done[c])
                        nc.vector.tensor_copy(nT[c][:, :, :], PA[c][:, :, :]).then_inc(sm["s1_nT"], 1)
                    for c in two:
                        dve.wait_ge(sm["s1_E"], done[c])
                        for a in range(2):
                            last = nc.vector.tensor_reduce(
                                den[c][SEG * a:SEG * a + SEG, :],
                                expS[c][SEG * a:SEG * a + SEG, :, SEG * a:SEG * a + SEG], AX.X, ALU.add)
                        last.then_inc(sm["s1_sum"], 1)
                        dve.wait_ge(sm["s1_sum"], done[c])
                        nc.vector.scalar_tensor_tensor(out=tmp[c][:, :], in0=den[c][:, :], scalar=float(R * R),
                                                       in1=den[c][:, :], op0=ALU.mult, op1=ALU.mult)\
                            .then_inc(sm["s1_sq"], 1)
                    for c in two:
                        dve.wait_ge(sm["s1_O"], done[c])
                        stats(lambda t: PA[c][:, t, :], c, done[c], "s1_o")
                        dve.wait_ge(sm["s1_sq"], done[c])
                        nc.vector.scalar_tensor_tensor(out=tmp[c][:, :], in0=tmp[c][:, :], scalar=LN_EPS,
                                                       in1=mv[c][:, :, 1], op0=ALU.mult, op1=ALU.add)\
                            .then_inc(sm["s1_var"], 1)
                    for c in two:
                        norm_scalars(c, done[c], "s1_o")
                    for c in two:
                        wait_alone(dve, sm["s1_x"], done[c])
                        stats(lambda t: X[:, (2 * i + c) * CT + t, :], c, done[c], "s2_")
                    for c in two:
                        norm_scalars(c, done[c], "s2_")
                    for c in two:
                        dve.wait_ge(sm["s2_xh"], done[c])
                        nc.vector.tensor_reduce(den[c][:, :], PB[c][:, :, :], AX.X, ALU.max,
                                                apply_absolute_value=True).then_inc(sm["s2_absmax"], 1)
                        dve.wait_ge(sm["s2_absmax"], done[c])
                        nc.vector.tensor_scalar(sc[c][:, :], den[c][:, :], LN_EPS, 1.0 / POS, ALU.max, ALU.mult)\
                            .then_inc(sm["s2_scale"], 1)
                        dve.wait_ge(sm["s2_scale"], done[c])
                        nc.vector.reciprocal(den[c][:, :], sc[c][:, :]).then_inc(sm["s2_rscale"], 1)
                        dve.wait_ge(sm["s2_rscale"], done[c])
                        nc.vector.tensor_tensor(ratio[c][:, :, :], PB[c][:, :, :],
                                                den[c][:, :].rearrange("p (t o) -> p t o", o=1).broadcast_to([128, CT, D]),
                                                ALU.mult).then_inc(sm["s2_ratio"], 1)
                        dve.wait_ge(sm["s2_ratio"], done[c])
                        nc.vector.tensor_scalar(q[c][:, :, :], ratio[c][:, :, :], ROUND, ROUND,
                                                ALU.add, ALU.subtract).then_inc(sm["s2_q"], 1)
                    for c in two:
                        dve.wait_ge(sm["s2_qT_psum"], done[c])
                        nc.vector.tensor_scalar(qT[c][:, :, :], PA[c][:, 0:CT // 2, :].bitcast(BF16), POS, NEG,
                                                ALU.min, ALU.max).then_inc(sm["s2_qT"], 1)
                        nc.vector.tensor_tensor(tmp[c][:, :], sc[c][:, :], sc[c][:, :], ALU.mult)\
                            .then_inc(sm["s2_sq"], 1)
                    for c in two:
                        dve.wait_ge(sm["s2_O"], done[c])
                        stats(lambda t: PB[c][:, t, :], c, done[c], "s2_o")
                        dve.wait_ge(sm["s2_sq"], done[c])
                        nc.vector.tensor_tensor(tmp[c][:, :], tmp[c][:, :], mv[c][:, :, 1], ALU.mult)\
                            .then_inc(sm["s2_var"], 1)
                    for c in two:
                        dve.wait_ge(sm["s2_ostd"], done[c])
                        nc.vector.reciprocal(tmp[c][:, :], std[c][:, :]).then_inc(sm["s2_ors"], 1)
                        dve.wait_ge(sm["s2_ors"], done[c])
                        nc.vector.tensor_tensor(rs[c][:, :], tmp[c][:, :], sc[c][:, :], ALU.mult)\
                            .then_inc(sm["s2_ors2"], 1)
                        dve.wait_ge(sm["s2_ors2"], done[c])
                        nc.vector.scalar_tensor_tensor(out=nb[c][:, :], in0=mv[c][:, :, 0], scalar=-1.0,
                                                       in1=rs[c][:, :], op0=ALU.mult, op1=ALU.mult)\
                            .then_inc(sm["s2_onorm"], 1)
                    for c in two:
                        wait_alone(dve, sm["s2_x"], done[c])
                        stats(lambda t: X[:, (2 * i + c) * CT + t, :], c, done[c], "s3_")
                    for c in two:
                        norm_scalars(c, done[c], "s3_")
                    for c in two:
                        dve.wait_ge(sm["s3_qm"], done[c])
                        stats(lambda t: PB[c][:, t, 0:DH], c, done[c], "s3_q")
                    for c in two:
                        norm_scalars(c, done[c], "s3_q")

            @block.scalar
            def _(act):
                def normalise(dst, src, c, k):
                    for t in range(CT):
                        last = nc.scalar.activation(dst(t), src(t), ACT.Identity, bias=nb[c][:, t:t + 1],
                                                    scale=rs[c][:, t:t + 1])
                    return last

                def deviations(s, src, ready, done, eps=True):
                    for c in two:
                        act.wait_ge(sm[ready], done[c])
                        nc.scalar.activation(std[c][:, :], src(c), ACT.Sqrt,
                                             bias=top.eps[:, :] if eps else 0.0).then_inc(sm[s + "std"], 1)

                variance = lambda c: mv[c][:, :, 1]
                with act.Fori(0, n_iter) as i:
                    done = counts(act, i)
                    deviations("s1_", variance, "s1_mv", done)
                    for c in two:
                        act.wait_ge(sm["s1_norm"], done[c])
                        normalise(lambda t: n[c][:, t, :], lambda t: X[:, (2 * i + c) * CT + t, :], c, done[c])\
                            .then_inc(sm["s1_n"], 1)
                    for c in two:
                        act.wait_ge(sm["s1_scores"], done[c])
                        for a in range(2):
                            seg = slice(SEG * a, SEG * a + SEG)
                            last = nc.scalar.activation(expS[c][seg, :, seg], PB[c][seg, :, seg], ACT.Exp,
                                                        scale=float(D) ** -0.5)
                        last.then_inc(sm["s1_E"], 1)
                    deviations("s1_o", lambda c: tmp[c][:, :], "s1_var", done, eps=False)
                    for c in two:
                        act.wait_ge(sm["s1_onorm"], done[c])
                        normalise(lambda t: y[c][:, t, :], lambda t: PA[c][:, t, :], c, done[c])\
                            .then_inc(sm["s1_y"], 1)
                    deviations("s2_", variance, "s2_mv", done)
                    for c in two:
                        wait_alone(act, sm["s2_norm"], done[c])
                        normalise(lambda t: n[c][:, t, :], lambda t: X[:, (2 * i + c) * CT + t, :], c, done[c])\
                            .then_inc(sm["s2_n"], 1)
                    for c in two:
                        act.wait_ge(sm["s2_nT_psum"], done[c])
                        nc.scalar.activation(nT[c][:, :, :], PA[c][:, :, :], ACT.Copy).then_inc(sm["s2_nT"], 1)
                    deviations("s2_o", lambda c: tmp[c][:, :], "s2_var", done)
                    for c in two:
                        act.wait_ge(sm["s2_onorm"], done[c])
                        normalise(lambda t: y[c][:, t, :], lambda t: PB[c][:, t, :], c, done[c])\
                            .then_inc(sm["s2_y"], 1)
                    deviations("s3_", variance, "s3_mv", done)
                    for c in two:
                        wait_alone(act, sm["s3_norm"], done[c])
                        normalise(lambda t: n[c][:, t, :], lambda t: X[:, (2 * i + c) * CT + t, :], c, done[c])\
                            .then_inc(sm["s3_n"], 1)
                    for c in two:
                        act.wait_ge(sm["s3_nT_psum"], done[c])
                        nc.scalar.activation(nT[c][:, :, :], PA[c][:, :, :], ACT.Copy).then_inc(sm["s3_nT"], 1)
                    deviations("s3_q", variance, "s3_qmv", done)
                    for c in two:
                        act.wait_ge(sm["s3_qnorm"], done[c])
                        normalise(lambda t: z[c][:, t, :], lambda t: PB[c][:, t, 0:DH], c, done[c])\
                            .then_inc(sm["s3_z"], 1)
                    for c in two:
                        act.wait_ge(sm["s3_zT_psum"], done[c])
                        nc.scalar.activation(HT[c][:, :], PA[c][0:DH, :, :].rearrange("p t d -> p (t d)"),
                                             ACT.Identity, bias=top.ln_gb[:, 1:2], scale=top.ln_gb[:, 0:1])\
                            .then_inc(sm["s3_H"], 1)
                    for c in two:
                        act.wait_ge(sm["s3_pre"], done[c])
                        nc.scalar.activation(u[c][:, :], PB[c][0:PROJ, :, :].rearrange("p t d -> p (t d)"), ACT.Gelu,
                                             bias=top.b1[:, :]).then_inc(sm["s3_hidden"], 1)
                    for c in two:
                        act.wait_ge(sm["s3_score_psum"], done[c])
                        nc.scalar.activation(score[c][:, :, :, :],
                                             PA[c][0:1, :, :].rearrange("a (b r) p -> a b p r", b=2),
                                             ACT.Identity, bias=top.b2[:, :]).then_inc(sm["s3_score"], 1)

            @block.gpsimd
            def _(pool):
                with pool.Fori(0, n_iter) as i:
                    done = counts(pool, i)
                    for s in ("s1", "s2"):
                        for c in two:
                            wait_alone(pool, sm[s + "_y"], done[c])
                            nc.gpsimd.tensor_tensor(X[:, chunk(i, c), :], X[:, chunk(i, c), :], y[c][:, :, :],
                                                    ALU.add).then_inc(sm[s + "_x"], 1)

            @block.tensor
            def _(pe):
                def transposes(dst, src, ident, c):
                    for t in range(CT):
                        last = nc.tensor.transpose(dst(t), src(t), ident)
                    return last

                def mm(out, lhsT, rhs, start=True, stop=True):
                    return nc.tensor.matmul(out, lhsT, rhs, start=start, stop=stop)

                with pe.Fori(0, n_iter) as i:
                    done = counts(pe, i)
                    for c in two:
                        pe.wait_ge(sm["s1_n"], done[c])
                        transposes(lambda t: PA[c][:, t, :], lambda t: n[c][:, t, :], top.ident[:, :], c)\
                            .then_inc(sm["s1_nT_psum"], 1)
                    for c in two:
                        pe.wait_ge(sm["s1_nT"], done[c])
                        for t in range(CT):
                            last = mm(PB[c][:, t, :], nT[c][:, t, :], nT[c][:, t, :])
                        last.then_inc(sm["s1_scores"], 1)
                    for c in two:
                        pe.wait_ge(sm["s1_E"], done[c])
                        for t in range(CT):
                            last = mm(PA[c][:, t, :], expS[c][:, t, :], n[c][:, t, :])
                        last.then_inc(sm["s1_O"], 1)
                    for c in two:
                        pe.wait_ge(sm["s2_n"], done[c])
                        transposes(lambda t: PA[c][:, t, :], lambda t: n[c][:, t, :], top.ident[:, :], c)\
                            .then_inc(sm["s2_nT_psum"], 1)
                    for c in two:
                        pe.wait_ge(sm["s2_nT"], done[c])
                        for t in range(CT):
                            last = mm(PB[c][:, t, :], nT[c][:, t, :], top.hadamard[:, :])
                        last.then_inc(sm["s2_xh"], 1)
                    for c in two:
                        pe.wait_ge(sm["s2_q"], done[c])
                        PAb = PA[c][:, 0:CT // 2, :].bitcast(BF16).rearrange("p a (b d) -> p (a b) d", b=2)
                        transposes(lambda t: PAb[:, t, :], lambda t: q[c][:, t, :], top.ident_bf[:, :], c)\
                            .then_inc(sm["s2_qT_psum"], 1)
                    for c in two:
                        pe.wait_ge(sm["s2_qT"], done[c])
                        for t in range(CT):
                            for j in range(3):
                                last = mm(PB[c][:, t, :], qT[c][:, t, :], top.ternT[:, j, :], j == 0, j == 2)
                        last.then_inc(sm["s2_O"], 1)
                    for c in two:
                        pe.wait_ge(sm["s3_n"], done[c])
                        transposes(lambda t: PA[c][:, t, :], lambda t: n[c][:, t, :], top.ident[:, :], c)\
                            .then_inc(sm["s3_nT_psum"], 1)
                    for c in two:
                        pe.wait_ge(sm["s3_nT"], done[c])
                        for t in range(CT):
                            last = mm(PB[c][:, t, 0:DH], nT[c][:, t, :], top.w_qmeanT[:, :])
                        last.then_inc(sm["s3_qm"], 1)
                    for c in two:
                        wait_alone(pe, sm["s3_z"], done[c])
                        transposes(lambda t: PA[c][0:DH, t, :], lambda t: z[c][:, t, :], top.ident[:, :], c)\
                            .then_inc(sm["s3_zT_psum"], 1)
                    for c in two:
                        wait_alone(pe, sm["s3_H"], done[c])
                        for a in range(2):
                            last = mm(PB[c][0:PROJ, 4 * a:4 * a + 4, :], top.w1T[:, :], HT[c][:, S * a:S * a + S])
                        last.then_inc(sm["s3_pre"], 1)
                    for c in two:
                        wait_alone(pe, sm["s3_hidden"], done[c])
                        for a in range(2):
                            last = mm(PA[c][0:1, 4 * a:4 * a + 4, :], top.w2T[:, :], u[c][:, S * a:S * a + S])
                        last.then_inc(sm["s3_score_psum"], 1)
        ph.close()


def gated_attention_phase(nc, top, dram):
    with ExitStack() as ctx:
        ph = Phase(nc, ctx, "b_")
        sm = ph.sems(
            "scores_in top8 replaced mask_row zeroed tok_psum tok mask_bf exp_gate gate_den gate rank_psum rank_sub "
            "rank rank_rows_psum rank_rows rank_wide selT plain sel gather_psum nonsel bars gathered "
            "qk_psum qk_out qk_out_a v_psum v_out c_psum c_out yuc_psum yu_copy yu dy "
            "dots_psum diag_d diag_a dmax dmax0 centred probs em dsum den rden probs_n blocks "
            "O_psum O_out Y_psum Y")
        NQ = TILES // 16
        SC = [ph.sb(f"SC{j}", [B, S]) for j in range(3)]
        top8 = ph.sb("top8", [B, 8])
        mask_row = ph.sb("mask_row", [B, S])
        tok = ph.sb("tok", [128, 2, R, B])
        mask_bf = ph.sb("mask_bf", [128, R, B], BF16)
        egate = ph.sb("egate", [128, R, B])
        gden = ph.sb("gden", [128, R, B])
        gate = ph.sb("gate", [128, R, B])
        rank = ph.sb("rank", [128, R, B])
        rank_rows = ph.sb("rank_rows", [B, S], BF16)
        SEL = ph.sb("SEL", [128, TILES, NSEL])
        gq = ph.sb("gq", [128, B, TOP_K])
        gv = ph.sb("gv", [128, B, TOP_K])
        means = ph.sb("means", [128, 2, B])
        QK = ph.sb("QK", [128, HEADS // 2, 2, B * TOP_K])
        V = ph.sb("V", [128, NQ, HEADS * DH])
        mv_ = ph.sb("meanv", [128, HEADS // 2, 2 * B])
        ya = ph.sb("ya", [B, D])
        dY = ph.sb("dY", [B, D])
        yu = ph.sb("yu", [B, D])
        diag = [ph.sb(f"diag{Q}", [128, HEADS, TOP_K]) for Q in range(NQ)]
        dmax = [ph.sb(f"dmax{Q}", [128, HEADS]) for Q in range(NQ)]
        em = [ph.sb(f"em{Q}", [128, HEADS]) for Q in range(NQ)]
        dsum = [ph.sb(f"dsum{Q}", [128, HEADS]) for Q in range(NQ)]
        PT = [ph.sb(f"PT{Q}", [128, HEADS, 128]) for Q in range(NQ)]
        OT = ph.sb("OT", [128, HEADS // 2, 128])
        P0 = ph.ps("P0", [128, 4, 512])
        P1 = ph.ps("P1", [128, 4, 512])
        HALF = HEADS // 4
        place = lambda h: h % 2 * (HEADS // 2) + h // 2
        bcast = lambda a, n: a.rearrange("p (t o) -> p t o", o=1).broadcast_to([128, a.shape[1], n])
        with nc.Block() as block:

            @block.sync
            def _(sp):
                sp.dma_start(SC[0][:, :], dram["scores"].rearrange("a (b s) -> (a b) s", b=B))\
                    .then_inc(sm["scores_in"], 16)

            @block.gpsimd
            def _(pool):
                nc.gpsimd.memset(SEL[:, :, NSEL - 1:NSEL], 1.0).then_inc(sm["zeroed"], 1)
                for Q in range(NQ):
                    nc.gpsimd.memset(PT[Q][:, :, :], 0.0).then_inc(sm["zeroed"], 1)

            @block.vector
            def _(dve):
                dve.wait_ge(sm["scores_in"], 16)
                for t in range(TOP_K // 8):
                    src = SC[0] if t == 0 else SC[1 + (t - 1) % 2]
                    if t:
                        dve.wait_ge(sm["replaced"], t)
                    nc.vector.max(top8[:, :], src[:, :]).then_inc(sm["top8"], 1)
                    dve.wait_ge(sm["top8"], t + 1)
                    nc.vector.match_replace(SC[1 + t % 2][:, :], top8[:, :], src[:, :], LOWEST)\
                        .then_inc(sm["replaced"], 1)
                dve.wait_ge(sm["replaced"], TOP_K // 8)
                nc.vector.tensor_tensor(mask_row[:, :], SC[0][:, :], SC[1 + (TOP_K // 8 - 1) % 2][:, :],
                                        ALU.not_equal).then_inc(sm["mask_row"], 1)
                dve.wait_ge(sm["tok_psum"], 1)
                nc.vector.tensor_copy(mask_bf[:, :, :], P0[:, 0, R * B:2 * R * B].rearrange("p (r b) -> p r b", r=R))\
                    .then_inc(sm["mask_bf"], 1)
                nc.vector.tensor_copy(tok[:, :, :, :], P0[:, 0, 0:2 * R * B].rearrange("p (k r b) -> p k r b", k=2, r=R))\
                    .then_inc(sm["tok"], 1)
                dve.wait_ge(sm["exp_gate"], 1)
                nc.vector.tensor_scalar(gden[:, :, :], egate[:, :, :], 1.0, None, ALU.add).then_inc(sm["gate_den"], 1)
                dve.wait_ge(sm["gate_den"], 1)
                nc.vector.reciprocal(gate[:, :, :], gden[:, :, :]).then_inc(sm["gate"], 1)
                dve.wait_ge(sm["rank_psum"], 1)
                dve.wait_ge(sm["tok"], 1)
                nc.vector.scalar_tensor_tensor(
                    out=rank[:, :, :], in0=P1[:, 0, 0:R * B].rearrange("p (r b) -> p r b", r=R), scalar=float(TOP_K),
                    in1=tok[:, 1, :, :], op0=ALU.subtract, op1=ALU.mult).then_inc(sm["rank_sub"], 1)
                dve.wait_ge(sm["rank_sub"], 1)
                nc.vector.tensor_scalar(rank[:, :, :], rank[:, :, :], float(TOP_K), None, ALU.add)\
                    .then_inc(sm["rank"], 1)
                dve.wait_ge(sm["rank"], 1)
                sel4 = SEL[:, :, :].rearrange("p (b r) j -> p b r j", b=B)
                rank4 = rank[:, :, :].rearrange("p r (b o) -> p b r o", o=1).broadcast_to([128, B, R, TOP_K + 1])
                gate4 = gate[:, :, :].rearrange("p r (b o) -> p b r o", o=1).broadcast_to([128, B, R, TOP_K])
                for b in range(B):
                    nc.vector.tensor_tensor(
                        sel4[:, b, :, TOP_K:2 * TOP_K + 1], rank4[:, b, :, :],
                        top.iota[:, 0:TOP_K + 1].rearrange("p (o j) -> p o j", o=1).broadcast_to([128, R, TOP_K + 1]),
                        ALU.is_equal).then_inc(sm["plain"], 1)
                dve.wait_ge(sm["gate"], 1)
                for b in range(B):
                    dve.wait_ge(sm["plain"], b + 1)
                    nc.vector.tensor_tensor(sel4[:, b, :, 0:TOP_K], sel4[:, b, :, TOP_K:2 * TOP_K],
                                            gate4[:, b, :, :], ALU.mult).then_inc(sm["sel"], 1)
                dve.wait_ge(sm["rank_rows_psum"], 1)
                nc.vector.tensor_copy(rank_rows[:, :], P1[0:B, 1, :]).then_inc(sm["rank_rows"], 1)
                dve.wait_ge(sm["rank_wide"], 1)
                for Q in range(NQ):
                    nc.vector.tensor_scalar(top.selT[Q][:, :], P1[:, 2 + Q, :], top.iota_col[:, :], None,
                                            ALU.is_equal).then_inc(sm["selT"], 1)
                dve.wait_ge(sm["gather_psum"], 1)
                G = P0[:, 0:2, :].rearrange("p a (b j) -> p (a b) j", j=128)
                nc.vector.tensor_scalar(means[:, 0, :], G[:, :, NSEL - 1], 1.0 / S, None, ALU.mult)
                nc.vector.tensor_scalar(means[:, 1, :], G[:, :, NSEL - 2], 1.0 / (S - TOP_K), None, ALU.mult)\
                    .then_inc(sm["bars"], 1)
                nc.vector.tensor_copy(gq[:, :, :], G[:, :, 0:TOP_K])
                dve.wait_ge(sm["bars"], 1)
                nc.vector.tensor_tensor(gv[:, :, :], G[:, :, TOP_K:2 * TOP_K], bcast(means[:, 1, :], TOP_K),
                                        ALU.subtract).then_inc(sm["gathered"], 1)
                dve.wait_ge(sm["qk_psum"], 1)
                nc.vector.tensor_copy(QK[:, 0:HALF, :, :], P1[:, :, :].rearrange("p i (k t) -> p i k t", k=2))\
                    .then_inc(sm["qk_out"], 1)
                dve.wait_ge(sm["v_psum"], 1)
                nc.vector.tensor_copy(V[:, :, :], P1[:, :, :].rearrange("p (Q a) n -> p Q (a n)", a=2))\
                    .then_inc(sm["v_out"], 1)
                dve.wait_ge(sm["c_psum"], 1)
                nc.vector.tensor_copy(mv_[:, :, :], P0[:, 0, 0:128].rearrange("p (i c) -> p i c", i=HEADS // 2))\
                    .then_inc(sm["c_out"], 1)
                dve.wait_ge(sm["yuc_psum"], 1)
                nc.vector.tensor_copy(ya[:, :], P0[0:B, 1, 0:D]).then_inc(sm["yu_copy"], 1)
                dve.wait_ge(sm["yu_copy"], 1)
                nc.vector.tensor_tensor(yu[:, :], ya[:, :], top.b_out[:, :], ALU.add).then_inc(sm["yu"], 1)
                nc.vector.tensor_tensor(dY[:, :], P0[0:B, 1, D:2 * D], ya[:, :], ALU.subtract).then_inc(sm["dy"], 1)
                for Q in range(NQ):
                    dve.wait_ge(sm["dots_psum"], Q + 1)
                    dots = (P0, P1)[Q][:, :, :].rearrange("p a (h k) -> p (a h) k", k=128)
                    for j in range(2):
                        rows = slice(32 * j, 32 * j + 32)
                        last = nc.vector.tensor_copy(diag[Q][rows, :, :], dots[rows, :, rows])
                    last.then_inc(sm["diag_d"], 1)
                for Q in range(NQ):
                    dve.wait_ge(sm["diag_d"], Q + 1)
                    dve.wait_ge(sm["diag_a"], Q + 1)
                    nc.vector.tensor_reduce(dmax[Q][:, :], diag[Q][:, :, :], AX.X, ALU.max).then_inc(sm["dmax"], 1)
                    dve.wait_ge(sm["dmax"], Q + 1)
                    nc.vector.tensor_scalar(dmax[Q][:, :], dmax[Q][:, :], 0.0, None, ALU.max).then_inc(sm["dmax0"], 1)
                    dve.wait_ge(sm["dmax0"], Q + 1)
                    nc.vector.tensor_tensor(diag[Q][:, :, :], diag[Q][:, :, :], bcast(dmax[Q][:, :], TOP_K),
                                            ALU.subtract).then_inc(sm["centred"], 1)
                for Q in range(NQ):
                    dve.wait_ge(sm["probs"], Q + 1)
                    nc.vector.tensor_reduce(dsum[Q][:, :], diag[Q][:, :, :], AX.X, ALU.add).then_inc(sm["dsum"], 1)
                    dve.wait_ge(sm["dsum"], Q + 1)
                    nc.vector.scalar_tensor_tensor(out=dsum[Q][:, :], in0=em[Q][:, :], scalar=float(S - TOP_K),
                                                   in1=dsum[Q][:, :], op0=ALU.mult, op1=ALU.add)\
                        .then_inc(sm["den"], 1)
                    dve.wait_ge(sm["den"], Q + 1)
                    nc.vector.reciprocal(dsum[Q][:, :], dsum[Q][:, :]).then_inc(sm["rden"], 1)
                    dve.wait_ge(sm["rden"], Q + 1)
                    nc.vector.tensor_tensor(diag[Q][:, :, :], diag[Q][:, :, :], bcast(dsum[Q][:, :], TOP_K),
                                            ALU.mult).then_inc(sm["probs_n"], 1)
                    dve.wait_ge(sm["probs_n"], Q + 1)
                    dve.wait_ge(sm["zeroed"], 1 + NQ)
                    for j in range(4):
                        rows = slice(32 * j, 32 * j + 32)
                        last = nc.vector.transpose(PT[Q][rows, :, rows], diag[Q][rows, :, :])
                    last.then_inc(sm["blocks"], 1)
                for Q in range(NQ):
                    dve.wait_ge(sm["O_psum"], Q + 1)
                    nc.vector.tensor_copy(OT[:, :, :], P0[:, 0:2, :].rearrange("p a (i t) -> p (a i) t", t=128))\
                        .then_inc(sm["O_out"], 1)
                    dve.wait_ge(sm["Y_psum"], Q + 1)
                    nc.vector.tensor_copy(top.Y[Q][:, :], P0[:, 2, 0:D])
                    nc.vector.tensor_copy(top.yU[Q][:, :], P0[:, 2, D:2 * D]).then_inc(sm["Y"], 1)

            @block.scalar
            def _(act):
                act.wait_ge(sm["tok"], 1)
                nc.scalar.activation(egate[:, :, :], tok[:, 0, :, :], ACT.Exp, scale=-1.0).then_inc(sm["exp_gate"], 1)
                act.wait_ge(sm["qk_psum"], 2)
                nc.scalar.activation(QK[:, HALF:, :, :], P0[:, :, :].rearrange("p i (k t) -> p i k t", k=2), ACT.Copy)\
                    .then_inc(sm["qk_out_a"], 1)
                for Q in range(NQ):
                    act.wait_ge(sm["dots_psum"], Q + 1)
                    dots = (P0, P1)[Q][:, :, :].rearrange("p a (h k) -> p (a h) k", k=128)
                    for j in range(2, 4):
                        rows = slice(32 * j, 32 * j + 32)
                        last = nc.scalar.activation(diag[Q][rows, :, :], dots[rows, :, rows], ACT.Copy)
                    last.then_inc(sm["diag_a"], 1)
                for Q in range(NQ):
                    act.wait_ge(sm["centred"], Q + 1)
                    nc.scalar.activation(em[Q][:, :], dmax[Q][:, :], ACT.Exp, scale=-float(DH) ** -0.5)
                    nc.scalar.activation(diag[Q][:, :, :], diag[Q][:, :, :], ACT.Exp, scale=float(DH) ** -0.5)\
                        .then_inc(sm["probs"], 1)

            @block.tensor
            def _(pe):
                def mm(out, lhsT, rhs, start=True, stop=True):
                    return nc.tensor.matmul(out, lhsT, rhs, start=start, stop=stop)

                pe.wait_ge(sm["mask_row"], 1)
                for k, src in enumerate((SC[0], mask_row)):
                    by_r = src[:, :].rearrange("b (p r) -> b r p", r=R)
                    for r in range(R):
                        o = (k * R + r) * B
                        last = nc.tensor.transpose(P0[:, 0, o:o + B], by_r[:, r, :], top.ident[0:B, 0:B])
                last.then_inc(sm["tok_psum"], 1)
                pe.wait_ge(sm["mask_bf"], 1)
                mm(P1[:, 0, 0:R * B], top.lower[:, :], mask_bf[:, :, :], True, False)
                for r in range(1, R):
                    for r2 in range(r):
                        last = mm(P1[:, 0, r * B:r * B + B], top.ones_bf[:, :], mask_bf[:, r2, :], False,
                                  r == R - 1 and r2 == r - 1)
                last.then_inc(sm["rank_psum"], 1)
                pe.wait_ge(sm["rank"], 1)
                for r in range(R):
                    last = nc.tensor.transpose(P1[0:B, 1, 128 * r:128 * r + 128], rank[:, r, :], top.ident[:, :])
                last.then_inc(sm["rank_rows_psum"], 1)
                pe.wait_ge(sm["tok"], 1)
                pe.wait_ge(sm["zeroed"], 1)
                for b in range(B):
                    pe.wait_ge(sm["sel"], b + 1)
                    for r in range(R):
                        last = mm(P0[:, b // 4, 128 * (b % 4):128 * (b % 4) + NSEL], top.N3[:, R * b + r, :],
                                  SEL[:, R * b + r, :], r == 0, r == R - 1)
                last.then_inc(sm["gather_psum"], 1)
                pe.wait_ge(sm["rank_rows"], 1)
                for Q in range(NQ):
                    last = mm(P1[:, 2 + Q, :], top.batch_rows_bf[:, Q, :], rank_rows[:, :])
                last.then_inc(sm["rank_wide"], 1)
                pe.wait_ge(sm["gathered"], 1)
                pe.wait_ge(sm["selT"], NQ)
                for half in range(2):
                    for i in range(HALF):
                        for k in range(2):
                            w = k * HEADS * DH + (half * HALF + i) * 128
                            last = mm((P1, P0)[half][:, i, 256 * k:256 * k + 256], top.w_qkvT[:, w:w + 128],
                                      gq[:, :, :])
                    last.then_inc(sm["qk_psum"], 1)
                pe.wait_ge(sm["qk_out"], 1)
                for Q in range(NQ):
                    for a in range(2):
                        w = 2 * HEADS * DH + 512 * a
                        last = mm(P1[:, 2 * Q + a, :], gv[:, 4 * Q:4 * Q + 4, :], top.w_qkvT[:, w:w + 512])
                last.then_inc(sm["v_psum"], 1)
                pe.wait_ge(sm["qk_out_a"], 1)
                for i in range(HEADS // 2):
                    w = 2 * HEADS * DH + 128 * i
                    last = mm(P0[:, 0, 16 * i:16 * i + 16], top.w_qkvT[:, w:w + 128], means[:, :, :])
                last.then_inc(sm["c_psum"], 1)
                pe.wait_ge(sm["c_out"], 1)
                for k in range(2):
                    for i in range(HEADS // 2):
                        last = mm(P0[0:B, 1, D * k:D * k + D], mv_[:, i, B * k:B * k + B], top.w_outT[:, i, :],
                                  i == 0, i == HEADS // 2 - 1)
                last.then_inc(sm["yuc_psum"], 1)
                for Q in range(NQ):
                    if Q == 0:
                        pe.wait_ge(sm["dy"], 1)
                    else:
                        pe.wait_ge(sm["v_out"], 1)
                    dots = (P0, P1)[Q]
                    for h in range(HEADS):
                        rows = slice(DH * (h % 2), DH * (h % 2) + DH)
                        at = place(h)
                        last = mm(dots[:, at // 4, 128 * (at % 4):128 * (at % 4) + 128],
                                  QK[rows, h // 2, 0, 128 * Q:128 * Q + 128], QK[rows, h // 2, 1, 128 * Q:128 * Q + 128])
                    last.then_inc(sm["dots_psum"], 1)
                for Q in range(NQ):
                    pe.wait_ge(sm["blocks"], Q + 1)
                    if Q:
                        pe.wait_ge(sm["O_out"], Q)
                    for h in range(HEADS):
                        rows = slice(DH * (h % 2), DH * (h % 2) + DH)
                        last = mm(P0[rows, h // 8, 128 * (h // 2 % 4):128 * (h // 2 % 4) + 128],
                                  V[:, Q, DH * h:DH * h + DH], PT[Q][:, place(h), :])
                    last.then_inc(sm["O_psum"], 1)
                    pe.wait_ge(sm["O_out"], Q + 1)
                    if Q:
                        pe.wait_ge(sm["Y"], Q)
                    for i in range(HEADS // 2):
                        mm(P0[:, 2, 0:D], OT[:, i, :], top.w_outT[:, i, :], i == 0, False)
                    mm(P0[:, 2, 0:D], top.batch_rows[:, Q, :], dY[:, :], False, True)
                    mm(P0[:, 2, D:2 * D], top.batch_rows[:, Q, :], yu[:, :]).then_inc(sm["Y_psum"], 1)
        ph.close()


def projection_phase(nc, top, dram):
    with ExitStack() as ctx:
        ph = Phase(nc, ctx, "c_")
        sm = ph.sems("y_psum y_stats y_mv y_std y_rstd y_norm y x stats mv var2 std rstd norm nb2 a n4 aT_psum aT "
                     "q_psum k_psum v_psum q1 k1 qr kr q2 k2 q3 k3 v_ready zeroed")
        stored = [ph.sem(f"stored{c}") for c in range(2)]
        two = range(2)
        a = [ph.sb(f"a{c}", [128, CT, D]) for c in two]
        y = [ph.sb(f"y{c}", [128, CT, D]) for c in two]
        aT = [ph.sb(f"aT{c}", [128, 2, S]) for c in two]
        Qp = [ph.sb(f"Qp{c}", [128, 3, 2, S], BF16) for c in two]
        Qr = [ph.sb(f"Qr{c}", [128, 2, S]) for c in two]
        Kp = [ph.sb(f"Kp{c}", [KVD, 3, 2, S], BF16) for c in two]
        Kr = [ph.sb(f"Kr{c}", [KVD, 2, S]) for c in two]
        st = [ph.sb(f"st{c}", [128, CT, 6]) for c in two]
        mv = [ph.sb(f"mv{c}", [128, CT, 2]) for c in two]
        std = [ph.sb(f"std{c}", [128, 2, CT]) for c in two]
        rs = [ph.sb(f"rs{c}", [128, 2, CT]) for c in two]
        nb = [ph.sb(f"nb{c}", [128, 2, CT]) for c in two]
        PA = [ph.ps(f"PA{c}", [128, CT, D]) for c in two]
        PB = [ph.ps(f"PB{c}", [128, CT, D]) for c in two]
        X, N4 = top.X, top.N4
        n_stored = [0, 0]

        with nc.Block() as block:

            @block.sync
            def _(sp):
                for k in range(CHUNKS):
                    c = k % 2
                    sp.wait_ge(sm["q3"], k + 1)
                    sp.wait_ge(sm["k3"], k + 1)
                    for b in (0, 1, 1) if k == CHUNKS - 1 else (0, 1):
                        entry = 2 * k + b + (1 if n_stored[c] == 12 * (k // 2) + 12 else 0)
                        for slot, n, qpart, kpart in PAIRS:
                            sp.dma_start(dram["q_store"](entry, slot, n), Qp[c][:, qpart:qpart + n, b, :])\
                                .then_inc(stored[c], 16)
                            sp.dma_start(dram["k_store"](entry, slot, n),
                                         Kp[c][:, kpart:kpart + 1, b, :].broadcast_to([KVD, n, S]))\
                                .then_inc(stored[c], 16)
                            n_stored[c] += 2
                for c in two:
                    sp.wait_ge(stored[c], 16 * n_stored[c])

            @block.gpsimd
            def _(pool):
                nc.gpsimd.memset(top.V4[:, :, :, HD4:VW], 0.0).then_inc(sm["zeroed"], 1)
                pool.wait_ge(sm["zeroed"], 1)
                nc.gpsimd.memset(top.V4[:, :, :, HD4:HD4 + 1], 1.0).then_inc(sm["zeroed"], 1)
                for k0 in range(0, CHUNKS, 2):
                    for k in (k0, k0 + 1):
                        c = k % 2
                        tiles = slice(CT * k, CT * k + CT)
                        pool.wait_ge(sm["y"], k + 1)
                        nc.gpsimd.tensor_tensor(X[:, tiles, :], X[:, tiles, :], y[c][:, :, :], ALU.add)\
                            .then_inc(sm["x"], 1)
                    for k in (k0, k0 + 1):
                        c = k % 2
                        for dst, src, s1, s2 in ((Kp, Kr, "k2", "k3"), (Qp, Qr, "q2", "q3")):
                            pool.wait_ge(sm[s1], k + 1)
                            nc.gpsimd.tensor_tensor(dst[c][:, 2, :, :], src[c][:, :, :], dst[c][:, 1, :, :],
                                                    ALU.subtract).then_inc(sm[s2], 1)

            @block.vector
            def _(dve):
                def stats(src, c, k, s):
                    for t in range(CT):
                        last = nc.vector.bn_stats(st[c][:, t, :], src(t))
                    last.then_inc(sm[s + "stats"], 1)
                    dve.wait_ge(sm[s + "stats"], k + 1)
                    for t in range(CT):
                        last = nc.vector.bn_aggr(mv[c][:, t, :], st[c][:, t, :])
                    last.then_inc(sm[s + "mv"], 1)

                def chunk_y(k):
                    c = k % 2
                    dve.wait_ge(sm["y_psum"], k + 1)
                    stats(lambda t: PA[c][:, t, :], c, k, "y_")
                    dve.wait_ge(sm["y_std"], k + 1)
                    nc.vector.reciprocal(rs[c][:, 0, :], std[c][:, 0, :]).then_inc(sm["y_rstd"], 1)
                    dve.wait_ge(sm["y_rstd"], k + 1)
                    dve.wait_ge(sm["y_mv"], k + 1)
                    nc.vector.scalar_tensor_tensor(out=nb[c][:, 0, :], in0=mv[c][:, :, 0], scalar=-1.0,
                                                   in1=rs[c][:, 0, :], op0=ALU.mult, op1=ALU.mult)\
                        .then_inc(sm["y_norm"], 1)

                def chunk_n(k):
                    c = k % 2
                    tiles = slice(CT * k, CT * k + CT)
                    dve.wait_ge(sm["x"], k + 1)
                    stats(lambda t: X[:, CT * k + t, :], c, k, "")
                    dve.wait_ge(sm["mv"], k + 1)
                    nc.vector.tensor_scalar(nb[c][:, 0, :], mv[c][:, :, 1], LN_EPS, None, ALU.add)
                    nc.vector.tensor_scalar(nb[c][:, 1, :], mv[c][:, :, 1], 1.0 + RMS_EPS, RMS_EPS * LN_EPS,
                                            ALU.mult, ALU.add).then_inc(sm["var2"], 1)
                    dve.wait_ge(sm["std"], k + 1)
                    nc.vector.reciprocal(rs[c][:, :, :], std[c][:, :, :]).then_inc(sm["rstd"], 1)
                    dve.wait_ge(sm["rstd"], k + 1)
                    nc.vector.scalar_tensor_tensor(out=nb[c][:, 1, :], in0=mv[c][:, :, 0], scalar=-1.0,
                                                   in1=rs[c][:, 1, :], op0=ALU.mult, op1=ALU.mult)\
                        .then_inc(sm["norm"], 1)
                    for t in range(CT):
                        last = nc.vector.tensor_scalar(N4[:, CT * k + t, :], X[:, CT * k + t, :], mv[c][:, t, 0:1],
                                                       rs[c][:, 0, t:t + 1], ALU.subtract, ALU.mult)
                    last.then_inc(sm["n4"], 1)
                    dve.wait_ge(sm["aT_psum"], k + 1)
                    nc.vector.tensor_copy(aT[c][:, :, :].rearrange("c b (p r) -> c b r p", r=R),
                                          PA[c][:, :, :].rearrange("c (b r) p -> c b r p", b=2)).then_inc(sm["aT"], 1)

                def chunk_p(k):
                    c = k % 2
                    dve.wait_ge(sm["k1"], k + 1)
                    nc.vector.tensor_tensor(Kr[c][:, :, :], PA[c][0:KVD, :, :].rearrange("p (b n) t -> p b (n t)", b=2),
                                            Kp[c][:, 0, :, :], ALU.subtract).then_inc(sm["kr"], 1)
                    dve.wait_ge(sm["q1"], k + 1)
                    nc.vector.tensor_tensor(Qr[c][:, :, :], PB[c][:, :, :].rearrange("p (b n) t -> p b (n t)", b=2),
                                            Qp[c][:, 0, :, :], ALU.subtract).then_inc(sm["qr"], 1)
                    dve.wait_ge(sm["v_psum"], k + 1)
                    if k == 0:
                        dve.wait_ge(sm["zeroed"], 2)
                    nc.vector.tensor_copy(top.V4[:, CT * k:CT * k + CT, :, 0:HD4],
                                          PB[c][:, 0:2, :].rearrange("p a (t g d) -> p (a t) g d", t=4, g=KV4))\
                        .then_inc(sm["v_ready"], 1)

                for k in range(0, CHUNKS, 2):
                    for f in (chunk_y, chunk_n, chunk_p):
                        for c in two:
                            f(k + c)

            @block.scalar
            def _(act):
                for k0 in range(0, CHUNKS, 2):
                    for k in (k0, k0 + 1):
                        c = k % 2
                        act.wait_ge(sm["y_mv"], k + 1)
                        nc.scalar.activation(std[c][:, 0, :], mv[c][:, :, 1], ACT.Sqrt, bias=top.eps[:, :])\
                            .then_inc(sm["y_std"], 1)
                    for k in (k0, k0 + 1):
                        c = k % 2
                        act.wait_ge(sm["y_norm"], k + 1)
                        for t in range(CT):
                            last = nc.scalar.activation(y[c][:, t, :], PA[c][:, t, :], ACT.Identity,
                                                        bias=nb[c][:, 0, t:t + 1], scale=rs[c][:, 0, t:t + 1])
                        last.then_inc(sm["y"], 1)
                    for k in (k0, k0 + 1):
                        c = k % 2
                        act.wait_ge(sm["var2"], k + 1)
                        nc.scalar.activation(std[c][:, :, :], nb[c][:, :, :], ACT.Sqrt).then_inc(sm["std"], 1)
                        act.wait_ge(sm["norm"], k + 1)
                        for t in range(CT):
                            last = nc.scalar.activation(a[c][:, t, :], X[:, CT * k + t, :], ACT.Identity,
                                                        bias=nb[c][:, 1, t:t + 1], scale=rs[c][:, 1, t:t + 1])
                        last.then_inc(sm["a"], 1)
                    for k in (k0, k0 + 1):
                        c = k % 2
                        kp = PA[c][0:KVD, :, :].rearrange("p (b n) t -> p b (n t)", b=2)
                        qp = PB[c][:, :, :].rearrange("p (b n) t -> p b (n t)", b=2)
                        for part, rest, ps, s0, s1, sr, s2 in ((Kp, Kr, kp, "k_psum", "k1", "kr", "k2"),
                                                               (Qp, Qr, qp, "q_psum", "q1", "qr", "q2")):
                            act.wait_ge(sm[s0], k + 1)
                            if k >= 2:
                                act.wait_ge(stored[c], 16 * 12 * (k // 2))
                            nc.scalar.activation(part[c][:, 0, :, :], ps, ACT.Copy).then_inc(sm[s1], 1)
                        for part, rest, sr, s2 in ((Kp, Kr, "kr", "k2"), (Qp, Qr, "qr", "q2")):
                            act.wait_ge(sm[sr], k + 1)
                            nc.scalar.activation(part[c][:, 1, :, :], rest[c][:, :, :], ACT.Copy).then_inc(sm[s2], 1)

            @block.tensor
            def _(pe):
                def mm(out, lhsT, rhs, start=True, stop=True):
                    return nc.tensor.matmul(out, lhsT, rhs, start=start, stop=stop)

                for k0 in range(0, CHUNKS, 2):
                    for k in (k0, k0 + 1):
                        c = k % 2
                        if k >= 2:
                            pe.wait_ge(sm["kr"], k - 1)
                        for t in range(CT):
                            b, r = 2 * k + t // R, t % R
                            rows = slice(TOP_K * (b % 4), TOP_K * (b % 4) + TOP_K)
                            mm(PA[c][:, t, :], top.selT[b // 4][rows, 128 * r:128 * r + 128],
                               top.Y[b // 4][rows, :], True, False)
                            last = mm(PA[c][:, t, :], top.first_row[rows, :], top.yU[b // 4][rows, :], False, True)
                        last.then_inc(sm["y_psum"], 1)
                    for k in (k0, k0 + 1):
                        c = k % 2
                        pe.wait_ge(sm["a"], k + 1)
                        for t in range(CT):
                            last = nc.tensor.transpose(PA[c][:, t, :], a[c][:, t, :], top.ident[:, :])
                        last.then_inc(sm["aT_psum"], 1)
                    for k in (k0, k0 + 1):
                        c = k % 2
                        pe.wait_ge(sm["aT"], k + 1)
                        if k >= 2:
                            pe.wait_ge(sm["v_ready"], k - 1)
                        for b in range(2):
                            last = mm(PA[c][0:KVD, R * b:R * b + R, :], top.wk4T[:, :], aT[c][:, b, :])
                        last.then_inc(sm["k_psum"], 1)
                        for b in range(2):
                            last = mm(PB[c][:, R * b:R * b + R, :], top.wq4T[:, :], aT[c][:, b, :])
                        last.then_inc(sm["q_psum"], 1)
                    for k in (k0, k0 + 1):
                        c = k % 2
                        pe.wait_ge(sm["qr"], k + 1)
                        for t in range(CT):
                            last = mm(PB[c][:, t // 4, KVD * (t % 4):KVD * (t % 4) + KVD],
                                      aT[c][:, t // 4, 128 * (t % 4):128 * (t % 4) + 128], top.wv4T[:, :])
                        last.then_inc(sm["v_psum"], 1)
        ph.close()


def causal_attention_phase(nc, top, dram):
    with ExitStack() as ctx:
        ph = Phase(nc, ctx, "d_")
        sm = ph.sems("ones S S_max part1 rest1 part2 rest2 parts mT_psum mT ST P masked PV O_sb O_T rden O_tok")
        two = range(2)
        stacks = [[ph.sem(f"stacks{c}{a}") for a in two] for c in two]
        v_in = [ph.sem(f"v_in{c}") for c in two]
        rows_stored = [ph.sem(f"rows_stored{c}") for c in two]
        rows_in = [ph.sem(f"rows_in{c}") for c in two]
        Qs = [ph.sb(f"Qs{c}", [128, HEADS // 2, S], BF16) for c in two]
        Ks = [ph.sb(f"Ks{c}", [128, KV4 // 2, S], BF16) for c in two]
        V = [ph.sb(f"V{c}", [128, QT, KV4, VW]) for c in two]
        mx = [ph.sb(f"mx{c}", [128, QT, HEADS]) for c in two]
        rest = [ph.sb(f"rest{c}", [128, 2, QT, HEADS]) for c in two]
        m3 = [ph.sb(f"m3{c}", [128, QT, 3, HEADS], BF16) for c in two]
        mT = [ph.sb(f"mT{c}", [3 * HEADS, S], BF16) for c in two]
        P = [ph.sb(f"P{k}", [128, 2, PAIRW]) for k in range(4)]
        OT = [ph.sb(f"OT{k}", [128, S]) for k in two]
        rden = ph.sb("rden", [128, QT, 4])
        pS = [ph.ps(f"pS{k}", [128, 512]) for k in two]
        pT = [ph.ps(f"pT{k}", [128, 2, 512]) for k in two]
        pO = ph.ps("pO", [128, S])
        pM = ph.ps("pM", [128, S])
        NS, NT, NG = 3 * HEADS, 3 * HEADS // 2, KV4
        ROWS = SLOTS * HD4
        P_AT = (0, 512, 896, 1152)

        def wait(eng, sem, value):
            if not isinstance(value, int) or value > 0:
                eng.wait_ge(sem, value)

        def steps(eng, step):
            step(0, 0, True)
            with eng.Fori(0, B // 2 - 1) as i:
                step(2 * i + 1, i, True)
                step(2 * i + 2, i + 1, True)
            step(B - 1, B // 2 - 1, False)

        parity = [0]

        def par(n):
            if isinstance(n, int):
                parity[0] = n % 2
            else:
                parity[0] = 1 - parity[0]
            return parity[0]

        with nc.Block() as block:

            @block.sync
            def _(sp):
                def load_stack(b, c, a):
                    sp.dma_start(Qs[c][64 * a:64 * a + ROWS, :, :], dram["q_load"](b, a)).then_inc(stacks[c][a], 16)
                    sp.dma_start(Ks[c][64 * a:64 * a + ROWS, :, :], dram["k_load"](b, a)).then_inc(stacks[c][a], 16)

                def load_v(b, c):
                    sp.dma_start(V[c][:, :, :, :], top.V4[:, bass.ds(b * QT, QT), :, :]).then_inc(v_in[c], 16)

                def max_rows(n, m, c):
                    sp.wait_ge(sm["mT"], n + 1)
                    sp.dma_start(dram["m_store"](c), mT[c][:, :]).then_inc(rows_stored[c], 16)
                    sp.wait_ge(rows_stored[c], 16 * m + 16)
                    for a in two:
                        sp.dma_start(Qs[c][64 * a + ROWS:64 * a + ROWS + 3, :, :], dram["m_load"](c, a))\
                            .then_inc(rows_in[c], 16)

                def step(n, m, more):
                    c = par(n)
                    if more:
                        wait(sp, sm["PV"], n * NG)
                        load_v(n + 1, 1 - c)
                        if not (isinstance(n, int) and n + 2 > B):
                            sp.wait_ge(sm["ST"], n * NT + NT // 2)
                            load_stack(n + 2, c, 0)
                        max_rows(n + 1, m if c == 0 else m + 1, 1 - c)
                        sp.wait_ge(sm["ST"], n * NT + NT)
                        load_stack(n + 2, c, 1)

                sp.wait_ge(sm["ones"], 2)
                for b in two:
                    for a in two:
                        load_stack(b, b, a)
                load_v(0, 0)
                max_rows(0, 0, 0)
                steps(sp, step)
                for a in two:
                    sp.wait_ge(stacks[0][a], 32 * (B // 2 + 1))

            @block.gpsimd
            def _(pool):
                def step(n, m, more):
                    par(n)
                    for pair in range(HEADS // 2):
                        for unit in range(3):
                            wait_alone(pool, sm["P"], n * NT + 3 * pair + unit + 1)
                            for at in ((P_AT[0],), (P_AT[1],), P_AT[2:])[unit]:
                                view = P[pair % 4][:, :, at:at + 128]
                                last = nc.gpsimd.affine_select(out=view, in_=view, compare_op=ALU.is_ge, fill=0.0,
                                                               base=0, pattern=[[0, 2], [1, 128]],
                                                               channel_multiplier=-1)
                            last.then_inc(sm["masked"], 1)

                for c in two:
                    nc.gpsimd.memset(Ks[c][:, :, :], 1.0).then_inc(sm["ones"], 1)
                steps(pool, step)

            @block.vector
            def _(dve):
                def maxima(n, c, heads):
                    for h in heads:
                        for f in range(3):
                            dve.wait_ge(sm["S"], n * NS + 3 * h + f + 1)
                            src = pS[(3 * h + f) % 2]
                            if f < 2:
                                last = nc.vector.reduce_max(mx[c][:, 3 - f, h:h + 1], src[:, 0:512 - 128 * f], AX.X)
                            else:
                                nc.vector.reduce_max(mx[c][:, 1, h:h + 1], src[:, 0:256], AX.X)
                                last = nc.vector.reduce_max(mx[c][:, 0, h:h + 1], src[:, 256:384], AX.X)
                            last.then_inc(sm["S_max"], 1)

                def split(n, c):
                    dve.wait_ge(sm["S_max"], n * NS + NS)
                    nc.vector.tensor_scalar(m3[c][:, :, 0, :], mx[c][:, :, :], -1.0, None, ALU.mult)\
                        .then_inc(sm["part1"], 1)
                    dve.wait_ge(sm["part1"], n + 1)
                    nc.vector.scalar_tensor_tensor(out=rest[c][:, 0, :, :], in0=mx[c][:, :, :], scalar=-1.0,
                                                   in1=m3[c][:, :, 0, :], op0=ALU.mult, op1=ALU.subtract)\
                        .then_inc(sm["rest1"], 1)
                    dve.wait_ge(sm["rest1"], n + 1)
                    nc.vector.tensor_copy(m3[c][:, :, 1, :], rest[c][:, 0, :, :]).then_inc(sm["part2"], 1)
                    dve.wait_ge(sm["part2"], n + 1)
                    nc.vector.tensor_tensor(m3[c][:, :, 2, :], rest[c][:, 0, :, :], m3[c][:, :, 1, :], ALU.subtract)\
                        .then_inc(sm["parts"], 1)

                def divide(n, g):
                    dve.wait_ge(sm["O_T"], n * NG + g + 1)
                    o = pM[:, :].rearrange("p (q j d) -> p q j d", q=QT, j=4)
                    nc.vector.reciprocal(rden[:, :, :], o[:, :, :, HD4]).then_inc(sm["rden"], 1)
                    dve.wait_ge(sm["rden"], n * NG + g + 1)
                    for q in range(QT):
                        last = nc.vector.tensor_tensor(
                            top.O4[:, n * QT + q, 4 * HD4 * g:4 * HD4 * g + 4 * HD4].rearrange("p (j d) -> p j d", j=4),
                            o[:, q, :, 0:HD4],
                            rden[:, q, :].rearrange("p (j o) -> p j o", o=1).broadcast_to([128, 4, HD4]), ALU.mult)
                    last.then_inc(sm["O_tok"], 1)

                def step(n, m, more):
                    c = par(n)
                    for pair in range(HEADS // 2):
                        if more:
                            maxima(n + 1, 1 - c, S_HEADS[pair])
                        if pair == 1 and not (isinstance(n, int) and n == 0):
                            divide(n - 1, 3)
                        if pair >= 3 and pair % 2:
                            divide(n, (pair - 3) // 2)
                        if more and pair == S_DONE:
                            split(n + 1, 1 - c)

                maxima(0, 0, range(HEADS))
                split(0, 0)
                steps(dve, step)
                divide(B - 1, 3)

            @block.scalar
            def _(act):
                def rows(n, c):
                    act.wait_ge(sm["mT_psum"], n + 1)
                    nc.scalar.activation(mT[c][:, :], pS[0][0:3 * HEADS, 0:S // 2].bitcast(BF16), ACT.Copy)\
                        .then_inc(sm["mT"], 1)

                def evacuate(n, g):
                    act.wait_ge(sm["PV"], n * NG + g + 1)
                    wait(act, sm["O_T"], n * NG + g - 1)
                    nc.scalar.activation(OT[g % 2][:, :], pO[:, :], ACT.Copy).then_inc(sm["O_sb"], 1)

                def step(n, m, more):
                    c = par(n)
                    for pair in range(HEADS // 2):
                        for unit in range(3):
                            act.wait_ge(sm["ST"], n * NT + 3 * pair + unit + 1)
                            if unit == 0:
                                wait(act, sm["PV"], n * NG + pair // 2 - 1)
                            w = 512 if unit == 0 else 384
                            nc.scalar.activation(P[pair % 4][:, :, P_AT[unit]:P_AT[unit] + w],
                                                 pT[(3 * pair + unit) % 2][:, :, 0:w], ACT.Exp,
                                                 scale=float(HD4) ** -0.5).then_inc(sm["P"], 1)
                        if pair == 0 and not (isinstance(n, int) and n == 0):
                            evacuate(n - 1, 3)
                        if pair >= 2 and pair % 2 == 0:
                            evacuate(n, pair // 2 - 1)
                        if more and pair == S_DONE + 1:
                            rows(n + 1, 1 - c)

                rows(0, 0)
                steps(act, step)
                evacuate(B - 1, 3)

            @block.tensor
            def _(pe):
                def mm(out, lhsT, rhs, start=True, stop=True):
                    return nc.tensor.matmul(out, lhsT, rhs, start=start, stop=stop)

                def first(n, m, c, heads):
                    for h in heads:
                        a, i = h // 8, h % 8
                        r = slice(64 * a, 64 * a + ROWS)
                        if h % 8 == 0:
                            pe.wait_ge(stacks[c][a], 32 * m + 32)
                        if h == 0:
                            wait(pe, sm["mT"], n)
                        for f in range(3):
                            wait(pe, sm["S_max"], n * NS + 3 * h + f - 1)
                            dst = pS[(3 * h + f) % 2]
                            for q, at in ((3, 0),) if f == 0 else ((2, 0),) if f == 1 else ((1, 0), (0, 256)):
                                w = 128 * q + 128
                                mm(dst[:, at:at + w], Qs[c][r, i, 128 * q:128 * q + 128], Ks[c][r, i // 4, 0:w],
                                   True, False)
                                last = mm(dst[:, at + w - 128:at + w], top.ident_bf[:, :], top.mask_bf[:, :],
                                          False, True)
                            last.then_inc(sm["S"], 1)

                def second(n, m, c, pair, unit):
                    if pair == 0 and unit == 0:
                        pe.wait_ge(rows_in[c], 32 * m + 32)
                    wait(pe, sm["P"], n * NT + 3 * pair + unit - 1)
                    dst = pT[(3 * pair + unit) % 2]
                    for j in two:
                        h = 2 * pair + j
                        a, i = h // 8, h % 8
                        r = slice(64 * a, 64 * a + ROWS + 3)
                        for kt, at in ((0, 0),) if unit == 0 else ((1, 0),) if unit == 1 else ((2, 0), (3, 256)):
                            w = S - 128 * kt
                            last = mm(dst[:, j, at:at + w], Ks[c][r, i // 4, 128 * kt:128 * kt + 128],
                                      Qs[c][r, i, 128 * kt:S])
                    last.then_inc(sm["ST"], 1)

                def values(n, m, c, g):
                    if g == 0:
                        pe.wait_ge(v_in[c], 16 * m + 16)
                    pe.wait_ge(sm["masked"], n * NT + 6 * g + 6)
                    wait(pe, sm["O_sb"], n * NG + g)
                    for kt in range(QT):
                        w = S - 128 * kt
                        for j in range(4):
                            last = mm(pO[32 * j:32 * j + 32, 128 * kt:S], V[c][:, kt, g, :],
                                      P[(2 * g + j // 2) % 4][:, j % 2, P_AT[kt]:P_AT[kt] + w], kt == 0, kt == QT - 1)
                    last.then_inc(sm["PV"], 1)

                def by_token(n, g):
                    pe.wait_ge(sm["O_sb"], n * NG + g + 1)
                    wait(pe, sm["O_tok"], n * NG + g)
                    for q in range(QT):
                        last = nc.tensor.transpose(pM[:, 128 * q:128 * q + 128],
                                                   OT[g % 2][:, 128 * q:128 * q + 128], top.ident[:, :])
                    last.then_inc(sm["O_T"], 1)

                def rows(n, c):
                    wait_alone(pe, sm["parts"], n + 1)
                    for q in range(QT):
                        last = nc.tensor.transpose(pS[0][0:3 * HEADS, 64 * q:64 * q + 64].bitcast(BF16),
                                                   m3[c][:, q, :, :].rearrange("p k h -> p (k h)"), top.ident_bf[:, :])
                    last.then_inc(sm["mT_psum"], 1)

                def step(n, m, more):
                    c = par(n)
                    m_next = m if c == 0 else m + 1
                    m_prev = m if c == 1 else m - 1
                    for pair in range(HEADS // 2):
                        heads = list(S_HEADS[pair]) if more else []
                        for unit in range(3):
                            second(n, m, c, pair, unit)
                            first(n + 1, m_next, 1 - c, heads[unit:unit + 1])
                        if pair == 0 and not (isinstance(n, int) and n == 0):
                            values(n - 1, m_prev, 1 - c, 3)
                        if pair == 1 and not (isinstance(n, int) and n == 0):
                            by_token(n - 1, 3)
                        if pair >= 2 and pair % 2 == 0:
                            values(n, m, c, pair // 2 - 1)
                        if pair >= 3 and pair % 2:
                            by_token(n, (pair - 3) // 2)
                        if more and pair == S_DONE + 1:
                            rows(n + 1, 1 - c)

                first(0, 0, 0, range(HEADS))
                rows(0, 0)
                steps(pe, step)
                values(B - 1, B // 2 - 1, 1, 3)
                by_token(B - 1, 3)
        ph.close()


def experts_phase(nc, top, dram, out):
    with ExitStack() as ctx:
        ph = Phase(nc, ctx, "e_")
        sm = ph.sems("oT_psum oT proj h sq rms rrms hT_psum hT logits best index diff ediff wden w1 w2 picks pick1 "
                     "comb0 comb0b comb scale exp_psum scaled_d scaled_a summed total stats mv std rstd norm y out")
        two = range(2)
        o_in = [ph.sem(f"o_in{c}") for c in two]
        stored = [ph.sem(f"stored{c}") for c in two]
        o = [ph.sb(f"o{c}", [128, CT, D]) for c in two]
        oT = [ph.sb(f"oT{c}", [128, 2, S]) for c in two]
        h = [ph.sb(f"h{c}", [128, CT, D]) for c in two]
        hT = oT
        sq = [ph.sb(f"sq{c}", [128, CT]) for c in two]
        rms = [ph.sb(f"rms{c}", [128, CT]) for c in two]
        rr = [ph.sb(f"rr{c}", [128, CT]) for c in two]
        best = [ph.sb(f"best{c}", [128, CT, 8]) for c in two]
        logit = [ph.sb(f"logit{c}", [128, CT, NE]) for c in two]
        index = [ph.sb(f"index{c}", [128, CT, 8], mybir.dt.uint32) for c in two]
        indexf = [ph.sb(f"indexf{c}", [128, CT, 2]) for c in two]
        w = [ph.sb(f"w{c}", [128, 4, CT]) for c in two]
        pick = [ph.sb(f"pick{c}", [128, 2, CT, NE]) for c in two]
        comb = [ph.sb(f"comb{c}", [128, CT, NE]) for c in two]
        T = [ph.sb(f"T{k}", [128, NE, D]) for k in two]
        moe = [ph.sb(f"moe{c}", [128, CT, D]) for c in two]
        st = [ph.sb(f"st{c}", [128, CT, 6]) for c in two]
        mv = [ph.sb(f"mv{c}", [128, CT, 2]) for c in two]
        rs = [ph.sb(f"rs{c}", [128, CT]) for c in two]
        nb = [ph.sb(f"nb{c}", [128, CT]) for c in two]
        PA = [ph.ps(f"PA{c}", [128, CT, D]) for c in two]
        PE_ = [ph.ps(f"PE{k}", [128, NE, D]) for k in two]
        wide = lambda a, n: a.rearrange("p (t o) -> p t o", o=1).broadcast_to([128, a.shape[1], n])
        n_iter = CHUNKS // 2

        def chunk(i, c):
            return bass.ds((2 * i + c) * CT, CT)

        with nc.Block() as block:

            @block.sync
            def _(sp):
                with sp.Fori(0, n_iter) as i:
                    for c in two:
                        sp.dma_start(o[c][:, :, :], top.O4[:, chunk(i, c), :]).then_inc(o_in[c], 16)
                    for c in two:
                        sp.wait_ge(sm["out"], 2 * i + c + 1)
                        sp.dma_start(out[:, chunk(i, c), :], moe[c][:, :, :]).then_inc(stored[c], 16)
                        wait_alone(sp, stored[c], 16 * i + 16, 16)

            @block.gpsimd
            def _(pool):
                with pool.Fori(0, n_iter) as i:
                    for c in two:
                        pool.wait_ge(sm["y"], 2 * i + c + 1)
                        nc.gpsimd.tensor_tensor(moe[c][:, :, :], h[c][:, :, :], top.X[:, chunk(i, c), :], ALU.add)\
                            .then_inc(sm["out"], 1)

            @block.vector
            def _(dve):
                with dve.Fori(0, n_iter) as i:
                    done = [2 * i + 1, 2 * i + 2]
                    for c in two:
                        dve.wait_ge(sm["oT_psum"], done[c])
                        nc.vector.tensor_copy(oT[c][:, :, :], PA[c][:, :, :].rearrange("p (b n) t -> p b (n t)", b=2))\
                            .then_inc(sm["oT"], 1)
                    for c in two:
                        dve.wait_ge(sm["proj"], done[c])
                        nc.vector.tensor_tensor(h[c][:, :, :], PA[c][:, :, :], top.N4[:, chunk(i, c), :], ALU.add)\
                            .then_inc(sm["h"], 1)
                    for c in two:
                        dve.wait_ge(sm["rms"], done[c])
                        nc.vector.reciprocal(rr[c][:, :], rms[c][:, :]).then_inc(sm["rrms"], 1)
                    for c in two:
                        dve.wait_ge(sm["hT_psum"], done[c])
                        nc.vector.tensor_copy(hT[c][:, :, :], PA[c][:, :, :].rearrange("p (b n) t -> p b (n t)", b=2))\
                            .then_inc(sm["hT"], 1)
                    for c in two:
                        dve.wait_ge(sm["rrms"], done[c])
                        dve.wait_ge(sm["logits"], done[c])
                        nc.vector.tensor_tensor(logit[c][:, :, :],
                                                PA[c][:, 0, 0:CT * NE].rearrange("p (t e) -> p t e", e=NE),
                                                wide(rr[c][:, :], NE), ALU.mult).then_inc(sm["scale"], 1)
                        wait_alone(dve, sm["scale"], done[c])
                        for t in range(CT):
                            last = nc.vector.max(best[c][:, t, :], logit[c][:, t, :])
                        last.then_inc(sm["best"], 1)
                        wait_alone(dve, sm["best"], done[c])
                        for t in range(CT):
                            last = nc.vector.max_index(index[c][:, t, :], best[c][:, t, :], logit[c][:, t, :])
                        last.then_inc(sm["index"], 1)
                        nc.vector.tensor_tensor(w[c][:, 0, :], best[c][:, :, 1], best[c][:, :, 0], ALU.subtract)\
                            .then_inc(sm["diff"], 1)
                        dve.wait_ge(sm["index"], done[c])
                        nc.vector.tensor_copy(indexf[c][:, :, :], index[c][:, :, 0:2]).then_inc(sm["picks"], 1)
                        dve.wait_ge(sm["picks"], done[c])
                        for j in two:
                            last = nc.vector.tensor_tensor(
                                pick[c][:, j, :, :], wide(indexf[c][:, :, j], NE),
                                top.iota[:, 0:NE].rearrange("p (o e) -> p o e", o=1).broadcast_to([128, CT, NE]),
                                ALU.is_equal)
                        last.then_inc(sm["pick1"], 1)
                    for c in two:
                        dve.wait_ge(sm["ediff"], done[c])
                        nc.vector.tensor_scalar(w[c][:, 2, :], w[c][:, 1, :], 1.0, None, ALU.add)\
                            .then_inc(sm["wden"], 1)
                        dve.wait_ge(sm["wden"], done[c])
                        nc.vector.reciprocal(w[c][:, 3, :], w[c][:, 2, :]).then_inc(sm["w1"], 1)
                        dve.wait_ge(sm["w1"], done[c])
                        nc.vector.tensor_tensor(w[c][:, 2, :], w[c][:, 3, :], rr[c][:, :], ALU.mult)\
                            .then_inc(sm["w2"], 1)
                        dve.wait_ge(sm["w2"], done[c])
                        nc.vector.tensor_tensor(w[c][:, 3, :], w[c][:, 2, :], w[c][:, 1, :], ALU.mult)
                        dve.wait_ge(sm["pick1"], done[c])
                        nc.vector.tensor_tensor(pick[c][:, 0, :, :], pick[c][:, 0, :, :], wide(w[c][:, 2, :], NE),
                                                ALU.mult).then_inc(sm["comb0"], 1)
                        dve.wait_ge(sm["comb0"], done[c])
                        nc.vector.tensor_tensor(pick[c][:, 1, :, :], pick[c][:, 1, :, :], wide(w[c][:, 3, :], NE),
                                                ALU.mult).then_inc(sm["comb0b"], 1)
                        dve.wait_ge(sm["comb0b"], done[c])
                        nc.vector.tensor_tensor(comb[c][:, :, :], pick[c][:, 0, :, :], pick[c][:, 1, :, :],
                                                ALU.add).then_inc(sm["comb"], 1)
                    for c in two:
                        dve.wait_ge(sm["comb"], done[c])
                        for t in range(CT):
                            u = (2 * i + c) * CT + t
                            k = t % 2
                            if k == 0:
                                dve.wait_ge(sm["exp_psum"], u + 1)
                                if t > 1 or c:
                                    dve.wait_ge(sm["summed"], u - 1)
                                nc.vector.tensor_tensor(T[k][:, :, :], PE_[k][:, :, :], wide(comb[c][:, t, :], D),
                                                        ALU.mult).then_inc(sm["scaled_d"], 1)
                                dve.wait_ge(sm["scaled_d"], (2 * i + c) * (CT // 2) + t // 2 + 1)
                            else:
                                dve.wait_ge(sm["scaled_a"], (2 * i + c) * (CT // 2) + t // 2 + 1)
                            nc.vector.tensor_reduce(moe[c][:, t, :], T[k][:, :, :].rearrange("p e d -> p d e"),
                                                    AX.X, ALU.add).then_inc(sm["summed"], 1)
                        dve.wait_ge(sm["summed"], (2 * i + c) * CT + CT)
                        nc.vector.tensor_tensor(h[c][:, :, :], h[c][:, :, :], moe[c][:, :, :], ALU.add)\
                            .then_inc(sm["total"], 1)
                        dve.wait_ge(sm["total"], done[c])
                        for t in range(CT):
                            last = nc.vector.bn_stats(st[c][:, t, :], h[c][:, t, :])
                        last.then_inc(sm["stats"], 1)
                        wait_alone(dve, sm["stats"], done[c])
                        for t in range(CT):
                            last = nc.vector.bn_aggr(mv[c][:, t, :], st[c][:, t, :])
                        last.then_inc(sm["mv"], 1)
                    for c in two:
                        dve.wait_ge(sm["std"], done[c])
                        nc.vector.reciprocal(rs[c][:, :], rms[c][:, :]).then_inc(sm["rstd"], 1)
                        dve.wait_ge(sm["rstd"], done[c])
                        for t in range(CT):
                            last = nc.vector.tensor_scalar(h[c][:, t, :], h[c][:, t, :], mv[c][:, t, 0:1],
                                                           rs[c][:, t:t + 1], ALU.subtract, ALU.mult)
                        last.then_inc(sm["y"], 1)

            @block.scalar
            def _(act):
                with act.Fori(0, n_iter) as i:
                    done = [2 * i + 1, 2 * i + 2]
                    for c in two:
                        act.wait_ge(sm["h"], done[c])
                        for t in range(CT):
                            last = nc.scalar.activation(moe[c][:, t, :], h[c][:, t, :], ACT.Square,
                                                        accum_out=sq[c][:, t:t + 1])
                        last.then_inc(sm["sq"], 1)
                    for c in two:
                        act.wait_ge(sm["sq"], done[c])
                        nc.scalar.activation(rms[c][:, :], sq[c][:, :], ACT.Sqrt, scale=1.0 / D, bias=top.eps_rms[:, :])\
                            .then_inc(sm["rms"], 1)
                    for c in two:
                        act.wait_ge(sm["diff"], done[c])
                        nc.scalar.activation(w[c][:, 1, :], w[c][:, 0, :], ACT.Exp).then_inc(sm["ediff"], 1)
                    for c in two:
                        act.wait_ge(sm["comb"], done[c])
                        for t in range(1, CT, 2):
                            u = (2 * i + c) * CT + t
                            act.wait_ge(sm["exp_psum"], u + 1)
                            if t > 1 or c:
                                act.wait_ge(sm["summed"], u - 1)
                            for e in range(NE):
                                last = nc.scalar.activation(T[1][:, e, :], PE_[1][:, e, :], ACT.Copy,
                                                            scale=comb[c][:, t, e:e + 1])
                            last.then_inc(sm["scaled_a"], 1)
                    for c in two:
                        act.wait_ge(sm["mv"], done[c])
                        nc.scalar.activation(rms[c][:, :], mv[c][:, :, 1], ACT.Sqrt, bias=top.eps[:, :])\
                            .then_inc(sm["std"], 1)

            @block.tensor
            def _(pe):
                def mm(out_, lhsT, rhs, start=True, stop=True):
                    return nc.tensor.matmul(out_, lhsT, rhs, start=start, stop=stop)

                with pe.Fori(0, n_iter) as i:
                    done = [2 * i + 1, 2 * i + 2]
                    for c in two:
                        pe.wait_ge(o_in[c], 16 * i + 16)
                        for t in range(CT):
                            last = nc.tensor.transpose(PA[c][:, t, :], o[c][:, t, :], top.ident[:, :])
                        last.then_inc(sm["oT_psum"], 1)
                    for c in two:
                        pe.wait_ge(sm["oT"], done[c])
                        for t in range(CT):
                            lhsT = oT[c][:, t // R, :].rearrange("d (p r) -> d r p", r=R)[:, t % R, :]
                            last = mm(PA[c][:, t, :], lhsT, top.wo4T[:, :])
                        last.then_inc(sm["proj"], 1)
                    for c in two:
                        pe.wait_ge(sm["h"], done[c])
                        for t in range(CT):
                            last = nc.tensor.transpose(PA[c][:, t, :], h[c][:, t, :], top.ident[:, :])
                        last.then_inc(sm["hT_psum"], 1)
                    for c in two:
                        pe.wait_ge(sm["hT"], done[c])
                        for t in range(CT):
                            last = mm(PA[c][:, 0, NE * t:NE * t + NE],
                                      hT[c][:, t // 4, 128 * (t % 4):128 * (t % 4) + 128], top.gate_expT[:, 0:NE])
                        last.then_inc(sm["logits"], 1)
                    for c in two:
                        for t in range(CT):
                            u = (2 * i + c) * CT + t
                            k = t % 2
                            if k == 0:
                                free, count = sm["scaled_d"], (2 * i + c) * (CT // 2) + t // 2
                            else:
                                free, count = sm["scaled_a"], (2 * i + c) * (CT // 2) + t // 2
                            if t >= 2 or c:
                                pe.wait_ge(free, count)
                            for a in two:
                                last = mm(PE_[k][:, 4 * a:4 * a + 4, :],
                                          hT[c][:, t // 4, 128 * (t % 4):128 * (t % 4) + 128],
                                          top.gate_expT[:, NE + 512 * a:NE + 512 * a + 512])
                            last.then_inc(sm["exp_psum"], 1)


def sandwich(nc, dram, out):
    with ExitStack() as ctx:
        top = Phase(nc, ctx)
        top.X = top.sb("X", [128, TILES, D])
        top.N3 = top.sb("N3", [128, TILES, D])
        top.N4 = top.N3
        top.V4 = top.sb("V4", [128, TILES, KV4, VW])
        top.O4 = top.sb("O4", [128, TILES, D])
        top.ident = top.sb("ident", [128, 128])
        top.ident_bf = top.sb("ident_bf", [128, 128], BF16)
        top.eps = top.sb("eps", [128, 1])
        top.eps_rms = top.sb("eps_rms", [128, 1])
        top.hadamard = top.sb("hadamard", [128, D])
        top.ternT = top.sb("ternT", [128, 3, D], BF16)
        top.w_qmeanT = top.sb("w_qmeanT", [128, DH])
        top.ln_gb = top.sb("ln_gb", [DH, 2])
        top.w1T = top.sb("w1T", [DH, PROJ])
        top.b1 = top.sb("b1", [PROJ, 1])
        top.w2T = top.sb("w2T", [PROJ, 1])
        top.b2 = top.sb("b2", [1, 1])
        top.w_qkvT = top.sb("w_qkvT", [128, 3 * HEADS * DH])
        top.w_outT = top.sb("w_outT", [128, HEADS // 2, D])
        top.b_out = top.sb("b_out", [B, D])
        top.iota = top.sb("iota", [128, TOP_K + 1])
        top.iota_col = top.sb("iota_col", [128, 1])
        top.batch_rows = top.sb("batch_rows", [B, 2, 128])
        top.batch_rows_bf = top.sb("batch_rows_bf", [B, 2, 128], BF16)
        top.first_row = top.sb("first_row", [128, 128])
        top.lower_f = top.sb("lower_f", [128, 128])
        top.lower = top.sb("lower", [128, 128], BF16)
        top.ones_bf = top.sb("ones_bf", [128, 128], BF16)
        top.selT = [top.sb(f"selT{Q}", [128, S]) for Q in range(2)]
        top.Y = [top.sb(f"Y{Q}", [128, D]) for Q in range(2)]
        top.yU = [top.sb(f"yU{Q}", [128, D]) for Q in range(2)]
        top.qkv4T = top.sb("qkv4T", [128, D + 2 * KVD])
        top.wq4T, top.wk4T, top.wv4T = (top.qkv4T[:, 0:D], top.qkv4T[:, D:D + KVD], top.qkv4T[:, D + KVD:D + 2 * KVD])
        top.wo4T = top.sb("wo4T", [128, D])
        top.gate_expT = top.sb("gate_expT", [128, NE + NE * D])
        top.norm_w = top.sb("norm_w", [128, 2])
        top.mask_f = top.sb("mask_f", [128, 128])
        top.mask_bf = top.sb("mask_bf", [128, 128], BF16)
        with ExitStack() as early:
            top.expS = [early.enter_context(nc.sbuf_tensor(f"expS{c}", [128, CT, D], FP32)) for c in range(2)]
            setup_phase(nc, top, dram)
            dilated_and_ternary_phase(nc, top, dram)
        gated_attention_phase(nc, top, dram)
        projection_phase(nc, top, dram)
        causal_attention_phase(nc, top, dram)
        experts_phase(nc, top, dram, out)


def kernel(**inputs):
    import numpy as np
    import concourse.bacc as bacc
    from concourse.bass_utils import run_bass_kernel_spmd

    def hadamard(size):
        h = np.array([[1.0]], dtype=np.float64)
        while h.shape[0] < size:
            h = np.block([[h, h], [h, -h]])
        return (h / np.sqrt(size)).astype(np.float32)

    a = {k: np.asarray(v) for k, v in inputs.items()}
    by_channel = lambda w: w.reshape(-1, HD4, D).transpose(1, 0, 2).reshape(-1, D)
    col = lambda v: np.ascontiguousarray(v.reshape(-1, 1))
    arrays = {
        "x": a["L0_attn_x"].reshape(B, 128, R, D).transpose(1, 0, 2, 3).reshape(128, TILES, D),
        "ffn_weight": a["L0_ffn_weight"],
        "w_qkvT": a["L1_attn_w_qkv"].T,
        "ln_gb": np.stack([a["L1_attn_ln_g"], a["L1_attn_ln_b"]], axis=1),
        "w1T": a["L1_attn_w1"].T,
        "b1": col(a["L1_attn_b1"]),
        "w2T": a["L1_attn_w2"].T,
        "b2": col(a["L1_attn_b2"]),
        "ident": np.eye(128, dtype=np.float32),
        "hadamard": hadamard(D),
        "w_outT": a["L1_attn_w_out"].T.reshape(HEADS // 2, 128, D).transpose(1, 0, 2),
        "b_out": np.broadcast_to(a["L1_attn_b_out"], (B, D)),
        "qkv4T": np.concatenate([by_channel(a["L1_ffn_wq"]), by_channel(a["L1_ffn_wk"]), a["L1_ffn_wv"]]).T,
        "wo4T": a["L1_ffn_wo"].T,
        "gate_expT": np.concatenate([a["L1_ffn_gate_w"], a["L1_ffn_expert_w"].reshape(NE * D, D)]).T,
        "norm_w": np.stack([a["L1_ffn_attn_norm_w"], a["L1_ffn_ffn_norm_w"]], axis=1),
        "iota": np.tile(np.arange(TOP_K + 1, dtype=np.float32), (128, 1)),
        "iota_col": (np.arange(128) % TOP_K).astype(np.float32).reshape(128, 1),
        "batch_rows": (np.arange(B)[:, None] == np.arange(2 * 128)[None] // TOP_K).astype(np.float32).reshape(B, 2, 128),
        "first_row": np.repeat((np.arange(128) % TOP_K == 0).astype(np.float32)[:, None], 128, axis=1),
        "lower": np.triu(np.ones((128, 128), np.float32), 1),
        "mask": np.triu(np.full((128, 128), -1e30, np.float32), 1),
    }
    nc = bacc.Bacc("TRN2", target_bir_lowering=False, num_devices=1)
    dram, send = {}, {}
    for name, v in arrays.items():
        send[f"in_{name}_dram"] = np.ascontiguousarray(v)
        dram[name] = nc.dram_tensor(f"in_{name}_dram", v.shape, mybir.dt.from_np(v.dtype), kind="ExternalInput").ap()
    dram["scores"] = nc.dram_tensor("scores", (1, B * S), FP32, kind="Internal").ap()
    q_stack = nc.dram_tensor("q_stack", (B + 1, SLOTS, HD4, HEADS, S), BF16, kind="Internal").ap()
    k_stack = nc.dram_tensor("k_stack", (B + 1, SLOTS, HD4, KV4, S), BF16, kind="Internal").ap()
    m_rows = nc.dram_tensor("m_rows", (2, 3, 2, HEADS // 2, S), BF16, kind="Internal").ap()

    def stack_load(stack, heads):
        return lambda b, a: stack[bass.ds(b, 1), :, :, heads // 2 * a:heads // 2 * a + heads // 2, :]\
            .rearrange("o j d h t -> (o j d) h t")

    def stack_store(stack):
        return lambda b, slot, n: stack[b, slot:slot + n].rearrange("j d h t -> (d h) j t")

    dram["q_load"], dram["k_load"] = stack_load(q_stack, HEADS), stack_load(k_stack, KV4)
    dram["q_store"], dram["k_store"] = stack_store(q_stack), stack_store(k_stack)
    dram["m_store"] = lambda c: m_rows[c].rearrange("k a i t -> (k a i) t")
    dram["m_load"] = lambda c, a: m_rows[c, :, a, :, :]
    out = nc.dram_tensor("out_0_dram", (128, TILES, D), FP32, kind="ExternalOutput").ap()
    sandwich(nc, dram, out)
    got = run_bass_kernel_spmd(nc, [send], core_ids=[0]).results[0]["out_0_dram"]
    return got.reshape(128, B, R, D).transpose(1, 0, 2, 3).reshape(B, S, D)
```

```python
import concourse.bass as bass
from concourse import mybir
from contextlib import ExitStack

FP32 = mybir.dt.float32
BF16 = mybir.dt.bfloat16
ALU = mybir.AluOpType
ACT = mybir.ActivationFunctionType
AX = mybir.AxisListType

B, S, D = 8, 512, 128
R = 4
SEG = 64
TILES = B * R
CT = 8
CHUNKS = TILES // CT
DH, HEADS = 64, 16
PROJ = 16
TOP_K = 32
NSEL = 2 * TOP_K + 2
LOWEST = -3e38
HD4, KV4, NE = 8, 4, 8
KVD = KV4 * HD4
VW = 32
QT = S // 128
SLOTS = 6
PAIRS = ((0, 3, 0, 0), (3, 2, 0, 1), (5, 1, 0, 2))
PAIRW = 512 + 384 + 256 + 128
LEAD = 3
RMS_EPS = 1e-6
LN_EPS = 1e-5
ROUND = 12582912.0
POS = 7.0
NEG = -8.0


def wait_alone(eng, sem, count, unit=1):
    if not isinstance(count, int):
        count = eng.to_reg(count)
        eng.wait_ge(sem, unit)
    eng.wait_ge(sem, count)


class Phase:

    def __init__(self, nc, ctx, tag=""):
        self.nc, self.ctx, self.tag, self.all_sems = nc, ctx, tag, []

    def sb(self, name, shape, dt=FP32):
        return self.ctx.enter_context(self.nc.sbuf_tensor(self.tag + name, shape, dt))

    def ps(self, name, shape, dt=FP32):
        return self.ctx.enter_context(self.nc.psum_tensor(self.tag + name, shape, dt))

    def sem(self, name):
        self.all_sems.append(self.nc.alloc_semaphore(name=self.tag + name))
        return self.all_sems[-1]

    def close(self):
        self.nc.clear_and_free_semaphores(self.all_sems)
        self.nc.all_engine_barrier()

    def sems(self, names):
        return {n: self.sem(n) for n in names.split()}


def dilated_and_ternary_phase(nc, top, dram):
    with ExitStack() as ctx:
        ph = Phase(nc, ctx, "a_")
        sm = ph.sems(
            "s1_std s1_ostd s1_orstd s2_std s2_ostd s3_std s3_qstd s1_stats s1_mv s1_rstd s1_norm s1_n s1_nT_psum s1_nT s1_scores s1_E s1_sum s1_O s1_ostats s1_omv "
            "s1_sq s1_var s1_onorm s1_y s1_x "
            "s2_stats s2_mv s2_rstd s2_norm s2_n s2_nT_psum s2_nT s2_xh s2_absmax s2_scale s2_rscale s2_ratio s2_q "
            "s2_qT_psum s2_qT s2_O s2_ostats s2_omv s2_sq s2_var s2_ors s2_ors2 s2_onorm s2_y s2_x s2_rounded "
            "s3_stats s3_mv s3_rstd s3_norm s3_n s3_nT_psum s3_nT s3_qm s3_qstats s3_qmv s3_qrstd s3_qnorm s3_z "
            "s3_zT_psum s3_H s3_pre s3_hidden s3_score_psum s3_score")
        sm |= ph.sems("loaded_first loaded zeroed ident_bf tern_abs tern_scale tern_steps tern_low tern_full "
                      "part1 rest1 part2 parts parts_psum parts_out mean_w mean_w_out eps")
        chunks = range(CHUNKS)
        flat = lambda a: a.rearrange("p t d -> p (t d)")
        x_in = [ph.sem(f"x_in{c}") for c in chunks]
        score_kept = ph.sem("score_kept")
        X = [top.X[:, CT * c:CT * c + CT, :] for c in chunks]
        n = [top.N3[:, CT * c:CT * c + CT, :] for c in chunks]
        nT = [ph.sb(f"nT{c}", [128, CT, D]) for c in chunks]
        y = nT
        u = [flat(nT[c][0:PROJ, :, :]) for c in chunks]
        expS = [ph.sb(f"expS{c}", [128, CT, D]) for c in chunks]
        ratio = expS
        HT = [flat(expS[c][0:DH, :, :]) for c in chunks]
        score = [flat(expS[c][0:1, :, :]).rearrange("a (b p r) -> a b p r", b=2, r=R) for c in chunks]
        q = [ph.sb(f"q{c}", [128, CT, D], BF16) for c in chunks]
        qT = [ph.sb(f"qT{c}", [128, CT, D], BF16) for c in chunks]
        z = [ph.sb(f"z{c}", [128, CT, DH]) for c in chunks]
        small = lambda name, *shape: [ph.sb(f"{name}{c}", [128, CT, *shape]) for c in chunks]
        st, mv = small("st", 6), small("mv", 2)
        rs, nb, den, std, tmp, sc = (small(name) for name in ("rs", "nb", "den", "std", "tmp", "sc"))
        w = ph.sb("w", [128, D])
        pos = ph.sb("pos", [128, D])
        low = ph.sb("low", [128, D])
        rest = ph.sb("rest", [128, D])
        part = ph.sb("part", [128, 3, D], BF16)
        absum = ph.sb("absum", [128, 1])
        scale = ph.sb("scale", [128, 1])
        lim = ph.sb("lim", [128, 2])
        PS = [ph.ps(f"PS{c}", [128, CT, D]) for c in chunks]
        partsT = PS[-1][:, 0:2, :].bitcast(BF16).rearrange("p a (b d) -> p (a b) d", b=2)[:, 0:3, :]
        done = [c + 1 for c in chunks]
        FIRST = (("ident", top.ident), ("ffn_weight", w), ("hadamard", top.hadamard))
        OTHERS = (("w_qkvT", top.w_qkvT), ("ln_gb", top.ln_gb), ("w1T", top.w1T), ("b1", top.b1), ("w2T", top.w2T),
                  ("b2", top.b2), ("w_outT", top.w_outT), ("qkv4T", top.qkv4T), ("wo4T", top.wo4T),
                  ("gate_expT", top.gate_expT), ("norm_w", top.norm_w), ("b_out", top.b_out), ("iota", top.iota),
                  ("iota_col", top.iota_col), ("batch_rows", top.batch_rows), ("first_row", top.first_row),
                  ("lower", top.lower_f), ("mask", top.mask_f))

        with nc.Block() as block:

            @block.sync
            def _(sp):
                for loads, sem in ((FIRST, "loaded_first"), (OTHERS, "loaded")):
                    for name, dst in loads:
                        sp.dma_start(dst[:], dram[name]).then_inc(sm[sem], 16)
                for c in chunks:
                    sp.wait_ge(sm["s3_score"], done[c])
                    sp.dma_start(dram["scores"][:, 2 * S * c:2 * S * c + 2 * S],
                                 score[c][:, :, :, :].rearrange("a b p r -> a (b p r)")).then_inc(score_kept, 16)
                sp.wait_ge(score_kept, 16 * CHUNKS)

            @block.vector
            def _(dve):
                def stats(src, c, k, s, width=D):
                    for t in range(CT):
                        last = nc.vector.bn_stats(st[c][:, t, :], src(t))
                    last.then_inc(sm[s + "stats"], 1)
                    dve.wait_ge(sm[s + "stats"], k)
                    for t in range(CT):
                        last = nc.vector.bn_aggr(mv[c][:, t, :], st[c][:, t, :])
                    last.then_inc(sm[s + "mv"], 1)
                    dve.wait_ge(sm[s + "mv"], k)

                def norm_scalars(c, k, s):
                    dve.wait_ge(sm[s + "std"], k)
                    nc.vector.reciprocal(rs[c][:, :], std[c][:, :]).then_inc(sm[s + "rstd"], 1)
                    dve.wait_ge(sm[s + "rstd"], k)
                    nc.vector.scalar_tensor_tensor(out=nb[c][:, :], in0=mv[c][:, :, 0], scalar=-1.0,
                                                   in1=rs[c][:, :], op0=ALU.mult, op1=ALU.mult)\
                        .then_inc(sm[s + "norm"], 1)

                def ternary_weights():
                    dve.wait_ge(sm["loaded_first"], 16 * len(FIRST))
                    nc.vector.tensor_copy(top.ident_bf[:, :], top.ident[:, :]).then_inc(sm["ident_bf"], 1)
                    nc.vector.tensor_reduce(absum[:, :], w[:, :], AX.X, ALU.add, apply_absolute_value=True)\
                        .then_inc(sm["tern_abs"], 1)
                    dve.wait_ge(sm["tern_abs"], 1)
                    nc.vector.tensor_scalar(scale[:, :], absum[:, :], 1.0 / D, LN_EPS, ALU.mult, ALU.max)\
                        .then_inc(sm["tern_scale"], 1)
                    dve.wait_ge(sm["tern_scale"], 1)
                    nc.vector.tensor_scalar(lim[:, 0:1], scale[:, :], 0.5, None, ALU.mult)
                    nc.vector.tensor_scalar(lim[:, 1:2], scale[:, :], -0.5, None, ALU.mult)\
                        .then_inc(sm["tern_steps"], 1)
                    dve.wait_ge(sm["tern_steps"], 1)
                    nc.vector.tensor_scalar(pos[:, :], w[:, :], lim[:, 0:1], scale[:, :], ALU.is_gt, ALU.mult)
                    nc.vector.tensor_scalar(low[:, :], w[:, :], lim[:, 1:2], scale[:, :], ALU.is_lt, ALU.mult)\
                        .then_inc(sm["tern_low"], 1)
                    dve.wait_ge(sm["tern_low"], 1)
                    nc.vector.tensor_tensor(w[:, :], pos[:, :], low[:, :], ALU.subtract).then_inc(sm["tern_full"], 1)
                    dve.wait_ge(sm["tern_full"], 1)
                    nc.vector.tensor_copy(part[:, 0, :], w[:, :]).then_inc(sm["part1"], 1)
                    dve.wait_ge(sm["part1"], 1)
                    nc.vector.tensor_tensor(rest[:, :], w[:, :], part[:, 0, :], ALU.subtract).then_inc(sm["rest1"], 1)
                    dve.wait_ge(sm["rest1"], 1)
                    nc.vector.tensor_copy(part[:, 1, :], rest[:, :]).then_inc(sm["part2"], 1)
                    dve.wait_ge(sm["part2"], 1)
                    nc.vector.tensor_tensor(part[:, 2, :], rest[:, :], part[:, 1, :], ALU.subtract)\
                        .then_inc(sm["parts"], 1)

                def other_weights():
                    dve.wait_ge(sm["loaded"], 16 * len(OTHERS))
                    nc.vector.tensor_reduce(
                        top.w_qmeanT[:, :], top.w_qkvT[:, 0:HEADS * DH].rearrange("p (h d) -> p d h", h=HEADS),
                        AX.X, ALU.add).then_inc(sm["mean_w"], 1)
                    nc.vector.tensor_copy(top.lower[:, :], top.lower_f[:, :])
                    nc.vector.tensor_copy(top.mask_bf[:, :], top.mask_f[:, :])
                    nc.vector.tensor_copy(top.batch_rows_bf[:, :, :], top.batch_rows[:, :, :])
                    nc.vector.tensor_scalar(top.qkv4T[:, :], top.qkv4T[:, :], top.norm_w[:, 0:1], None, ALU.mult)
                    nc.vector.tensor_scalar(top.gate_expT[:, :], top.gate_expT[:, :], top.norm_w[:, 1:2], None,
                                            ALU.mult)
                    dve.wait_ge(sm["mean_w"], 1)
                    nc.vector.tensor_scalar(top.w_qmeanT[:, :], top.w_qmeanT[:, :], 1.0 / HEADS, None, ALU.mult)\
                        .then_inc(sm["mean_w_out"], 1)

                ternary_weights()
                for c in chunks:
                    dve.wait_ge(x_in[c], 16)
                    stats(lambda t: X[c][:, t, :], c, done[c], "s1_")
                dve.wait_ge(sm["parts_psum"], 1)
                nc.vector.tensor_copy(top.ternT[:, :, :], partsT).then_inc(sm["parts_out"], 1)
                for c in chunks:
                    norm_scalars(c, done[c], "s1_")
                for c in chunks:
                    dve.wait_ge(sm["s1_nT_psum"], done[c])
                    nc.vector.tensor_copy(nT[c][:, :, :], PS[c][:, :, :]).then_inc(sm["s1_nT"], 1)
                for c in chunks:
                    dve.wait_ge(sm["s1_E"], done[c])
                    for a in range(2):
                        last = nc.vector.tensor_reduce(
                            den[c][SEG * a:SEG * a + SEG, :],
                            expS[c][SEG * a:SEG * a + SEG, :, SEG * a:SEG * a + SEG], AX.X, ALU.add)
                    last.then_inc(sm["s1_sum"], 1)
                    dve.wait_ge(sm["s1_sum"], done[c])
                    nc.vector.scalar_tensor_tensor(out=tmp[c][:, :], in0=den[c][:, :], scalar=float(R * R),
                                                   in1=den[c][:, :], op0=ALU.mult, op1=ALU.mult)\
                        .then_inc(sm["s1_sq"], 1)
                for c in chunks:
                    dve.wait_ge(sm["s1_O"], done[c])
                    stats(lambda t: PS[c][:, t, :], c, done[c], "s1_o")
                    dve.wait_ge(sm["s1_sq"], done[c])
                    nc.vector.scalar_tensor_tensor(out=tmp[c][:, :], in0=tmp[c][:, :], scalar=LN_EPS,
                                                   in1=mv[c][:, :, 1], op0=ALU.mult, op1=ALU.add)\
                        .then_inc(sm["s1_var"], 1)
                for c in chunks:
                    norm_scalars(c, done[c], "s1_o")
                for c in chunks:
                    dve.wait_ge(sm["s1_x"], done[c])
                    stats(lambda t: X[c][:, t, :], c, done[c], "s2_")
                for c in chunks:
                    norm_scalars(c, done[c], "s2_")
                for c in chunks:
                    dve.wait_ge(sm["s2_xh"], done[c])
                    nc.vector.tensor_reduce(den[c][:, :], PS[c][:, :, :], AX.X, ALU.max,
                                            apply_absolute_value=True).then_inc(sm["s2_absmax"], 1)
                    dve.wait_ge(sm["s2_absmax"], done[c])
                    nc.vector.tensor_scalar(sc[c][:, :], den[c][:, :], LN_EPS, 1.0 / POS, ALU.max, ALU.mult)\
                        .then_inc(sm["s2_scale"], 1)
                    dve.wait_ge(sm["s2_scale"], done[c])
                    nc.vector.reciprocal(den[c][:, :], sc[c][:, :]).then_inc(sm["s2_rscale"], 1)
                    dve.wait_ge(sm["s2_rscale"], done[c])
                    nc.vector.tensor_tensor(ratio[c][:, :, :], PS[c][:, :, :],
                                            den[c][:, :].rearrange("p (t o) -> p t o", o=1).broadcast_to([128, CT, D]),
                                            ALU.mult).then_inc(sm["s2_ratio"], 1)
                    dve.wait_ge(sm["s2_ratio"], done[c])
                    nc.vector.tensor_scalar(q[c][:, :, :], ratio[c][:, :, :], ROUND, ROUND,
                                            ALU.add, ALU.subtract).then_inc(sm["s2_q"], 1)
                for c in chunks:
                    dve.wait_ge(sm["s2_qT_psum"], done[c])
                    nc.vector.tensor_scalar(qT[c][:, :, :], PS[c][:, 0:CT // 2, :].bitcast(BF16), POS, NEG,
                                            ALU.min, ALU.max).then_inc(sm["s2_qT"], 1)
                    nc.vector.tensor_tensor(tmp[c][:, :], sc[c][:, :], sc[c][:, :], ALU.mult)\
                        .then_inc(sm["s2_sq"], 1)
                for c in chunks:
                    dve.wait_ge(sm["s2_O"], done[c])
                    stats(lambda t: PS[c][:, t, :], c, done[c], "s2_o")
                    dve.wait_ge(sm["s2_sq"], done[c])
                    nc.vector.tensor_tensor(tmp[c][:, :], tmp[c][:, :], mv[c][:, :, 1], ALU.mult)\
                        .then_inc(sm["s2_var"], 1)
                for c in chunks:
                    dve.wait_ge(sm["s2_ostd"], done[c])
                    nc.vector.reciprocal(tmp[c][:, :], std[c][:, :]).then_inc(sm["s2_ors"], 1)
                    dve.wait_ge(sm["s2_ors"], done[c])
                    nc.vector.tensor_tensor(rs[c][:, :], tmp[c][:, :], sc[c][:, :], ALU.mult)\
                        .then_inc(sm["s2_ors2"], 1)
                    dve.wait_ge(sm["s2_ors2"], done[c])
                    nc.vector.scalar_tensor_tensor(out=nb[c][:, :], in0=mv[c][:, :, 0], scalar=-1.0,
                                                   in1=rs[c][:, :], op0=ALU.mult, op1=ALU.mult)\
                        .then_inc(sm["s2_onorm"], 1)
                other_weights()
                for c in chunks:
                    dve.wait_ge(sm["s2_x"], done[c])
                    stats(lambda t: X[c][:, t, :], c, done[c], "s3_")
                for c in chunks:
                    norm_scalars(c, done[c], "s3_")
                for c in chunks:
                    dve.wait_ge(sm["s3_qm"], done[c])
                    stats(lambda t: PS[c][:, t, 0:DH], c, done[c], "s3_q")
                for c in chunks:
                    norm_scalars(c, done[c], "s3_q")

            @block.scalar
            def _(act):
                def normalise(dst, src, c, k):
                    for t in range(CT):
                        last = nc.scalar.activation(dst(t), src(t), ACT.Identity, bias=nb[c][:, t:t + 1],
                                                    scale=rs[c][:, t:t + 1])
                    return last

                def deviations(s, src, ready, done, eps=True):
                    for c in chunks:
                        act.wait_ge(sm[ready], done[c])
                        nc.scalar.activation(std[c][:, :], src(c), ACT.Sqrt,
                                             bias=top.eps[:, :] if eps else 0.0).then_inc(sm[s + "std"], 1)

                for c in chunks:
                    act.dma_start(X[c][:, :, :], dram["x"][:, CT * c:CT * c + CT, :]).then_inc(x_in[c], 16)
                act.wait_ge(sm["eps"], 1)
                variance = lambda c: mv[c][:, :, 1]
                deviations("s1_", variance, "s1_mv", done)
                for c in chunks:
                    act.wait_ge(sm["s1_norm"], done[c])
                    normalise(lambda t: n[c][:, t, :], lambda t: X[c][:, t, :], c, done[c])\
                        .then_inc(sm["s1_n"], 1)
                for c in chunks:
                    act.wait_ge(sm["zeroed"], done[c])
                    act.wait_ge(sm["s1_scores"], done[c])
                    for a in range(2):
                        seg = slice(SEG * a, SEG * a + SEG)
                        last = nc.scalar.activation(expS[c][seg, :, seg], PS[c][seg, :, seg], ACT.Exp,
                                                    scale=float(D) ** -0.5)
                    last.then_inc(sm["s1_E"], 1)
                deviations("s1_o", lambda c: tmp[c][:, :], "s1_var", done, eps=False)
                for c in chunks:
                    act.wait_ge(sm["s1_onorm"], done[c])
                    normalise(lambda t: y[c][:, t, :], lambda t: PS[c][:, t, :], c, done[c])\
                        .then_inc(sm["s1_y"], 1)
                deviations("s2_", variance, "s2_mv", done)
                for c in chunks:
                    act.wait_ge(sm["s2_norm"], done[c])
                    normalise(lambda t: n[c][:, t, :], lambda t: X[c][:, t, :], c, done[c])\
                        .then_inc(sm["s2_n"], 1)
                for c in chunks:
                    act.wait_ge(sm["s2_nT_psum"], done[c])
                    nc.scalar.activation(nT[c][:, :, :], PS[c][:, :, :], ACT.Copy).then_inc(sm["s2_nT"], 1)
                deviations("s2_o", lambda c: tmp[c][:, :], "s2_var", done)
                for c in chunks:
                    act.wait_ge(sm["s2_onorm"], done[c])
                    normalise(lambda t: y[c][:, t, :], lambda t: PS[c][:, t, :], c, done[c])\
                        .then_inc(sm["s2_y"], 1)
                deviations("s3_", variance, "s3_mv", done)
                for c in chunks:
                    act.wait_ge(sm["s3_norm"], done[c])
                    normalise(lambda t: n[c][:, t, :], lambda t: X[c][:, t, :], c, done[c])\
                        .then_inc(sm["s3_n"], 1)
                for c in chunks:
                    act.wait_ge(sm["s3_nT_psum"], done[c])
                    nc.scalar.activation(nT[c][:, :, :], PS[c][:, :, :], ACT.Copy).then_inc(sm["s3_nT"], 1)
                deviations("s3_q", variance, "s3_qmv", done)
                for c in chunks:
                    act.wait_ge(sm["s3_qnorm"], done[c])
                    normalise(lambda t: z[c][:, t, :], lambda t: PS[c][:, t, 0:DH], c, done[c])\
                        .then_inc(sm["s3_z"], 1)
                for c in chunks:
                    if c == 0:
                        act.wait_ge(sm["loaded"], 16 * len(OTHERS))
                    act.wait_ge(sm["s3_zT_psum"], done[c])
                    nc.scalar.activation(HT[c][:, :], PS[c][0:DH, :, :].rearrange("p t d -> p (t d)"),
                                         ACT.Identity, bias=top.ln_gb[:, 1:2], scale=top.ln_gb[:, 0:1])\
                        .then_inc(sm["s3_H"], 1)
                for c in chunks:
                    act.wait_ge(sm["s3_pre"], done[c])
                    nc.scalar.activation(u[c][:, :], PS[c][0:PROJ, :, :].rearrange("p t d -> p (t d)"), ACT.Gelu,
                                         bias=top.b1[:, :]).then_inc(sm["s3_hidden"], 1)
                for c in chunks:
                    act.wait_ge(sm["s3_score_psum"], done[c])
                    nc.scalar.activation(score[c][:, :, :, :],
                                         PS[c][0:1, :, :].rearrange("a (b r) p -> a b p r", b=2),
                                         ACT.Identity, bias=top.b2[:, :]).then_inc(sm["s3_score"], 1)

            @block.gpsimd
            def _(pool):
                nc.gpsimd.memset(top.eps_rms[:, :], RMS_EPS)
                nc.gpsimd.memset(top.eps[:, :], LN_EPS).then_inc(sm["eps"], 1)
                nc.gpsimd.memset(top.ones_bf[:, :], 1.0)
                for c in chunks:
                    nc.gpsimd.memset(expS[c][:, :, :], 0.0).then_inc(sm["zeroed"], 1)
                for s in ("s1", "s2"):
                    for c in chunks:
                        pool.wait_ge(sm[s + "_y"], done[c])
                        nc.gpsimd.tensor_tensor(X[c][:, :, :], X[c][:, :, :], y[c][:, :, :], ALU.add).then_inc(sm[s + "_x"], 1)

            @block.tensor
            def _(pe):
                def transposes(dst, src, ident, n=CT):
                    for t in range(n):
                        last = nc.tensor.transpose(dst(t), src(t), ident)
                    return last

                def mm(out, lhsT, rhs, start=True, stop=True):
                    return nc.tensor.matmul(out, lhsT, rhs, start=start, stop=stop)

                pe.wait_ge(sm["parts"], 1)
                transposes(lambda t: partsT[:, t, :], lambda t: part[:, t, :], top.ident_bf[:, :], 3)\
                    .then_inc(sm["parts_psum"], 1)
                pe.wait_ge(sm["parts_out"], 1)
                for c in chunks:
                    pe.wait_ge(sm["s1_n"], done[c])
                    transposes(lambda t: PS[c][:, t, :], lambda t: n[c][:, t, :], top.ident[:, :])\
                        .then_inc(sm["s1_nT_psum"], 1)
                for c in chunks:
                    pe.wait_ge(sm["s1_nT"], done[c])
                    for t in range(CT):
                        last = mm(PS[c][:, t, :], nT[c][:, t, :], nT[c][:, t, :])
                    last.then_inc(sm["s1_scores"], 1)
                for c in chunks:
                    pe.wait_ge(sm["s1_E"], done[c])
                    for t in range(CT):
                        last = mm(PS[c][:, t, :], expS[c][:, t, :], n[c][:, t, :])
                    last.then_inc(sm["s1_O"], 1)
                for c in chunks:
                    pe.wait_ge(sm["s2_n"], done[c])
                    transposes(lambda t: PS[c][:, t, :], lambda t: n[c][:, t, :], top.ident[:, :])\
                        .then_inc(sm["s2_nT_psum"], 1)
                for c in chunks:
                    pe.wait_ge(sm["s2_nT"], done[c])
                    for t in range(CT):
                        last = mm(PS[c][:, t, :], nT[c][:, t, :], top.hadamard[:, :])
                    last.then_inc(sm["s2_xh"], 1)
                for c in chunks:
                    pe.wait_ge(sm["s2_q"], done[c])
                    PAb = PS[c][:, 0:CT // 2, :].bitcast(BF16).rearrange("p a (b d) -> p (a b) d", b=2)
                    transposes(lambda t: PAb[:, t, :], lambda t: q[c][:, t, :], top.ident_bf[:, :])\
                        .then_inc(sm["s2_qT_psum"], 1)
                for c in chunks:
                    pe.wait_ge(sm["s2_qT"], done[c])
                    for t in range(CT):
                        for j in range(3):
                            last = mm(PS[c][:, t, :], qT[c][:, t, :], top.ternT[:, j, :], j == 0, j == 2)
                    last.then_inc(sm["s2_O"], 1)
                for c in chunks:
                    pe.wait_ge(sm["s3_n"], done[c])
                    transposes(lambda t: PS[c][:, t, :], lambda t: n[c][:, t, :], top.ident[:, :])\
                        .then_inc(sm["s3_nT_psum"], 1)
                for c in chunks:
                    if c == 0:
                        pe.wait_ge(sm["mean_w_out"], 1)
                    pe.wait_ge(sm["s3_nT"], done[c])
                    for t in range(CT):
                        last = mm(PS[c][:, t, 0:DH], nT[c][:, t, :], top.w_qmeanT[:, :])
                    last.then_inc(sm["s3_qm"], 1)
                for c in chunks:
                    pe.wait_ge(sm["s3_z"], done[c])
                    transposes(lambda t: PS[c][0:DH, t, :], lambda t: z[c][:, t, :], top.ident[:, :])\
                        .then_inc(sm["s3_zT_psum"], 1)
                for c in chunks:
                    pe.wait_ge(sm["s3_H"], done[c])
                    for a in range(2):
                        last = mm(PS[c][0:PROJ, 4 * a:4 * a + 4, :], top.w1T[:, :], HT[c][:, S * a:S * a + S])
                    last.then_inc(sm["s3_pre"], 1)
                for c in chunks:
                    pe.wait_ge(sm["s3_hidden"], done[c])
                    for a in range(2):
                        last = mm(PS[c][0:1, 4 * a:4 * a + 4, :], top.w2T[:, :], u[c][:, S * a:S * a + S])
                    last.then_inc(sm["s3_score_psum"], 1)
        ph.close()


def gated_attention_phase(nc, top, dram):
    with ExitStack() as ctx:
        ph = Phase(nc, ctx, "b_")
        sm = ph.sems(
            "scores_in top8 replaced mask_row zeroed tok_psum tok mask_bf exp_gate gate_den gate rank_psum rank_sub "
            "rank rank_rows_psum rank_rows rank_wide selT plain sel gather_psum nonsel bars gathered "
            "qk_psum qk_out qk_out_a v_psum v_out c_psum c_out yuc_psum yu_copy yu dy "
            "dots_psum diag_d diag_a dmax dmax0 centred probs em dsum den rden probs_n blocks "
            "O_psum O_out Y_psum Y")
        NQ = TILES // 16
        SC = [ph.sb(f"SC{j}", [B, S]) for j in range(3)]
        top8 = ph.sb("top8", [B, 8])
        mask_row = ph.sb("mask_row", [B, S])
        tok = ph.sb("tok", [128, 2, R, B])
        mask_bf = ph.sb("mask_bf", [128, R, B], BF16)
        egate = ph.sb("egate", [128, R, B])
        gden = ph.sb("gden", [128, R, B])
        gate = ph.sb("gate", [128, R, B])
        rank = ph.sb("rank", [128, R, B])
        rank_rows = ph.sb("rank_rows", [B, S], BF16)
        SEL = ph.sb("SEL", [128, TILES, NSEL])
        gq = ph.sb("gq", [128, B, TOP_K])
        gv = ph.sb("gv", [128, B, TOP_K])
        means = ph.sb("means", [128, 2, B])
        QK = ph.sb("QK", [128, HEADS // 2, 2, B * TOP_K])
        V = ph.sb("V", [128, NQ, HEADS * DH])
        mv_ = ph.sb("meanv", [128, HEADS // 2, 2 * B])
        ya = ph.sb("ya", [B, D])
        dY = ph.sb("dY", [B, D])
        yu = ph.sb("yu", [B, D])
        diag = [ph.sb(f"diag{Q}", [128, HEADS, TOP_K]) for Q in range(NQ)]
        dmax = [ph.sb(f"dmax{Q}", [128, HEADS]) for Q in range(NQ)]
        em = [ph.sb(f"em{Q}", [128, HEADS]) for Q in range(NQ)]
        dsum = [ph.sb(f"dsum{Q}", [128, HEADS]) for Q in range(NQ)]
        PT = [ph.sb(f"PT{Q}", [128, HEADS, 128]) for Q in range(NQ)]
        OT = ph.sb("OT", [128, HEADS // 2, 128])
        P0 = ph.ps("P0", [128, 4, 512])
        P1 = ph.ps("P1", [128, 4, 512])
        HALF = HEADS // 4
        place = lambda h: h % 2 * (HEADS // 2) + h // 2
        bcast = lambda a, n: a.rearrange("p (t o) -> p t o", o=1).broadcast_to([128, a.shape[1], n])
        with nc.Block() as block:

            @block.sync
            def _(sp):
                sp.dma_start(SC[0][:, :], dram["scores"].rearrange("a (b s) -> (a b) s", b=B))\
                    .then_inc(sm["scores_in"], 16)

            @block.gpsimd
            def _(pool):
                nc.gpsimd.memset(SEL[:, :, NSEL - 1:NSEL], 1.0).then_inc(sm["zeroed"], 1)
                for Q in range(NQ):
                    nc.gpsimd.memset(PT[Q][:, :, :], 0.0).then_inc(sm["zeroed"], 1)

            @block.vector
            def _(dve):
                dve.wait_ge(sm["scores_in"], 16)
                for t in range(TOP_K // 8):
                    src = SC[0] if t == 0 else SC[1 + (t - 1) % 2]
                    if t:
                        dve.wait_ge(sm["replaced"], t)
                    nc.vector.max(top8[:, :], src[:, :]).then_inc(sm["top8"], 1)
                    dve.wait_ge(sm["top8"], t + 1)
                    nc.vector.match_replace(SC[1 + t % 2][:, :], top8[:, :], src[:, :], LOWEST)\
                        .then_inc(sm["replaced"], 1)
                dve.wait_ge(sm["replaced"], TOP_K // 8)
                nc.vector.tensor_tensor(mask_row[:, :], SC[0][:, :], SC[1 + (TOP_K // 8 - 1) % 2][:, :],
                                        ALU.not_equal).then_inc(sm["mask_row"], 1)
                dve.wait_ge(sm["tok_psum"], 1)
                nc.vector.tensor_copy(mask_bf[:, :, :], P0[:, 0, R * B:2 * R * B].rearrange("p (r b) -> p r b", r=R))\
                    .then_inc(sm["mask_bf"], 1)
                nc.vector.tensor_copy(tok[:, :, :, :], P0[:, 0, 0:2 * R * B].rearrange("p (k r b) -> p k r b", k=2, r=R))\
                    .then_inc(sm["tok"], 1)
                dve.wait_ge(sm["exp_gate"], 1)
                nc.vector.tensor_scalar(gden[:, :, :], egate[:, :, :], 1.0, None, ALU.add).then_inc(sm["gate_den"], 1)
                dve.wait_ge(sm["gate_den"], 1)
                nc.vector.reciprocal(gate[:, :, :], gden[:, :, :]).then_inc(sm["gate"], 1)
                dve.wait_ge(sm["rank_psum"], 1)
                dve.wait_ge(sm["tok"], 1)
                nc.vector.scalar_tensor_tensor(
                    out=rank[:, :, :], in0=P1[:, 0, 0:R * B].rearrange("p (r b) -> p r b", r=R), scalar=float(TOP_K),
                    in1=tok[:, 1, :, :], op0=ALU.subtract, op1=ALU.mult).then_inc(sm["rank_sub"], 1)
                dve.wait_ge(sm["rank_sub"], 1)
                nc.vector.tensor_scalar(rank[:, :, :], rank[:, :, :], float(TOP_K), None, ALU.add)\
                    .then_inc(sm["rank"], 1)
                dve.wait_ge(sm["rank"], 1)
                sel4 = SEL[:, :, :].rearrange("p (b r) j -> p b r j", b=B)
                rank4 = rank[:, :, :].rearrange("p r (b o) -> p b r o", o=1).broadcast_to([128, B, R, TOP_K + 1])
                gate4 = gate[:, :, :].rearrange("p r (b o) -> p b r o", o=1).broadcast_to([128, B, R, TOP_K])
                for b in range(B):
                    nc.vector.tensor_tensor(
                        sel4[:, b, :, TOP_K:2 * TOP_K + 1], rank4[:, b, :, :],
                        top.iota[:, 0:TOP_K + 1].rearrange("p (o j) -> p o j", o=1).broadcast_to([128, R, TOP_K + 1]),
                        ALU.is_equal).then_inc(sm["plain"], 1)
                dve.wait_ge(sm["gate"], 1)
                for b in range(B):
                    dve.wait_ge(sm["plain"], b + 1)
                    nc.vector.tensor_tensor(sel4[:, b, :, 0:TOP_K], sel4[:, b, :, TOP_K:2 * TOP_K],
                                            gate4[:, b, :, :], ALU.mult).then_inc(sm["sel"], 1)
                dve.wait_ge(sm["rank_rows_psum"], 1)
                nc.vector.tensor_copy(rank_rows[:, :], P1[0:B, 1, :]).then_inc(sm["rank_rows"], 1)
                dve.wait_ge(sm["rank_wide"], 1)
                for Q in range(NQ):
                    nc.vector.tensor_scalar(top.selT[Q][:, :], P1[:, 2 + Q, :], top.iota_col[:, :], None,
                                            ALU.is_equal).then_inc(sm["selT"], 1)
                dve.wait_ge(sm["gather_psum"], 1)
                G = P0[:, 0:2, :].rearrange("p a (b j) -> p (a b) j", j=128)
                nc.vector.tensor_scalar(means[:, 0, :], G[:, :, NSEL - 1], 1.0 / S, None, ALU.mult)
                nc.vector.tensor_scalar(means[:, 1, :], G[:, :, NSEL - 2], 1.0 / (S - TOP_K), None, ALU.mult)\
                    .then_inc(sm["bars"], 1)
                nc.vector.tensor_copy(gq[:, :, :], G[:, :, 0:TOP_K])
                dve.wait_ge(sm["bars"], 1)
                nc.vector.tensor_tensor(gv[:, :, :], G[:, :, TOP_K:2 * TOP_K], bcast(means[:, 1, :], TOP_K),
                                        ALU.subtract).then_inc(sm["gathered"], 1)
                dve.wait_ge(sm["qk_psum"], 1)
                nc.vector.tensor_copy(QK[:, 0:HALF, :, :], P1[:, :, :].rearrange("p i (k t) -> p i k t", k=2))\
                    .then_inc(sm["qk_out"], 1)
                dve.wait_ge(sm["v_psum"], 1)
                nc.vector.tensor_copy(V[:, :, :], P1[:, :, :].rearrange("p (Q a) n -> p Q (a n)", a=2))\
                    .then_inc(sm["v_out"], 1)
                dve.wait_ge(sm["c_psum"], 1)
                nc.vector.tensor_copy(mv_[:, :, :], P0[:, 0, 0:128].rearrange("p (i c) -> p i c", i=HEADS // 2))\
                    .then_inc(sm["c_out"], 1)
                dve.wait_ge(sm["yuc_psum"], 1)
                nc.vector.tensor_copy(ya[:, :], P0[0:B, 1, 0:D]).then_inc(sm["yu_copy"], 1)
                dve.wait_ge(sm["yu_copy"], 1)
                nc.vector.tensor_tensor(yu[:, :], ya[:, :], top.b_out[:, :], ALU.add).then_inc(sm["yu"], 1)
                nc.vector.tensor_tensor(dY[:, :], P0[0:B, 1, D:2 * D], ya[:, :], ALU.subtract).then_inc(sm["dy"], 1)
                for Q in range(NQ):
                    dve.wait_ge(sm["dots_psum"], Q + 1)
                    dots = (P0, P1)[Q][:, :, :].rearrange("p a (h k) -> p (a h) k", k=128)
                    for j in range(2):
                        rows = slice(32 * j, 32 * j + 32)
                        last = nc.vector.tensor_copy(diag[Q][rows, :, :], dots[rows, :, rows])
                    last.then_inc(sm["diag_d"], 1)
                for Q in range(NQ):
                    dve.wait_ge(sm["diag_d"], Q + 1)
                    dve.wait_ge(sm["diag_a"], Q + 1)
                    nc.vector.tensor_reduce(dmax[Q][:, :], diag[Q][:, :, :], AX.X, ALU.max).then_inc(sm["dmax"], 1)
                    dve.wait_ge(sm["dmax"], Q + 1)
                    nc.vector.tensor_scalar(dmax[Q][:, :], dmax[Q][:, :], 0.0, None, ALU.max).then_inc(sm["dmax0"], 1)
                    dve.wait_ge(sm["dmax0"], Q + 1)
                    nc.vector.tensor_tensor(diag[Q][:, :, :], diag[Q][:, :, :], bcast(dmax[Q][:, :], TOP_K),
                                            ALU.subtract).then_inc(sm["centred"], 1)
                for Q in range(NQ):
                    dve.wait_ge(sm["probs"], Q + 1)
                    nc.vector.tensor_reduce(dsum[Q][:, :], diag[Q][:, :, :], AX.X, ALU.add).then_inc(sm["dsum"], 1)
                    dve.wait_ge(sm["dsum"], Q + 1)
                    nc.vector.scalar_tensor_tensor(out=dsum[Q][:, :], in0=em[Q][:, :], scalar=float(S - TOP_K),
                                                   in1=dsum[Q][:, :], op0=ALU.mult, op1=ALU.add)\
                        .then_inc(sm["den"], 1)
                    dve.wait_ge(sm["den"], Q + 1)
                    nc.vector.reciprocal(dsum[Q][:, :], dsum[Q][:, :]).then_inc(sm["rden"], 1)
                    dve.wait_ge(sm["rden"], Q + 1)
                    nc.vector.tensor_tensor(diag[Q][:, :, :], diag[Q][:, :, :], bcast(dsum[Q][:, :], TOP_K),
                                            ALU.mult).then_inc(sm["probs_n"], 1)
                    dve.wait_ge(sm["probs_n"], Q + 1)
                    dve.wait_ge(sm["zeroed"], 1 + NQ)
                    for j in range(4):
                        rows = slice(32 * j, 32 * j + 32)
                        last = nc.vector.transpose(PT[Q][rows, :, rows], diag[Q][rows, :, :])
                    last.then_inc(sm["blocks"], 1)
                for Q in range(NQ):
                    dve.wait_ge(sm["O_psum"], Q + 1)
                    nc.vector.tensor_copy(OT[:, :, :], P0[:, 0:2, :].rearrange("p a (i t) -> p (a i) t", t=128))\
                        .then_inc(sm["O_out"], 1)
                    dve.wait_ge(sm["Y_psum"], Q + 1)
                    nc.vector.tensor_copy(top.Y[Q][:, :], P0[:, 2, 0:D])
                    nc.vector.tensor_copy(top.yU[Q][:, :], P0[:, 2, D:2 * D]).then_inc(sm["Y"], 1)

            @block.scalar
            def _(act):
                act.wait_ge(sm["tok"], 1)
                nc.scalar.activation(egate[:, :, :], tok[:, 0, :, :], ACT.Exp, scale=-1.0).then_inc(sm["exp_gate"], 1)
                act.wait_ge(sm["qk_psum"], 2)
                nc.scalar.activation(QK[:, HALF:, :, :], P0[:, :, :].rearrange("p i (k t) -> p i k t", k=2), ACT.Copy)\
                    .then_inc(sm["qk_out_a"], 1)
                for Q in range(NQ):
                    act.wait_ge(sm["dots_psum"], Q + 1)
                    dots = (P0, P1)[Q][:, :, :].rearrange("p a (h k) -> p (a h) k", k=128)
                    for j in range(2, 4):
                        rows = slice(32 * j, 32 * j + 32)
                        last = nc.scalar.activation(diag[Q][rows, :, :], dots[rows, :, rows], ACT.Copy)
                    last.then_inc(sm["diag_a"], 1)
                for Q in range(NQ):
                    act.wait_ge(sm["centred"], Q + 1)
                    nc.scalar.activation(em[Q][:, :], dmax[Q][:, :], ACT.Exp, scale=-float(DH) ** -0.5)
                    nc.scalar.activation(diag[Q][:, :, :], diag[Q][:, :, :], ACT.Exp, scale=float(DH) ** -0.5)\
                        .then_inc(sm["probs"], 1)

            @block.tensor
            def _(pe):
                def mm(out, lhsT, rhs, start=True, stop=True):
                    return nc.tensor.matmul(out, lhsT, rhs, start=start, stop=stop)

                pe.wait_ge(sm["mask_row"], 1)
                for k, src in enumerate((SC[0], mask_row)):
                    by_r = src[:, :].rearrange("b (p r) -> b r p", r=R)
                    for r in range(R):
                        o = (k * R + r) * B
                        last = nc.tensor.transpose(P0[:, 0, o:o + B], by_r[:, r, :], top.ident[0:B, 0:B])
                last.then_inc(sm["tok_psum"], 1)
                pe.wait_ge(sm["mask_bf"], 1)
                mm(P1[:, 0, 0:R * B], top.lower[:, :], mask_bf[:, :, :], True, False)
                for r in range(1, R):
                    for r2 in range(r):
                        last = mm(P1[:, 0, r * B:r * B + B], top.ones_bf[:, :], mask_bf[:, r2, :], False,
                                  r == R - 1 and r2 == r - 1)
                last.then_inc(sm["rank_psum"], 1)
                pe.wait_ge(sm["rank"], 1)
                for r in range(R):
                    last = nc.tensor.transpose(P1[0:B, 1, 128 * r:128 * r + 128], rank[:, r, :], top.ident[:, :])
                last.then_inc(sm["rank_rows_psum"], 1)
                pe.wait_ge(sm["tok"], 1)
                pe.wait_ge(sm["zeroed"], 1)
                for b in range(B):
                    pe.wait_ge(sm["sel"], b + 1)
                    for r in range(R):
                        last = mm(P0[:, b // 4, 128 * (b % 4):128 * (b % 4) + NSEL], top.N3[:, R * b + r, :],
                                  SEL[:, R * b + r, :], r == 0, r == R - 1)
                last.then_inc(sm["gather_psum"], 1)
                pe.wait_ge(sm["rank_rows"], 1)
                for Q in range(NQ):
                    last = mm(P1[:, 2 + Q, :], top.batch_rows_bf[:, Q, :], rank_rows[:, :])
                last.then_inc(sm["rank_wide"], 1)
                pe.wait_ge(sm["gathered"], 1)
                pe.wait_ge(sm["selT"], NQ)
                for half in range(2):
                    for i in range(HALF):
                        for k in range(2):
                            w = k * HEADS * DH + (half * HALF + i) * 128
                            last = mm((P1, P0)[half][:, i, 256 * k:256 * k + 256], top.w_qkvT[:, w:w + 128],
                                      gq[:, :, :])
                    last.then_inc(sm["qk_psum"], 1)
                pe.wait_ge(sm["qk_out"], 1)
                for Q in range(NQ):
                    for a in range(2):
                        w = 2 * HEADS * DH + 512 * a
                        last = mm(P1[:, 2 * Q + a, :], gv[:, 4 * Q:4 * Q + 4, :], top.w_qkvT[:, w:w + 512])
                last.then_inc(sm["v_psum"], 1)
                pe.wait_ge(sm["qk_out_a"], 1)
                for i in range(HEADS // 2):
                    w = 2 * HEADS * DH + 128 * i
                    last = mm(P0[:, 0, 16 * i:16 * i + 16], top.w_qkvT[:, w:w + 128], means[:, :, :])
                last.then_inc(sm["c_psum"], 1)
                pe.wait_ge(sm["c_out"], 1)
                for k in range(2):
                    for i in range(HEADS // 2):
                        last = mm(P0[0:B, 1, D * k:D * k + D], mv_[:, i, B * k:B * k + B], top.w_outT[:, i, :],
                                  i == 0, i == HEADS // 2 - 1)
                last.then_inc(sm["yuc_psum"], 1)
                for Q in range(NQ):
                    if Q == 0:
                        pe.wait_ge(sm["dy"], 1)
                    else:
                        pe.wait_ge(sm["v_out"], 1)
                    dots = (P0, P1)[Q]
                    for h in range(HEADS):
                        rows = slice(DH * (h % 2), DH * (h % 2) + DH)
                        at = place(h)
                        last = mm(dots[:, at // 4, 128 * (at % 4):128 * (at % 4) + 128],
                                  QK[rows, h // 2, 0, 128 * Q:128 * Q + 128], QK[rows, h // 2, 1, 128 * Q:128 * Q + 128])
                    last.then_inc(sm["dots_psum"], 1)
                for Q in range(NQ):
                    pe.wait_ge(sm["blocks"], Q + 1)
                    if Q:
                        pe.wait_ge(sm["O_out"], Q)
                    for h in range(HEADS):
                        rows = slice(DH * (h % 2), DH * (h % 2) + DH)
                        last = mm(P0[rows, h // 8, 128 * (h // 2 % 4):128 * (h // 2 % 4) + 128],
                                  V[:, Q, DH * h:DH * h + DH], PT[Q][:, place(h), :])
                    last.then_inc(sm["O_psum"], 1)
                    pe.wait_ge(sm["O_out"], Q + 1)
                    if Q:
                        pe.wait_ge(sm["Y"], Q)
                    for i in range(HEADS // 2):
                        mm(P0[:, 2, 0:D], OT[:, i, :], top.w_outT[:, i, :], i == 0, False)
                    mm(P0[:, 2, 0:D], top.batch_rows[:, Q, :], dY[:, :], False, True)
                    mm(P0[:, 2, D:2 * D], top.batch_rows[:, Q, :], yu[:, :]).then_inc(sm["Y_psum"], 1)
        ph.close()


def projection_phase(nc, top, dram):
    with ExitStack() as ctx:
        ph = Phase(nc, ctx, "c_")
        sm = ph.sems("y_psum y_stats y_mv y_std y_rstd y_norm y x stats mv var2 std rstd norm nb2 a n4 aT_psum aT "
                     "q_psum k_psum v_psum q1 k1 qr kr q2 k2 q3 k3 v_ready zeroed")
        stored = [ph.sem(f"stored{c}") for c in range(2)]
        two = range(2)
        a = [ph.sb(f"a{c}", [128, CT, D]) for c in two]
        y = [ph.sb(f"y{c}", [128, CT, D]) for c in two]
        aT = [ph.sb(f"aT{c}", [128, 2, S]) for c in two]
        Qp = [ph.sb(f"Qp{c}", [128, 3, 2, S], BF16) for c in two]
        Qr = [ph.sb(f"Qr{c}", [128, 2, S]) for c in two]
        Kp = [ph.sb(f"Kp{c}", [KVD, 3, 2, S], BF16) for c in two]
        Kr = [ph.sb(f"Kr{c}", [KVD, 2, S]) for c in two]
        st = [ph.sb(f"st{c}", [128, CT, 6]) for c in two]
        mv = [ph.sb(f"mv{c}", [128, CT, 2]) for c in two]
        std = [ph.sb(f"std{c}", [128, 2, CT]) for c in two]
        rs = [ph.sb(f"rs{c}", [128, 2, CT]) for c in two]
        nb = [ph.sb(f"nb{c}", [128, 2, CT]) for c in two]
        PA = [ph.ps(f"PA{c}", [128, CT, D]) for c in two]
        PB = [ph.ps(f"PB{c}", [128, CT, D]) for c in two]
        X, N4 = top.X, top.N4
        n_stored = [0, 0]

        with nc.Block() as block:

            @block.sync
            def _(sp):
                for k in range(CHUNKS):
                    c = k % 2
                    sp.wait_ge(sm["q3"], k + 1)
                    sp.wait_ge(sm["k3"], k + 1)
                    for b in (0, 1, 1) if k == CHUNKS - 1 else (0, 1):
                        entry = 2 * k + b + (1 if n_stored[c] == 12 * (k // 2) + 12 else 0)
                        for slot, n, qpart, kpart in PAIRS:
                            sp.dma_start(dram["q_store"](entry, slot, n), Qp[c][:, qpart:qpart + n, b, :])\
                                .then_inc(stored[c], 16)
                            sp.dma_start(dram["k_store"](entry, slot, n),
                                         Kp[c][:, kpart:kpart + 1, b, :].broadcast_to([KVD, n, S]))\
                                .then_inc(stored[c], 16)
                            n_stored[c] += 2
                for c in two:
                    sp.wait_ge(stored[c], 16 * n_stored[c])

            @block.gpsimd
            def _(pool):
                nc.gpsimd.memset(top.V4[:, :, :, HD4:VW], 0.0).then_inc(sm["zeroed"], 1)
                pool.wait_ge(sm["zeroed"], 1)
                nc.gpsimd.memset(top.V4[:, :, :, HD4:HD4 + 1], 1.0).then_inc(sm["zeroed"], 1)
                for k0 in range(0, CHUNKS, 2):
                    for k in (k0, k0 + 1):
                        c = k % 2
                        tiles = slice(CT * k, CT * k + CT)
                        pool.wait_ge(sm["y"], k + 1)
                        nc.gpsimd.tensor_tensor(X[:, tiles, :], X[:, tiles, :], y[c][:, :, :], ALU.add)\
                            .then_inc(sm["x"], 1)
                    for k in (k0, k0 + 1):
                        c = k % 2
                        for dst, src, s1, s2 in ((Kp, Kr, "k2", "k3"), (Qp, Qr, "q2", "q3")):
                            pool.wait_ge(sm[s1], k + 1)
                            nc.gpsimd.tensor_tensor(dst[c][:, 2, :, :], src[c][:, :, :], dst[c][:, 1, :, :],
                                                    ALU.subtract).then_inc(sm[s2], 1)

            @block.vector
            def _(dve):
                def stats(src, c, k, s):
                    for t in range(CT):
                        last = nc.vector.bn_stats(st[c][:, t, :], src(t))
                    last.then_inc(sm[s + "stats"], 1)
                    dve.wait_ge(sm[s + "stats"], k + 1)
                    for t in range(CT):
                        last = nc.vector.bn_aggr(mv[c][:, t, :], st[c][:, t, :])
                    last.then_inc(sm[s + "mv"], 1)

                def chunk_y(k):
                    c = k % 2
                    dve.wait_ge(sm["y_psum"], k + 1)
                    stats(lambda t: PA[c][:, t, :], c, k, "y_")
                    dve.wait_ge(sm["y_std"], k + 1)
                    nc.vector.reciprocal(rs[c][:, 0, :], std[c][:, 0, :]).then_inc(sm["y_rstd"], 1)
                    dve.wait_ge(sm["y_rstd"], k + 1)
                    dve.wait_ge(sm["y_mv"], k + 1)
                    nc.vector.scalar_tensor_tensor(out=nb[c][:, 0, :], in0=mv[c][:, :, 0], scalar=-1.0,
                                                   in1=rs[c][:, 0, :], op0=ALU.mult, op1=ALU.mult)\
                        .then_inc(sm["y_norm"], 1)

                def chunk_n(k):
                    c = k % 2
                    tiles = slice(CT * k, CT * k + CT)
                    dve.wait_ge(sm["x"], k + 1)
                    stats(lambda t: X[:, CT * k + t, :], c, k, "")
                    dve.wait_ge(sm["mv"], k + 1)
                    nc.vector.tensor_scalar(nb[c][:, 0, :], mv[c][:, :, 1], LN_EPS, None, ALU.add)
                    nc.vector.tensor_scalar(nb[c][:, 1, :], mv[c][:, :, 1], 1.0 + RMS_EPS, RMS_EPS * LN_EPS,
                                            ALU.mult, ALU.add).then_inc(sm["var2"], 1)
                    dve.wait_ge(sm["std"], k + 1)
                    nc.vector.reciprocal(rs[c][:, :, :], std[c][:, :, :]).then_inc(sm["rstd"], 1)
                    dve.wait_ge(sm["rstd"], k + 1)
                    nc.vector.scalar_tensor_tensor(out=nb[c][:, 1, :], in0=mv[c][:, :, 0], scalar=-1.0,
                                                   in1=rs[c][:, 1, :], op0=ALU.mult, op1=ALU.mult)\
                        .then_inc(sm["norm"], 1)
                    for t in range(CT):
                        last = nc.vector.tensor_scalar(N4[:, CT * k + t, :], X[:, CT * k + t, :], mv[c][:, t, 0:1],
                                                       rs[c][:, 0, t:t + 1], ALU.subtract, ALU.mult)
                    last.then_inc(sm["n4"], 1)
                    dve.wait_ge(sm["aT_psum"], k + 1)
                    nc.vector.tensor_copy(aT[c][:, :, :].rearrange("c b (p r) -> c b r p", r=R),
                                          PA[c][:, :, :].rearrange("c (b r) p -> c b r p", b=2)).then_inc(sm["aT"], 1)

                def chunk_p(k):
                    c = k % 2
                    dve.wait_ge(sm["k1"], k + 1)
                    nc.vector.tensor_tensor(Kr[c][:, :, :], PA[c][0:KVD, :, :].rearrange("p (b n) t -> p b (n t)", b=2),
                                            Kp[c][:, 0, :, :], ALU.subtract).then_inc(sm["kr"], 1)
                    dve.wait_ge(sm["q1"], k + 1)
                    nc.vector.tensor_tensor(Qr[c][:, :, :], PB[c][:, :, :].rearrange("p (b n) t -> p b (n t)", b=2),
                                            Qp[c][:, 0, :, :], ALU.subtract).then_inc(sm["qr"], 1)
                    dve.wait_ge(sm["v_psum"], k + 1)
                    if k == 0:
                        dve.wait_ge(sm["zeroed"], 2)
                    nc.vector.tensor_copy(top.V4[:, CT * k:CT * k + CT, :, 0:HD4],
                                          PB[c][:, 0:2, :].rearrange("p a (t g d) -> p (a t) g d", t=4, g=KV4))\
                        .then_inc(sm["v_ready"], 1)

                for k in range(0, CHUNKS, 2):
                    for f in (chunk_y, chunk_n, chunk_p):
                        for c in two:
                            f(k + c)

            @block.scalar
            def _(act):
                for k0 in range(0, CHUNKS, 2):
                    for k in (k0, k0 + 1):
                        c = k % 2
                        act.wait_ge(sm["y_mv"], k + 1)
                        nc.scalar.activation(std[c][:, 0, :], mv[c][:, :, 1], ACT.Sqrt, bias=top.eps[:, :])\
                            .then_inc(sm["y_std"], 1)
                    for k in (k0, k0 + 1):
                        c = k % 2
                        act.wait_ge(sm["y_norm"], k + 1)
                        for t in range(CT):
                            last = nc.scalar.activation(y[c][:, t, :], PA[c][:, t, :], ACT.Identity,
                                                        bias=nb[c][:, 0, t:t + 1], scale=rs[c][:, 0, t:t + 1])
                        last.then_inc(sm["y"], 1)
                    for k in (k0, k0 + 1):
                        c = k % 2
                        act.wait_ge(sm["var2"], k + 1)
                        nc.scalar.activation(std[c][:, :, :], nb[c][:, :, :], ACT.Sqrt).then_inc(sm["std"], 1)
                        act.wait_ge(sm["norm"], k + 1)
                        for t in range(CT):
                            last = nc.scalar.activation(a[c][:, t, :], X[:, CT * k + t, :], ACT.Identity,
                                                        bias=nb[c][:, 1, t:t + 1], scale=rs[c][:, 1, t:t + 1])
                        last.then_inc(sm["a"], 1)
                    for k in (k0, k0 + 1):
                        c = k % 2
                        kp = PA[c][0:KVD, :, :].rearrange("p (b n) t -> p b (n t)", b=2)
                        qp = PB[c][:, :, :].rearrange("p (b n) t -> p b (n t)", b=2)
                        for part, rest, ps, s0, s1, sr, s2 in ((Kp, Kr, kp, "k_psum", "k1", "kr", "k2"),
                                                               (Qp, Qr, qp, "q_psum", "q1", "qr", "q2")):
                            act.wait_ge(sm[s0], k + 1)
                            if k >= 2:
                                act.wait_ge(stored[c], 16 * 12 * (k // 2))
                            nc.scalar.activation(part[c][:, 0, :, :], ps, ACT.Copy).then_inc(sm[s1], 1)
                        for part, rest, sr, s2 in ((Kp, Kr, "kr", "k2"), (Qp, Qr, "qr", "q2")):
                            act.wait_ge(sm[sr], k + 1)
                            nc.scalar.activation(part[c][:, 1, :, :], rest[c][:, :, :], ACT.Copy).then_inc(sm[s2], 1)

            @block.tensor
            def _(pe):
                def mm(out, lhsT, rhs, start=True, stop=True):
                    return nc.tensor.matmul(out, lhsT, rhs, start=start, stop=stop)

                for k0 in range(0, CHUNKS, 2):
                    for k in (k0, k0 + 1):
                        c = k % 2
                        if k >= 2:
                            pe.wait_ge(sm["kr"], k - 1)
                        for t in range(CT):
                            b, r = 2 * k + t // R, t % R
                            rows = slice(TOP_K * (b % 4), TOP_K * (b % 4) + TOP_K)
                            mm(PA[c][:, t, :], top.selT[b // 4][rows, 128 * r:128 * r + 128],
                               top.Y[b // 4][rows, :], True, False)
                            last = mm(PA[c][:, t, :], top.first_row[rows, :], top.yU[b // 4][rows, :], False, True)
                        last.then_inc(sm["y_psum"], 1)
                    for k in (k0, k0 + 1):
                        c = k % 2
                        pe.wait_ge(sm["a"], k + 1)
                        for t in range(CT):
                            last = nc.tensor.transpose(PA[c][:, t, :], a[c][:, t, :], top.ident[:, :])
                        last.then_inc(sm["aT_psum"], 1)
                    for k in (k0, k0 + 1):
                        c = k % 2
                        pe.wait_ge(sm["aT"], k + 1)
                        if k >= 2:
                            pe.wait_ge(sm["v_ready"], k - 1)
                        for b in range(2):
                            last = mm(PA[c][0:KVD, R * b:R * b + R, :], top.wk4T[:, :], aT[c][:, b, :])
                        last.then_inc(sm["k_psum"], 1)
                        for b in range(2):
                            last = mm(PB[c][:, R * b:R * b + R, :], top.wq4T[:, :], aT[c][:, b, :])
                        last.then_inc(sm["q_psum"], 1)
                    for k in (k0, k0 + 1):
                        c = k % 2
                        pe.wait_ge(sm["qr"], k + 1)
                        for t in range(CT):
                            last = mm(PB[c][:, t // 4, KVD * (t % 4):KVD * (t % 4) + KVD],
                                      aT[c][:, t // 4, 128 * (t % 4):128 * (t % 4) + 128], top.wv4T[:, :])
                        last.then_inc(sm["v_psum"], 1)
        ph.close()


def causal_attention_phase(nc, top, dram):
    with ExitStack() as ctx:
        ph = Phase(nc, ctx, "d_")
        sm = ph.sems("zeros ones ones_from max_ones S S_max part1 rest1 part2 rest2 parts mT_psum mT ST P masked PV O_sb O_T rden O_tok")
        two = range(2)
        stacks = [[ph.sem(f"stacks{c}{a}") for a in two] for c in two]
        v_in = [ph.sem(f"v_in{c}") for c in two]
        rows_stored = [ph.sem(f"rows_stored{c}") for c in two]
        rows_in = [ph.sem(f"rows_in{c}") for c in two]
        Qs = [ph.sb(f"Qs{c}", [128, HEADS // 2, S], BF16) for c in two]
        Ks = [ph.sb(f"Ks{c}", [128, KV4, S], BF16) for c in two]
        V = [ph.sb(f"V{c}", [128, QT, KV4, VW]) for c in two]
        mx = [ph.sb(f"mx{c}", [128, QT, HEADS]) for c in two]
        rest = [ph.sb(f"rest{c}", [128, 2, QT, HEADS]) for c in two]
        m3 = [ph.sb(f"m3{c}", [128, QT, 3, HEADS], BF16) for c in two]
        mT = [ph.sb(f"mT{c}", [3 * HEADS, S], BF16) for c in two]
        P = [ph.sb(f"P{k}", [128, 2, PAIRW]) for k in range(4)]
        OT = [ph.sb(f"OT{k}", [128, S]) for k in two]
        rden = ph.sb("rden", [128, QT, 2, 2])
        pS = [ph.ps(f"pS{k}", [128, 512]) for k in two]
        pT = [ph.ps(f"pT{k}", [128, 2, 512]) for k in two]
        pO = ph.ps("pO", [128, S])
        pM = ph.ps("pM", [128, S])
        NS, NT, NG = 3 * HEADS, 3 * HEADS // 2, KV4
        ROWS = SLOTS * HD4
        ALL_ROWS = 2 * ROWS
        WITH_MAX = ALL_ROWS + 6
        ORDER = [8 * a + i for i in range(HEADS // 2) for a in two]
        P_AT = (0, 512, 896, 1152)

        def wait(eng, sem, value):
            if not isinstance(value, int) or value > 0:
                eng.wait_ge(sem, value)

        def steps(eng, step):
            step(0, 0, True)
            with eng.Fori(0, B // 2 - 1) as i:
                step(2 * i + 1, i, True)
                step(2 * i + 2, i + 1, True)
            step(B - 1, B // 2 - 1, False)

        def fills(pair):
            places = [2 * (pair + LEAD) + j for j in two]
            return [(1 + k // HEADS, k % HEADS, f) for k in places for f in range(3)]

        def others(n, m, c, ahead):
            return (n + 1, m + c, 1 - c) if ahead == 1 else (n + 2, m + 1, c)

        def turn(pair, unit, at):
            g, off = divmod(3 * (pair - 2) + unit - 1 - at, 6)
            return None if off else (0 if g >= 0 else 1, g % NG)

        def turns(n, pair, unit, at):
            got = turn(pair, unit, at)
            ended = isinstance(n, int) and n == B
            if got is None or (got[0] == 0 and ended) or (got[0] == 1 and isinstance(n, int) and n == 0):
                return []
            return [(n - got[0], got[1], got[0])]

        LAST_TURNS = [(u // 3, u % 3) for u in range(7)]
        everything = [(k, f) for k in range(HEADS) for f in range(3)]
        SPLIT_AT = HEADS // 2 - LEAD
        parity = [0]

        def par(n):
            if isinstance(n, int):
                parity[0] = n % 2
            else:
                parity[0] = 1 - parity[0]
            return parity[0]

        with nc.Block() as block:

            @block.sync
            def _(sp):
                def load_stack(b, c, u):
                    for a in two:
                        rows = slice(ROWS * a, ROWS * a + ROWS)
                        sp.dma_start(Qs[c][rows, 4 * u:4 * u + 4, :], dram["q_load"](b, 8 * a + 4 * u, 4))\
                            .then_inc(stacks[c][u], 16)
                        sp.dma_start(Ks[c][rows, 2 * a + u:2 * a + u + 1, :], dram["k_load"](b, 2 * a + u, 1))\
                            .then_inc(stacks[c][u], 16)

                def load_v(b, c):
                    sp.dma_start(V[c][:, :, :, :], top.V4[:, bass.ds(b * QT, QT), :, :]).then_inc(v_in[c], 16)

                def max_rows(n, m, c):
                    sp.wait_ge(sm["mT"], n + 1)
                    sp.dma_start(dram["m_store"](c), mT[c][:, :]).then_inc(rows_stored[c], 16)
                    sp.wait_ge(rows_stored[c], 16 * m + 16)
                    for a in two:
                        at = ALL_ROWS + 3 * a
                        sp.dma_start(Qs[c][at:at + 3, :, :], dram["m_load"](c, a))\
                            .then_inc(rows_in[c], 16)

                def step(n, m, more):
                    c = par(n)
                    if more:
                        wait(sp, sm["PV"], n * NG)
                        load_v(n + 1, 1 - c)
                        if not (isinstance(n, int) and n + 2 > B):
                            sp.wait_ge(sm["ST"], n * NT + NT // 2)
                            load_stack(n + 2, c, 0)
                        max_rows(n + 1, m if c == 0 else m + 1, 1 - c)
                        sp.wait_ge(sm["ST"], n * NT + NT)
                        load_stack(n + 2, c, 1)

                sp.wait_ge(sm["zeros"], 2)
                for b in two:
                    for u in two:
                        load_stack(b, b, u)
                load_v(0, 0)
                max_rows(0, 0, 0)
                steps(sp, step)
                for a in two:
                    sp.wait_ge(stacks[0][a], 64 * (B // 2 + 1))

            @block.gpsimd
            def _(pool):
                def step(n, m, more):
                    par(n)
                    for pair in range(HEADS // 2):
                        for unit in range(3):
                            wait_alone(pool, sm["P"], n * NT + 3 * pair + unit + 1)
                            for at in ((P_AT[0],), (P_AT[1],), P_AT[2:])[unit]:
                                view = P[pair % 4][:, :, at:at + 128]
                                last = nc.gpsimd.affine_select(out=view, in_=view, compare_op=ALU.is_ge, fill=0.0,
                                                               base=0, pattern=[[0, 2], [1, 128]],
                                                               channel_multiplier=-1)
                            last.then_inc(sm["masked"], 1)

                for c in two:
                    nc.gpsimd.memset(Ks[c][0:ALL_ROWS, :, :], 0.0).then_inc(sm["zeros"], 1)
                    nc.gpsimd.memset(Ks[c][ALL_ROWS:128, :, :], 1.0).then_inc(sm["ones"], 1)
                for c in two:
                    pool.wait_ge(sm["ones"], c + 1)
                    for a in two:
                        view = Ks[c][ALL_ROWS:128, 2 * a:2 * a + 2, :]
                        nc.gpsimd.affine_select(out=view, in_=view, compare_op=ALU.is_ge, fill=0.0, base=-3 * a,
                                                pattern=[[0, 2], [0, S]], channel_multiplier=1)\
                            .then_inc(sm["ones_from"], 1)
                        pool.wait_ge(sm["ones_from"], 2 * c + a + 1)
                        nc.gpsimd.affine_select(out=view, in_=view, compare_op=ALU.is_ge, fill=0.0, base=3 * a + 2,
                                                pattern=[[0, 2], [0, S]], channel_multiplier=-1)\
                            .then_inc(sm["max_ones"], 1)
                steps(pool, step)

            @block.vector
            def _(dve):
                def maxima(n, c, some):
                    for k, f in some:
                        h, fill = ORDER[k], 3 * k + f
                        dve.wait_ge(sm["S"], n * NS + fill + 1)
                        src = pS[fill % 2]
                        if f < 2:
                            last = nc.vector.reduce_max(mx[c][:, 3 - f, h:h + 1], src[:, 0:512 - 128 * f], AX.X)
                        else:
                            nc.vector.reduce_max(mx[c][:, 1, h:h + 1], src[:, 0:256], AX.X)
                            last = nc.vector.reduce_max(mx[c][:, 0, h:h + 1], src[:, 256:384], AX.X)
                        last.then_inc(sm["S_max"], 1)

                def split(n, c):
                    dve.wait_ge(sm["S_max"], n * NS + NS)
                    nc.vector.tensor_scalar(m3[c][:, :, 0, :], mx[c][:, :, :], -1.0, None, ALU.mult)\
                        .then_inc(sm["part1"], 1)
                    dve.wait_ge(sm["part1"], n + 1)
                    nc.vector.scalar_tensor_tensor(out=rest[c][:, 0, :, :], in0=mx[c][:, :, :], scalar=-1.0,
                                                   in1=m3[c][:, :, 0, :], op0=ALU.mult, op1=ALU.subtract)\
                        .then_inc(sm["rest1"], 1)
                    dve.wait_ge(sm["rest1"], n + 1)
                    nc.vector.tensor_copy(m3[c][:, :, 1, :], rest[c][:, 0, :, :]).then_inc(sm["part2"], 1)
                    dve.wait_ge(sm["part2"], n + 1)
                    nc.vector.tensor_tensor(m3[c][:, :, 2, :], rest[c][:, 0, :, :], m3[c][:, :, 1, :], ALU.subtract)\
                        .then_inc(sm["parts"], 1)

                def divide(n, g):
                    dve.wait_ge(sm["O_T"], n * NG + g + 1)
                    o = pM[:, :].rearrange("p (q i a d) -> p q i a d", q=QT, i=2, a=2)
                    nc.vector.reciprocal(rden[:, :, :, :], o[:, :, :, :, HD4]).then_inc(sm["rden"], 1)
                    dve.wait_ge(sm["rden"], n * NG + g + 1)
                    for i in two:
                        at = HD4 * (2 * g + i)
                        last = nc.vector.tensor_tensor(
                            top.O4[:, bass.ds(n * QT, QT), :].rearrange("p q (a x) -> p q a x", a=2)
                            [:, :, :, at:at + HD4], o[:, :, i, :, 0:HD4],
                            rden[:, :, i, :].rearrange("p q (a o) -> p q a o", o=1)
                            .broadcast_to([128, QT, 2, HD4]), ALU.mult)
                    last.then_inc(sm["O_tok"], 1)

                def step(n, m, more):
                    c = par(n)
                    for pair in range(HEADS // 2):
                        if more and pair == SPLIT_AT:
                            split(n + 1, 1 - c)
                        for unit in range(3):
                            if more:
                                for ahead, k, f in fills(pair)[2 * unit:2 * unit + 2]:
                                    b, _, b_c = others(n, m, c, ahead)
                                    maxima(b, b_c, [(k, f)])
                            for b, g, _ in turns(n, pair, unit, 5):
                                divide(b, g)

                maxima(0, 0, everything)
                split(0, 0)
                maxima(1, 1, everything[:6 * LEAD])
                steps(dve, step)
                for pair, unit in LAST_TURNS:
                    for b, g, _ in turns(B, pair, unit, 5):
                        divide(b, g)

            @block.scalar
            def _(act):
                def rows(n, c):
                    act.wait_ge(sm["mT_psum"], n + 1)
                    nc.scalar.activation(mT[c][:, :], pM[0:3 * HEADS, 0:S // 2].bitcast(BF16), ACT.Copy)\
                        .then_inc(sm["mT"], 1)

                def evacuate(n, g):
                    act.wait_ge(sm["PV"], n * NG + g + 1)
                    wait(act, sm["O_T"], n * NG + g - 1)
                    nc.scalar.activation(OT[g % 2][:, :], pO[:, :], ACT.Copy).then_inc(sm["O_sb"], 1)

                def step(n, m, more):
                    c = par(n)
                    for pair in range(HEADS // 2):
                        for unit in range(3):
                            act.wait_ge(sm["ST"], n * NT + 3 * pair + unit + 1)
                            if unit == 0:
                                wait(act, sm["PV"], n * NG + pair // 2 - 1)
                            w = 512 if unit == 0 else 384
                            nc.scalar.activation(P[pair % 4][:, :, P_AT[unit]:P_AT[unit] + w],
                                                 pT[(3 * pair + unit) % 2][:, :, 0:w], ACT.Exp,
                                                 scale=float(HD4) ** -0.5).then_inc(sm["P"], 1)
                            if more and pair == SPLIT_AT and unit == 1:
                                rows(n + 1, 1 - c)
                            for b, g, _ in turns(n, pair, unit, 3):
                                evacuate(b, g)

                rows(0, 0)
                steps(act, step)
                for pair, unit in LAST_TURNS:
                    for b, g, _ in turns(B, pair, unit, 3):
                        evacuate(b, g)

            @block.tensor
            def _(pe):
                def mm(out, lhsT, rhs, start=True, stop=True):
                    return nc.tensor.matmul(out, lhsT, rhs, start=start, stop=stop)

                def first(n, m, c, some):
                    for k, f in some:
                        h, i = ORDER[k], ORDER[k] % 8
                        if k % 8 == 0 and f == 0:
                            pe.wait_ge(stacks[c][k // 8], 64 * m + 64)
                        wait(pe, sm["S_max"], n * NS + 3 * k + f - 1)
                        dst = pS[(3 * k + f) % 2]
                        for q, at in ((3, 0),) if f == 0 else ((2, 0),) if f == 1 else ((1, 0), (0, 256)):
                            w = 128 * q + 128
                            mm(dst[:, at:at + w], Qs[c][0:ALL_ROWS, i, 128 * q:128 * q + 128],
                               Ks[c][0:ALL_ROWS, h // 4, 0:w], True, False)
                            last = mm(dst[:, at + w - 128:at + w], top.ident_bf[:, :], top.mask_bf[:, :],
                                      False, True)
                        last.then_inc(sm["S"], 1)

                def second(n, m, c, pair, unit):
                    if pair == 0 and unit == 0:
                        pe.wait_ge(sm["max_ones"], 4)
                        pe.wait_ge(rows_in[c], 32 * m + 32)
                    wait(pe, sm["P"], n * NT + 3 * pair + unit - 1)
                    dst = pT[(3 * pair + unit) % 2]
                    for j in two:
                        for kt, at in ((0, 0),) if unit == 0 else ((1, 0),) if unit == 1 else ((2, 0), (3, 256)):
                            w = S - 128 * kt
                            last = mm(dst[:, j, at:at + w], Ks[c][0:WITH_MAX, 2 * j + pair // 4,
                                                                  128 * kt:128 * kt + 128],
                                      Qs[c][0:WITH_MAX, pair, 128 * kt:S])
                    last.then_inc(sm["ST"], 1)

                def values(n, m, c, g, kt):
                    if kt == 0:
                        if g == 0:
                            pe.wait_ge(v_in[c], 16 * m + 16)
                        pe.wait_ge(sm["masked"], n * NT + 6 * g + 6)
                        wait(pe, sm["O_sb"], n * NG + g)
                    w = S - 128 * kt
                    for j in range(4):
                        last = mm(pO[32 * j:32 * j + 32, 128 * kt:S], V[c][:, kt, 2 * (j % 2) + g // 2, :],
                                  P[(2 * g + j // 2) % 4][:, j % 2, P_AT[kt]:P_AT[kt] + w], kt == 0, kt == QT - 1)
                    if kt == QT - 1:
                        last.then_inc(sm["PV"], 1)

                def outputs(n, m, c, pair, unit, more):
                    for kt in range(QT):
                        for b, g, back in turns(n, pair, unit, kt):
                            values(b, m + c - 1 if back else m, 1 - c if back else c, g, kt)
                    for b, g, _ in turns(n, pair, unit, 5):
                        by_token(b, g, more)

                def by_token(n, g, more=False):
                    pe.wait_ge(sm["O_sb"], n * NG + g + 1)
                    wait(pe, sm["O_tok"], n * NG + g)
                    if more and g == 1:
                        pe.wait_ge(sm["mT"], n + 2)
                    for q in range(QT):
                        last = nc.tensor.transpose(pM[:, 128 * q:128 * q + 128],
                                                   OT[g % 2][:, 128 * q:128 * q + 128], top.ident[:, :])
                    last.then_inc(sm["O_T"], 1)

                def rows(n, c):
                    if not (isinstance(n, int) and n == 0):
                        wait_alone(pe, sm["O_tok"], (n - 1) * NG + 1)
                    wait_alone(pe, sm["parts"], n + 1)
                    for q in range(QT):
                        last = nc.tensor.transpose(pM[0:3 * HEADS, 64 * q:64 * q + 64].bitcast(BF16),
                                                   m3[c][:, q, :, :].rearrange("p k h -> p (k h)"), top.ident_bf[:, :])
                    last.then_inc(sm["mT_psum"], 1)

                def step(n, m, more):
                    c = par(n)
                    for pair in range(HEADS // 2):
                        for unit in range(3):
                            second(n, m, c, pair, unit)
                            if more:
                                for ahead, k, f in fills(pair)[2 * unit:2 * unit + 2]:
                                    first(*others(n, m, c, ahead), [(k, f)])
                                if pair == SPLIT_AT and unit == 1:
                                    rows(n + 1, 1 - c)
                            outputs(n, m, c, pair, unit, more)

                first(0, 0, 0, everything)
                rows(0, 0)
                first(1, 0, 1, everything[:6 * LEAD])
                steps(pe, step)
                for pair, unit in LAST_TURNS:
                    outputs(B, B // 2, 0, pair, unit, False)
        ph.close()


def experts_phase(nc, top, dram, out):
    with ExitStack() as ctx:
        ph = Phase(nc, ctx, "e_")
        sm = ph.sems("oT_psum oT proj h sq rms rrms hT_psum hT logits best index diff ediff wden w1 w2 picks pick1 "
                     "comb0 comb0b comb scale exp_psum scaled_d scaled_a summed total stats mv std rstd norm y out")
        two = range(2)
        o_in = [ph.sem(f"o_in{c}") for c in two]
        stored = [ph.sem(f"stored{c}") for c in two]
        o = [ph.sb(f"o{c}", [128, CT, D]) for c in two]
        oT = [ph.sb(f"oT{c}", [128, 2, S]) for c in two]
        h = [ph.sb(f"h{c}", [128, CT, D]) for c in two]
        hT = oT
        sq = [ph.sb(f"sq{c}", [128, CT]) for c in two]
        rms = [ph.sb(f"rms{c}", [128, CT]) for c in two]
        rr = [ph.sb(f"rr{c}", [128, CT]) for c in two]
        best = [ph.sb(f"best{c}", [128, CT, 8]) for c in two]
        logit = [ph.sb(f"logit{c}", [128, CT, NE]) for c in two]
        index = [ph.sb(f"index{c}", [128, CT, 8], mybir.dt.uint32) for c in two]
        indexf = [ph.sb(f"indexf{c}", [128, CT, 2]) for c in two]
        w = [ph.sb(f"w{c}", [128, 4, CT]) for c in two]
        pick = [ph.sb(f"pick{c}", [128, 2, CT, NE]) for c in two]
        comb = [ph.sb(f"comb{c}", [128, CT, NE]) for c in two]
        T = [ph.sb(f"T{k}", [128, NE, D]) for k in two]
        moe = [ph.sb(f"moe{c}", [128, CT, D]) for c in two]
        st = [ph.sb(f"st{c}", [128, CT, 6]) for c in two]
        mv = [ph.sb(f"mv{c}", [128, CT, 2]) for c in two]
        rs = [ph.sb(f"rs{c}", [128, CT]) for c in two]
        nb = [ph.sb(f"nb{c}", [128, CT]) for c in two]
        PA = [ph.ps(f"PA{c}", [128, CT, D]) for c in two]
        PE_ = [ph.ps(f"PE{k}", [128, NE, D]) for k in two]
        wide = lambda a, n: a.rearrange("p (t o) -> p t o", o=1).broadcast_to([128, a.shape[1], n])
        n_iter = CHUNKS // 2

        def chunk(i, c):
            return bass.ds((2 * i + c) * CT, CT)

        with nc.Block() as block:

            @block.sync
            def _(sp):
                with sp.Fori(0, n_iter) as i:
                    for c in two:
                        sp.dma_start(o[c][:, :, :], top.O4[:, chunk(i, c), :]).then_inc(o_in[c], 16)
                    for c in two:
                        sp.wait_ge(sm["out"], 2 * i + c + 1)
                        sp.dma_start(out[:, chunk(i, c), :], moe[c][:, :, :]).then_inc(stored[c], 16)
                        wait_alone(sp, stored[c], 16 * i + 16, 16)

            @block.gpsimd
            def _(pool):
                with pool.Fori(0, n_iter) as i:
                    for c in two:
                        pool.wait_ge(sm["y"], 2 * i + c + 1)
                        nc.gpsimd.tensor_tensor(moe[c][:, :, :], h[c][:, :, :], top.X[:, chunk(i, c), :], ALU.add)\
                            .then_inc(sm["out"], 1)

            @block.vector
            def _(dve):
                with dve.Fori(0, n_iter) as i:
                    done = [2 * i + 1, 2 * i + 2]
                    for c in two:
                        dve.wait_ge(sm["oT_psum"], done[c])
                        nc.vector.tensor_copy(oT[c][:, :, :], PA[c][:, :, :].rearrange("p (b n) t -> p b (n t)", b=2))\
                            .then_inc(sm["oT"], 1)
                    for c in two:
                        dve.wait_ge(sm["proj"], done[c])
                        nc.vector.tensor_tensor(h[c][:, :, :], PA[c][:, :, :], top.N4[:, chunk(i, c), :], ALU.add)\
                            .then_inc(sm["h"], 1)
                    for c in two:
                        dve.wait_ge(sm["rms"], done[c])
                        nc.vector.reciprocal(rr[c][:, :], rms[c][:, :]).then_inc(sm["rrms"], 1)
                    for c in two:
                        dve.wait_ge(sm["hT_psum"], done[c])
                        nc.vector.tensor_copy(hT[c][:, :, :], PA[c][:, :, :].rearrange("p (b n) t -> p b (n t)", b=2))\
                            .then_inc(sm["hT"], 1)
                    for c in two:
                        dve.wait_ge(sm["rrms"], done[c])
                        dve.wait_ge(sm["logits"], done[c])
                        nc.vector.tensor_tensor(logit[c][:, :, :],
                                                PA[c][:, 0, 0:CT * NE].rearrange("p (t e) -> p t e", e=NE),
                                                wide(rr[c][:, :], NE), ALU.mult).then_inc(sm["scale"], 1)
                        wait_alone(dve, sm["scale"], done[c])
                        for t in range(CT):
                            last = nc.vector.max(best[c][:, t, :], logit[c][:, t, :])
                        last.then_inc(sm["best"], 1)
                        wait_alone(dve, sm["best"], done[c])
                        for t in range(CT):
                            last = nc.vector.max_index(index[c][:, t, :], best[c][:, t, :], logit[c][:, t, :])
                        last.then_inc(sm["index"], 1)
                        nc.vector.tensor_tensor(w[c][:, 0, :], best[c][:, :, 1], best[c][:, :, 0], ALU.subtract)\
                            .then_inc(sm["diff"], 1)
                        dve.wait_ge(sm["index"], done[c])
                        nc.vector.tensor_copy(indexf[c][:, :, :], index[c][:, :, 0:2]).then_inc(sm["picks"], 1)
                        dve.wait_ge(sm["picks"], done[c])
                        for j in two:
                            last = nc.vector.tensor_tensor(
                                pick[c][:, j, :, :], wide(indexf[c][:, :, j], NE),
                                top.iota[:, 0:NE].rearrange("p (o e) -> p o e", o=1).broadcast_to([128, CT, NE]),
                                ALU.is_equal)
                        last.then_inc(sm["pick1"], 1)
                    for c in two:
                        dve.wait_ge(sm["ediff"], done[c])
                        nc.vector.tensor_scalar(w[c][:, 2, :], w[c][:, 1, :], 1.0, None, ALU.add)\
                            .then_inc(sm["wden"], 1)
                        dve.wait_ge(sm["wden"], done[c])
                        nc.vector.reciprocal(w[c][:, 3, :], w[c][:, 2, :]).then_inc(sm["w1"], 1)
                        dve.wait_ge(sm["w1"], done[c])
                        nc.vector.tensor_tensor(w[c][:, 2, :], w[c][:, 3, :], rr[c][:, :], ALU.mult)\
                            .then_inc(sm["w2"], 1)
                        dve.wait_ge(sm["w2"], done[c])
                        nc.vector.tensor_tensor(w[c][:, 3, :], w[c][:, 2, :], w[c][:, 1, :], ALU.mult)
                        dve.wait_ge(sm["pick1"], done[c])
                        nc.vector.tensor_tensor(pick[c][:, 0, :, :], pick[c][:, 0, :, :], wide(w[c][:, 2, :], NE),
                                                ALU.mult).then_inc(sm["comb0"], 1)
                        dve.wait_ge(sm["comb0"], done[c])
                        nc.vector.tensor_tensor(pick[c][:, 1, :, :], pick[c][:, 1, :, :], wide(w[c][:, 3, :], NE),
                                                ALU.mult).then_inc(sm["comb0b"], 1)
                        dve.wait_ge(sm["comb0b"], done[c])
                        nc.vector.tensor_tensor(comb[c][:, :, :], pick[c][:, 0, :, :], pick[c][:, 1, :, :],
                                                ALU.add).then_inc(sm["comb"], 1)
                    for c in two:
                        dve.wait_ge(sm["comb"], done[c])
                        for t in range(CT):
                            u = (2 * i + c) * CT + t
                            k = t % 2
                            if k == 0:
                                dve.wait_ge(sm["exp_psum"], u + 1)
                                if t > 1 or c:
                                    dve.wait_ge(sm["summed"], u - 1)
                                nc.vector.tensor_tensor(T[k][:, :, :], PE_[k][:, :, :], wide(comb[c][:, t, :], D),
                                                        ALU.mult).then_inc(sm["scaled_d"], 1)
                                dve.wait_ge(sm["scaled_d"], (2 * i + c) * (CT // 2) + t // 2 + 1)
                            else:
                                dve.wait_ge(sm["scaled_a"], (2 * i + c) * (CT // 2) + t // 2 + 1)
                            nc.vector.tensor_reduce(moe[c][:, t, :], T[k][:, :, :].rearrange("p e d -> p d e"),
                                                    AX.X, ALU.add).then_inc(sm["summed"], 1)
                        dve.wait_ge(sm["summed"], (2 * i + c) * CT + CT)
                        nc.vector.tensor_tensor(h[c][:, :, :], h[c][:, :, :], moe[c][:, :, :], ALU.add)\
                            .then_inc(sm["total"], 1)
                        dve.wait_ge(sm["total"], done[c])
                        for t in range(CT):
                            last = nc.vector.bn_stats(st[c][:, t, :], h[c][:, t, :])
                        last.then_inc(sm["stats"], 1)
                        wait_alone(dve, sm["stats"], done[c])
                        for t in range(CT):
                            last = nc.vector.bn_aggr(mv[c][:, t, :], st[c][:, t, :])
                        last.then_inc(sm["mv"], 1)
                    for c in two:
                        dve.wait_ge(sm["std"], done[c])
                        nc.vector.reciprocal(rs[c][:, :], rms[c][:, :]).then_inc(sm["rstd"], 1)
                        dve.wait_ge(sm["rstd"], done[c])
                        for t in range(CT):
                            last = nc.vector.tensor_scalar(h[c][:, t, :], h[c][:, t, :], mv[c][:, t, 0:1],
                                                           rs[c][:, t:t + 1], ALU.subtract, ALU.mult)
                        last.then_inc(sm["y"], 1)

            @block.scalar
            def _(act):
                with act.Fori(0, n_iter) as i:
                    done = [2 * i + 1, 2 * i + 2]
                    for c in two:
                        act.wait_ge(sm["h"], done[c])
                        for t in range(CT):
                            last = nc.scalar.activation(moe[c][:, t, :], h[c][:, t, :], ACT.Square,
                                                        accum_out=sq[c][:, t:t + 1])
                        last.then_inc(sm["sq"], 1)
                    for c in two:
                        act.wait_ge(sm["sq"], done[c])
                        nc.scalar.activation(rms[c][:, :], sq[c][:, :], ACT.Sqrt, scale=1.0 / D, bias=top.eps_rms[:, :])\
                            .then_inc(sm["rms"], 1)
                    for c in two:
                        act.wait_ge(sm["diff"], done[c])
                        nc.scalar.activation(w[c][:, 1, :], w[c][:, 0, :], ACT.Exp).then_inc(sm["ediff"], 1)
                    for c in two:
                        act.wait_ge(sm["comb"], done[c])
                        for t in range(1, CT, 2):
                            u = (2 * i + c) * CT + t
                            act.wait_ge(sm["exp_psum"], u + 1)
                            if t > 1 or c:
                                act.wait_ge(sm["summed"], u - 1)
                            for e in range(NE):
                                last = nc.scalar.activation(T[1][:, e, :], PE_[1][:, e, :], ACT.Copy,
                                                            scale=comb[c][:, t, e:e + 1])
                            last.then_inc(sm["scaled_a"], 1)
                    for c in two:
                        act.wait_ge(sm["mv"], done[c])
                        nc.scalar.activation(rms[c][:, :], mv[c][:, :, 1], ACT.Sqrt, bias=top.eps[:, :])\
                            .then_inc(sm["std"], 1)

            @block.tensor
            def _(pe):
                def mm(out_, lhsT, rhs, start=True, stop=True):
                    return nc.tensor.matmul(out_, lhsT, rhs, start=start, stop=stop)

                with pe.Fori(0, n_iter) as i:
                    done = [2 * i + 1, 2 * i + 2]
                    for c in two:
                        pe.wait_ge(o_in[c], 16 * i + 16)
                        for t in range(CT):
                            last = nc.tensor.transpose(PA[c][:, t, :], o[c][:, t, :], top.ident[:, :])
                        last.then_inc(sm["oT_psum"], 1)
                    for c in two:
                        pe.wait_ge(sm["oT"], done[c])
                        for t in range(CT):
                            lhsT = oT[c][:, t // R, :].rearrange("d (p r) -> d r p", r=R)[:, t % R, :]
                            last = mm(PA[c][:, t, :], lhsT, top.wo4T[:, :])
                        last.then_inc(sm["proj"], 1)
                    for c in two:
                        pe.wait_ge(sm["h"], done[c])
                        for t in range(CT):
                            last = nc.tensor.transpose(PA[c][:, t, :], h[c][:, t, :], top.ident[:, :])
                        last.then_inc(sm["hT_psum"], 1)
                    for c in two:
                        pe.wait_ge(sm["hT"], done[c])
                        for t in range(CT):
                            last = mm(PA[c][:, 0, NE * t:NE * t + NE],
                                      hT[c][:, t // 4, 128 * (t % 4):128 * (t % 4) + 128], top.gate_expT[:, 0:NE])
                        last.then_inc(sm["logits"], 1)
                    for c in two:
                        for t in range(CT):
                            u = (2 * i + c) * CT + t
                            k = t % 2
                            if k == 0:
                                free, count = sm["scaled_d"], (2 * i + c) * (CT // 2) + t // 2
                            else:
                                free, count = sm["scaled_a"], (2 * i + c) * (CT // 2) + t // 2
                            if t >= 2 or c:
                                pe.wait_ge(free, count)
                            for a in two:
                                last = mm(PE_[k][:, 4 * a:4 * a + 4, :],
                                          hT[c][:, t // 4, 128 * (t % 4):128 * (t % 4) + 128],
                                          top.gate_expT[:, NE + 512 * a:NE + 512 * a + 512])
                            last.then_inc(sm["exp_psum"], 1)


def sandwich(nc, dram, out):
    with ExitStack() as ctx:
        top = Phase(nc, ctx)
        top.X = top.sb("X", [128, TILES, D])
        top.N3 = top.sb("N3", [128, TILES, D])
        top.N4 = top.N3
        top.V4 = top.sb("V4", [128, TILES, KV4, VW])
        top.O4 = top.sb("O4", [128, TILES, D])
        top.ident = top.sb("ident", [128, 128])
        top.ident_bf = top.sb("ident_bf", [128, 128], BF16)
        top.eps = top.sb("eps", [128, 1])
        top.eps_rms = top.sb("eps_rms", [128, 1])
        top.hadamard = top.sb("hadamard", [128, D])
        top.ternT = top.sb("ternT", [128, 3, D], BF16)
        top.w_qmeanT = top.sb("w_qmeanT", [128, DH])
        top.ln_gb = top.sb("ln_gb", [DH, 2])
        top.w1T = top.sb("w1T", [DH, PROJ])
        top.b1 = top.sb("b1", [PROJ, 1])
        top.w2T = top.sb("w2T", [PROJ, 1])
        top.b2 = top.sb("b2", [1, 1])
        top.w_qkvT = top.sb("w_qkvT", [128, 3 * HEADS * DH])
        top.w_outT = top.sb("w_outT", [128, HEADS // 2, D])
        top.b_out = top.sb("b_out", [B, D])
        top.iota = top.sb("iota", [128, TOP_K + 1])
        top.iota_col = top.sb("iota_col", [128, 1])
        top.batch_rows = top.sb("batch_rows", [B, 2, 128])
        top.batch_rows_bf = top.sb("batch_rows_bf", [B, 2, 128], BF16)
        top.first_row = top.sb("first_row", [128, 128])
        top.lower_f = top.sb("lower_f", [128, 128])
        top.lower = top.sb("lower", [128, 128], BF16)
        top.ones_bf = top.sb("ones_bf", [128, 128], BF16)
        top.selT = [top.sb(f"selT{Q}", [128, S]) for Q in range(2)]
        top.Y = [top.sb(f"Y{Q}", [128, D]) for Q in range(2)]
        top.yU = [top.sb(f"yU{Q}", [128, D]) for Q in range(2)]
        top.qkv4T = top.sb("qkv4T", [128, D + 2 * KVD])
        top.wq4T, top.wk4T, top.wv4T = (top.qkv4T[:, 0:D], top.qkv4T[:, D:D + KVD], top.qkv4T[:, D + KVD:D + 2 * KVD])
        top.wo4T = top.sb("wo4T", [128, D])
        top.gate_expT = top.sb("gate_expT", [128, NE + NE * D])
        top.norm_w = top.sb("norm_w", [128, 2])
        top.mask_f = top.sb("mask_f", [128, 128])
        top.mask_bf = top.sb("mask_bf", [128, 128], BF16)
        dilated_and_ternary_phase(nc, top, dram)
        gated_attention_phase(nc, top, dram)
        projection_phase(nc, top, dram)
        causal_attention_phase(nc, top, dram)
        experts_phase(nc, top, dram, out)


def kernel(**inputs):
    import numpy as np
    import concourse.bacc as bacc
    from concourse.bass_utils import run_bass_kernel_spmd

    def hadamard(size):
        h = np.array([[1.0]], dtype=np.float64)
        while h.shape[0] < size:
            h = np.block([[h, h], [h, -h]])
        return (h / np.sqrt(size)).astype(np.float32)

    a = {k: np.asarray(v) for k, v in inputs.items()}
    by_channel = lambda w: w.reshape(-1, HD4, D).transpose(1, 0, 2).reshape(-1, D)
    col = lambda v: np.ascontiguousarray(v.reshape(-1, 1))
    arrays = {
        "x": a["L0_attn_x"].reshape(B, 128, R, D).transpose(1, 0, 2, 3).reshape(128, TILES, D),
        "ffn_weight": a["L0_ffn_weight"],
        "w_qkvT": a["L1_attn_w_qkv"].T,
        "ln_gb": np.stack([a["L1_attn_ln_g"], a["L1_attn_ln_b"]], axis=1),
        "w1T": a["L1_attn_w1"].T,
        "b1": col(a["L1_attn_b1"]),
        "w2T": a["L1_attn_w2"].T,
        "b2": col(a["L1_attn_b2"]),
        "ident": np.eye(128, dtype=np.float32),
        "hadamard": hadamard(D),
        "w_outT": a["L1_attn_w_out"].T.reshape(HEADS // 2, 128, D).transpose(1, 0, 2),
        "b_out": np.broadcast_to(a["L1_attn_b_out"], (B, D)),
        "qkv4T": np.concatenate([by_channel(a["L1_ffn_wq"]), by_channel(a["L1_ffn_wk"]), a["L1_ffn_wv"]]).T,
        "wo4T": a["L1_ffn_wo"].T,
        "gate_expT": np.concatenate([a["L1_ffn_gate_w"], a["L1_ffn_expert_w"].reshape(NE * D, D)]).T,
        "norm_w": np.stack([a["L1_ffn_attn_norm_w"], a["L1_ffn_ffn_norm_w"]], axis=1),
        "iota": np.tile(np.arange(TOP_K + 1, dtype=np.float32), (128, 1)),
        "iota_col": (np.arange(128) % TOP_K).astype(np.float32).reshape(128, 1),
        "batch_rows": (np.arange(B)[:, None] == np.arange(2 * 128)[None] // TOP_K).astype(np.float32).reshape(B, 2, 128),
        "first_row": np.repeat((np.arange(128) % TOP_K == 0).astype(np.float32)[:, None], 128, axis=1),
        "lower": np.triu(np.ones((128, 128), np.float32), 1),
        "mask": np.triu(np.full((128, 128), -1e30, np.float32), 1),
    }
    nc = bacc.Bacc("TRN2", target_bir_lowering=False, num_devices=1)
    dram, send = {}, {}
    for name, v in arrays.items():
        send[f"in_{name}_dram"] = np.ascontiguousarray(v)
        dram[name] = nc.dram_tensor(f"in_{name}_dram", v.shape, mybir.dt.from_np(v.dtype), kind="ExternalInput").ap()
    dram["scores"] = nc.dram_tensor("scores", (1, B * S), FP32, kind="Internal").ap()
    q_stack = nc.dram_tensor("q_stack", (B + 1, SLOTS, HD4, HEADS, S), BF16, kind="Internal").ap()
    k_stack = nc.dram_tensor("k_stack", (B + 1, SLOTS, HD4, KV4, S), BF16, kind="Internal").ap()
    m_rows = nc.dram_tensor("m_rows", (2, 3, 2, HEADS // 2, S), BF16, kind="Internal").ap()

    def stack_load(stack):
        return lambda b, head, n: stack[bass.ds(b, 1), :, :, head:head + n, :].rearrange("o j d h t -> (o j d) h t")

    def stack_store(stack):
        return lambda b, slot, n: stack[b, slot:slot + n].rearrange("j d h t -> (d h) j t")

    dram["q_load"], dram["k_load"] = stack_load(q_stack), stack_load(k_stack)
    dram["q_store"], dram["k_store"] = stack_store(q_stack), stack_store(k_stack)
    dram["m_store"] = lambda c: m_rows[c].rearrange("k a i t -> (k a i) t")
    dram["m_load"] = lambda c, a: m_rows[c, :, a, :, :]
    out = nc.dram_tensor("out_0_dram", (128, TILES, D), FP32, kind="ExternalOutput").ap()
    sandwich(nc, dram, out)
    got = run_bass_kernel_spmd(nc, [send], core_ids=[0]).results[0]["out_0_dram"]
    return got.reshape(128, B, R, D).transpose(1, 0, 2, 3).reshape(B, S, D)
```

```python
import concourse.bass as bass
from concourse import mybir
from contextlib import ExitStack

FP32 = mybir.dt.float32
BF16 = mybir.dt.bfloat16
ALU = mybir.AluOpType
ACT = mybir.ActivationFunctionType
AX = mybir.AxisListType

B, S, D = 8, 512, 128
R = 4
SEG = 64
TILES = B * R
CT = 8
CHUNKS = TILES // CT
DH, HEADS = 64, 16
PROJ = 16
TOP_K = 32
NSEL = 2 * TOP_K + 2
LOWEST = -3e38
HD4, KV4, NE = 8, 4, 8
KVD = KV4 * HD4
VW = 32
QT = S // 128
SLOTS = 6
PAIRS = ((0, 3, 0, 0), (3, 2, 0, 1), (5, 1, 0, 2))
PAIRW = 512 + 384 + 256 + 128
LEAD = 3
RMS_EPS = 1e-6
LN_EPS = 1e-5
ROUND = 12582912.0
POS = 7.0
NEG = -8.0


def wait_alone(eng, sem, count, unit=1):
    if not isinstance(count, int):
        count = eng.to_reg(count)
        eng.wait_ge(sem, unit)
    eng.wait_ge(sem, count)


class Phase:

    def __init__(self, nc, ctx, tag=""):
        self.nc, self.ctx, self.tag, self.all_sems = nc, ctx, tag, []

    def sb(self, name, shape, dt=FP32):
        return self.ctx.enter_context(self.nc.sbuf_tensor(self.tag + name, shape, dt))

    def ps(self, name, shape, dt=FP32):
        return self.ctx.enter_context(self.nc.psum_tensor(self.tag + name, shape, dt))

    def sem(self, name):
        self.all_sems.append(self.nc.alloc_semaphore(name=self.tag + name))
        return self.all_sems[-1]

    def close(self):
        self.nc.clear_and_free_semaphores(self.all_sems)
        self.nc.all_engine_barrier()

    def sems(self, names):
        return {n: self.sem(n) for n in names.split()}


def dilated_and_ternary_phase(nc, top, dram):
    with ExitStack() as ctx:
        ph = Phase(nc, ctx, "a_")
        sm = ph.sems(
            "s1_std s1_ostd s1_orstd s2_std s2_ostd s3_std s3_qstd s1_stats s1_mv s1_rstd s1_norm s1_n s1_nT_psum s1_nT s1_scores s1_E s1_sum s1_O s1_ostats s1_omv "
            "s1_sq s1_var s1_onorm s1_y s1_x "
            "s2_stats s2_mv s2_rstd s2_norm s2_n s2_nT_psum s2_nT s2_xh s2_absmax s2_scale s2_rscale s2_ratio s2_q "
            "s2_qT_psum s2_qT s2_O s2_ostats s2_omv s2_sq s2_var s2_ors s2_ors2 s2_onorm s2_y s2_x s2_rounded "
            "s3_stats s3_mv s3_rstd s3_norm s3_n s3_nT_psum s3_nT s3_qm s3_qstats s3_qmv s3_qrstd s3_qnorm s3_z "
            "s3_zT_psum s3_H s3_pre s3_hidden s3_score_psum s3_score")
        sm |= ph.sems("loaded_first loaded zeroed ident_bf tern_abs tern_scale tern_steps tern_low tern_full "
                      "part1 rest1 part2 parts parts_psum parts_out mean_w mean_w_out eps")
        chunks = range(CHUNKS)
        flat = lambda a: a.rearrange("p t d -> p (t d)")
        x_in = [ph.sem(f"x_in{c}") for c in chunks]
        score_kept = ph.sem("score_kept")
        X = [top.X[:, CT * c:CT * c + CT, :] for c in chunks]
        n = [top.N3[:, CT * c:CT * c + CT, :] for c in chunks]
        nT = [ph.sb(f"nT{c}", [128, CT, D]) for c in chunks]
        y = nT
        u = [flat(nT[c][0:PROJ, :, :]) for c in chunks]
        expS = [ph.sb(f"expS{c}", [128, CT, D]) for c in chunks]
        ratio = expS
        HT = [flat(expS[c][0:DH, :, :]) for c in chunks]
        score = [flat(expS[c][0:1, :, :]).rearrange("a (b p r) -> a b p r", b=2, r=R) for c in chunks]
        q = [ph.sb(f"q{c}", [128, CT, D], BF16) for c in chunks]
        qT = [ph.sb(f"qT{c}", [128, CT, D], BF16) for c in chunks]
        z = [ph.sb(f"z{c}", [128, CT, DH]) for c in chunks]
        small = lambda name, *shape: [ph.sb(f"{name}{c}", [128, CT, *shape]) for c in chunks]
        st, mv = small("st", 6), small("mv", 2)
        rs, nb, den, std, tmp, sc = (small(name) for name in ("rs", "nb", "den", "std", "tmp", "sc"))
        w = ph.sb("w", [128, D])
        pos = ph.sb("pos", [128, D])
        low = ph.sb("low", [128, D])
        rest = ph.sb("rest", [128, D])
        part = ph.sb("part", [128, 3, D], BF16)
        absum = ph.sb("absum", [128, 1])
        scale = ph.sb("scale", [128, 1])
        lim = ph.sb("lim", [128, 2])
        PS = [ph.ps(f"PS{c}", [128, CT, D]) for c in chunks]
        partsT = PS[-1][:, 0:2, :].bitcast(BF16).rearrange("p a (b d) -> p (a b) d", b=2)[:, 0:3, :]
        done = [c + 1 for c in chunks]
        staggered = list(zip([None, *chunks], [*chunks, None]))
        FIRST = (("ident", top.ident), ("ffn_weight", w), ("hadamard", top.hadamard))
        OTHERS = (("w_qkvT", top.w_qkvT), ("ln_gb", top.ln_gb), ("w1T", top.w1T), ("b1", top.b1), ("w2T", top.w2T),
                  ("b2", top.b2), ("w_outT", top.w_outT), ("qkv4T", top.qkv4T), ("wo4T", top.wo4T),
                  ("gate_expT", top.gate_expT), ("norm_w", top.norm_w), ("b_out", top.b_out), ("iota", top.iota),
                  ("iota_col", top.iota_col), ("batch_rows", top.batch_rows), ("first_row", top.first_row),
                  ("lower", top.lower_f), ("mask", top.mask_f))

        with nc.Block() as block:

            @block.sync
            def _(sp):
                for loads, sem in ((FIRST, "loaded_first"), (OTHERS, "loaded")):
                    for name, dst in loads:
                        sp.dma_start(dst[:], dram[name]).then_inc(sm[sem], 16)
                for c in chunks:
                    sp.wait_ge(sm["s3_score"], done[c])
                    sp.dma_start(dram["scores"][:, 2 * S * c:2 * S * c + 2 * S],
                                 score[c][:, :, :, :].rearrange("a b p r -> a (b p r)")).then_inc(score_kept, 16)
                sp.wait_ge(score_kept, 16 * CHUNKS)

            @block.vector
            def _(dve):
                def stats(src, c, k, s, width=D):
                    for t in range(CT):
                        last = nc.vector.bn_stats(st[c][:, t, :], src(t))
                    last.then_inc(sm[s + "stats"], 1)
                    dve.wait_ge(sm[s + "stats"], k)
                    for t in range(CT):
                        last = nc.vector.bn_aggr(mv[c][:, t, :], st[c][:, t, :])
                    last.then_inc(sm[s + "mv"], 1)
                    dve.wait_ge(sm[s + "mv"], k)

                def norm_scalars(c, k, s):
                    dve.wait_ge(sm[s + "std"], k)
                    nc.vector.reciprocal(rs[c][:, :], std[c][:, :]).then_inc(sm[s + "rstd"], 1)
                    dve.wait_ge(sm[s + "rstd"], k)
                    nc.vector.scalar_tensor_tensor(out=nb[c][:, :], in0=mv[c][:, :, 0], scalar=-1.0,
                                                   in1=rs[c][:, :], op0=ALU.mult, op1=ALU.mult)\
                        .then_inc(sm[s + "norm"], 1)

                def ternary_weights():
                    dve.wait_ge(sm["loaded_first"], 16 * len(FIRST))
                    nc.vector.tensor_copy(top.ident_bf[:, :], top.ident[:, :]).then_inc(sm["ident_bf"], 1)
                    nc.vector.tensor_reduce(absum[:, :], w[:, :], AX.X, ALU.add, apply_absolute_value=True)\
                        .then_inc(sm["tern_abs"], 1)
                    dve.wait_ge(sm["tern_abs"], 1)
                    nc.vector.tensor_scalar(scale[:, :], absum[:, :], 1.0 / D, LN_EPS, ALU.mult, ALU.max)\
                        .then_inc(sm["tern_scale"], 1)
                    dve.wait_ge(sm["tern_scale"], 1)
                    nc.vector.tensor_scalar(lim[:, 0:1], scale[:, :], 0.5, None, ALU.mult)
                    nc.vector.tensor_scalar(lim[:, 1:2], scale[:, :], -0.5, None, ALU.mult)\
                        .then_inc(sm["tern_steps"], 1)
                    dve.wait_ge(sm["tern_steps"], 1)
                    nc.vector.tensor_scalar(pos[:, :], w[:, :], lim[:, 0:1], scale[:, :], ALU.is_gt, ALU.mult)
                    nc.vector.tensor_scalar(low[:, :], w[:, :], lim[:, 1:2], scale[:, :], ALU.is_lt, ALU.mult)\
                        .then_inc(sm["tern_low"], 1)
                    dve.wait_ge(sm["tern_low"], 1)
                    nc.vector.tensor_tensor(w[:, :], pos[:, :], low[:, :], ALU.subtract).then_inc(sm["tern_full"], 1)
                    dve.wait_ge(sm["tern_full"], 1)
                    nc.vector.tensor_copy(part[:, 0, :], w[:, :]).then_inc(sm["part1"], 1)
                    dve.wait_ge(sm["part1"], 1)
                    nc.vector.tensor_tensor(rest[:, :], w[:, :], part[:, 0, :], ALU.subtract).then_inc(sm["rest1"], 1)
                    dve.wait_ge(sm["rest1"], 1)
                    nc.vector.tensor_copy(part[:, 1, :], rest[:, :]).then_inc(sm["part2"], 1)
                    dve.wait_ge(sm["part2"], 1)
                    nc.vector.tensor_tensor(part[:, 2, :], rest[:, :], part[:, 1, :], ALU.subtract)\
                        .then_inc(sm["parts"], 1)

                def other_weights():
                    dve.wait_ge(sm["loaded"], 16 * len(OTHERS))
                    nc.vector.tensor_reduce(
                        top.w_qmeanT[:, :], top.w_qkvT[:, 0:HEADS * DH].rearrange("p (h d) -> p d h", h=HEADS),
                        AX.X, ALU.add).then_inc(sm["mean_w"], 1)
                    nc.vector.tensor_copy(top.lower[:, :], top.lower_f[:, :])
                    nc.vector.tensor_copy(top.mask_bf[:, :], top.mask_f[:, :])
                    nc.vector.tensor_copy(top.batch_rows_bf[:, :, :], top.batch_rows[:, :, :])
                    nc.vector.tensor_scalar(top.qkv4T[:, :], top.qkv4T[:, :], top.norm_w[:, 0:1], None, ALU.mult)
                    nc.vector.tensor_scalar(top.gate_expT[:, :], top.gate_expT[:, :], top.norm_w[:, 1:2], None,
                                            ALU.mult)
                    dve.wait_ge(sm["mean_w"], 1)
                    nc.vector.tensor_scalar(top.w_qmeanT[:, :], top.w_qmeanT[:, :], 1.0 / HEADS, None, ALU.mult)\
                        .then_inc(sm["mean_w_out"], 1)

                ternary_weights()
                for last_c, c in staggered:
                    if c is not None:
                        dve.wait_ge(x_in[c], 16)
                        stats(lambda t: X[c][:, t, :], c, done[c], "s1_")
                    if last_c is not None:
                        norm_scalars(last_c, done[last_c], "s1_")
                dve.wait_ge(sm["parts_psum"], 1)
                nc.vector.tensor_copy(top.ternT[:, :, :], partsT).then_inc(sm["parts_out"], 1)
                for c in chunks:
                    dve.wait_ge(sm["s1_nT_psum"], done[c])
                    nc.vector.tensor_copy(nT[c][:, :, :], PS[c][:, :, :]).then_inc(sm["s1_nT"], 1)
                for c in chunks:
                    dve.wait_ge(sm["s1_E"], done[c])
                    for a in range(2):
                        last = nc.vector.tensor_reduce(
                            den[c][SEG * a:SEG * a + SEG, :],
                            expS[c][SEG * a:SEG * a + SEG, :, SEG * a:SEG * a + SEG], AX.X, ALU.add)
                    last.then_inc(sm["s1_sum"], 1)
                    dve.wait_ge(sm["s1_sum"], done[c])
                    nc.vector.scalar_tensor_tensor(out=tmp[c][:, :], in0=den[c][:, :], scalar=float(R * R),
                                                   in1=den[c][:, :], op0=ALU.mult, op1=ALU.mult)\
                        .then_inc(sm["s1_sq"], 1)
                for last_c, c in staggered:
                    if c is not None:
                        dve.wait_ge(sm["s1_O"], done[c])
                        stats(lambda t: PS[c][:, t, :], c, done[c], "s1_o")
                        dve.wait_ge(sm["s1_sq"], done[c])
                        nc.vector.scalar_tensor_tensor(out=tmp[c][:, :], in0=tmp[c][:, :], scalar=LN_EPS,
                                                       in1=mv[c][:, :, 1], op0=ALU.mult, op1=ALU.add)\
                            .then_inc(sm["s1_var"], 1)
                    if last_c is not None:
                        norm_scalars(last_c, done[last_c], "s1_o")
                for last_c, c in staggered:
                    if c is not None:
                        dve.wait_ge(sm["s1_x"], done[c])
                        stats(lambda t: X[c][:, t, :], c, done[c], "s2_")
                    if last_c is not None:
                        norm_scalars(last_c, done[last_c], "s2_")
                for c in chunks:
                    dve.wait_ge(sm["s2_nT_psum"], done[c])
                    nc.vector.tensor_copy(nT[c][:, :, :], PS[c][:, :, :]).then_inc(sm["s2_nT"], 1)
                for c in chunks:
                    dve.wait_ge(sm["s2_xh"], done[c])
                    nc.vector.tensor_reduce(den[c][:, :], PS[c][:, :, :], AX.X, ALU.max,
                                            apply_absolute_value=True).then_inc(sm["s2_absmax"], 1)
                    dve.wait_ge(sm["s2_absmax"], done[c])
                    nc.vector.tensor_scalar(sc[c][:, :], den[c][:, :], LN_EPS, 1.0 / POS, ALU.max, ALU.mult)\
                        .then_inc(sm["s2_scale"], 1)
                    dve.wait_ge(sm["s2_scale"], done[c])
                    nc.vector.reciprocal(den[c][:, :], sc[c][:, :]).then_inc(sm["s2_rscale"], 1)
                    dve.wait_ge(sm["s2_rscale"], done[c])
                    nc.vector.tensor_tensor(ratio[c][:, :, :], PS[c][:, :, :],
                                            den[c][:, :].rearrange("p (t o) -> p t o", o=1).broadcast_to([128, CT, D]),
                                            ALU.mult).then_inc(sm["s2_ratio"], 1)
                    dve.wait_ge(sm["s2_ratio"], done[c])
                    nc.vector.tensor_scalar(q[c][:, :, :], ratio[c][:, :, :], ROUND, ROUND,
                                            ALU.add, ALU.subtract).then_inc(sm["s2_q"], 1)
                for c in chunks:
                    dve.wait_ge(sm["s2_qT_psum"], done[c])
                    nc.vector.tensor_scalar(qT[c][:, :, :], PS[c][:, 0:CT // 2, :].bitcast(BF16), POS, NEG,
                                            ALU.min, ALU.max).then_inc(sm["s2_qT"], 1)
                    nc.vector.tensor_tensor(tmp[c][:, :], sc[c][:, :], sc[c][:, :], ALU.mult)\
                        .then_inc(sm["s2_sq"], 1)
                for last_c, c in staggered:
                    if c is not None:
                        dve.wait_ge(sm["s2_O"], done[c])
                        stats(lambda t: PS[c][:, t, :], c, done[c], "s2_o")
                        dve.wait_ge(sm["s2_sq"], done[c])
                        nc.vector.tensor_tensor(tmp[c][:, :], tmp[c][:, :], mv[c][:, :, 1], ALU.mult)\
                            .then_inc(sm["s2_var"], 1)
                    if last_c is not None:
                        dve.wait_ge(sm["s2_ostd"], done[last_c])
                        nc.vector.reciprocal(tmp[last_c][:, :], std[last_c][:, :]).then_inc(sm["s2_ors"], 1)
                        dve.wait_ge(sm["s2_ors"], done[last_c])
                        nc.vector.tensor_tensor(rs[last_c][:, :], tmp[last_c][:, :], sc[last_c][:, :], ALU.mult)\
                            .then_inc(sm["s2_ors2"], 1)
                        dve.wait_ge(sm["s2_ors2"], done[last_c])
                        nc.vector.scalar_tensor_tensor(out=nb[last_c][:, :], in0=mv[last_c][:, :, 0], scalar=-1.0,
                                                       in1=rs[last_c][:, :], op0=ALU.mult, op1=ALU.mult)\
                            .then_inc(sm["s2_onorm"], 1)
                other_weights()
                for last_c, c in staggered:
                    if c is not None:
                        dve.wait_ge(sm["s2_x"], done[c])
                        stats(lambda t: X[c][:, t, :], c, done[c], "s3_")
                    if last_c is not None:
                        norm_scalars(last_c, done[last_c], "s3_")
                for c in chunks:
                    dve.wait_ge(sm["s3_nT_psum"], done[c])
                    nc.vector.tensor_copy(nT[c][:, :, :], PS[c][:, :, :]).then_inc(sm["s3_nT"], 1)
                for last_c, c in staggered:
                    if c is not None:
                        dve.wait_ge(sm["s3_qm"], done[c])
                        stats(lambda t: PS[c][:, t, 0:DH], c, done[c], "s3_q")
                    if last_c is not None:
                        norm_scalars(last_c, done[last_c], "s3_q")

            @block.scalar
            def _(act):
                def normalise(dst, src, c, k):
                    for t in range(CT):
                        last = nc.scalar.activation(dst(t), src(t), ACT.Identity, bias=nb[c][:, t:t + 1],
                                                    scale=rs[c][:, t:t + 1])
                    return last

                def deviation(s, src, c, ready, eps=True):
                    act.wait_ge(sm[ready], done[c])
                    nc.scalar.activation(std[c][:, :], src(c), ACT.Sqrt,
                                         bias=top.eps[:, :] if eps else 0.0).then_inc(sm[s + "std"], 1)

                for c in chunks:
                    act.dma_start(X[c][:, :, :], dram["x"][:, CT * c:CT * c + CT, :]).then_inc(x_in[c], 16)
                act.wait_ge(sm["eps"], 1)
                variance = lambda c: mv[c][:, :, 1]
                for last_c, c in staggered:
                    if c is not None:
                        deviation("s1_", variance, c, "s1_mv")
                    if last_c is not None:
                        act.wait_ge(sm["s1_norm"], done[last_c])
                        normalise(lambda t: n[last_c][:, t, :], lambda t: X[last_c][:, t, :], last_c, done[last_c])\
                            .then_inc(sm["s1_n"], 1)
                for c in chunks:
                    act.wait_ge(sm["zeroed"], done[c])
                    act.wait_ge(sm["s1_scores"], done[c])
                    for a in range(2):
                        seg = slice(SEG * a, SEG * a + SEG)
                        last = nc.scalar.activation(expS[c][seg, :, seg], PS[c][seg, :, seg], ACT.Exp,
                                                    scale=float(D) ** -0.5)
                    last.then_inc(sm["s1_E"], 1)
                for last_c, c in staggered:
                    if c is not None:
                        deviation("s1_o", lambda c: tmp[c][:, :], c, "s1_var", eps=False)
                    if last_c is not None:
                        act.wait_ge(sm["s1_onorm"], done[last_c])
                        normalise(lambda t: y[last_c][:, t, :], lambda t: PS[last_c][:, t, :], last_c, done[last_c])\
                            .then_inc(sm["s1_y"], 1)
                for last_c, c in staggered:
                    if c is not None:
                        deviation("s2_", variance, c, "s2_mv")
                    if last_c is not None:
                        act.wait_ge(sm["s2_norm"], done[last_c])
                        normalise(lambda t: n[last_c][:, t, :], lambda t: X[last_c][:, t, :], last_c, done[last_c])\
                            .then_inc(sm["s2_n"], 1)
                for last_c, c in staggered:
                    if c is not None:
                        deviation("s2_o", lambda c: tmp[c][:, :], c, "s2_var")
                    if last_c is not None:
                        act.wait_ge(sm["s2_onorm"], done[last_c])
                        normalise(lambda t: y[last_c][:, t, :], lambda t: PS[last_c][:, t, :], last_c, done[last_c])\
                            .then_inc(sm["s2_y"], 1)
                for last_c, c in staggered:
                    if c is not None:
                        deviation("s3_", variance, c, "s3_mv")
                    if last_c is not None:
                        act.wait_ge(sm["s3_norm"], done[last_c])
                        normalise(lambda t: n[last_c][:, t, :], lambda t: X[last_c][:, t, :], last_c, done[last_c])\
                            .then_inc(sm["s3_n"], 1)
                for last_c, c in staggered:
                    if c is not None:
                        deviation("s3_q", variance, c, "s3_qmv")
                    if last_c is not None:
                        act.wait_ge(sm["s3_qnorm"], done[last_c])
                        normalise(lambda t: z[last_c][:, t, :], lambda t: PS[last_c][:, t, 0:DH], last_c, done[last_c])\
                            .then_inc(sm["s3_z"], 1)
                for c in chunks:
                    if c == 0:
                        act.wait_ge(sm["loaded"], 16 * len(OTHERS))
                    act.wait_ge(sm["s3_zT_psum"], done[c])
                    nc.scalar.activation(HT[c][:, :], PS[c][0:DH, :, :].rearrange("p t d -> p (t d)"),
                                         ACT.Identity, bias=top.ln_gb[:, 1:2], scale=top.ln_gb[:, 0:1])\
                        .then_inc(sm["s3_H"], 1)
                for c in chunks:
                    act.wait_ge(sm["s3_pre"], done[c])
                    nc.scalar.activation(u[c][:, :], PS[c][0:PROJ, :, :].rearrange("p t d -> p (t d)"), ACT.Gelu,
                                         bias=top.b1[:, :]).then_inc(sm["s3_hidden"], 1)
                for c in chunks:
                    act.wait_ge(sm["s3_score_psum"], done[c])
                    nc.scalar.activation(score[c][:, :, :, :],
                                         PS[c][0:1, :, :].rearrange("a (b r) p -> a b p r", b=2),
                                         ACT.Identity, bias=top.b2[:, :]).then_inc(sm["s3_score"], 1)

            @block.gpsimd
            def _(pool):
                nc.gpsimd.memset(top.eps_rms[:, :], RMS_EPS)
                nc.gpsimd.memset(top.eps[:, :], LN_EPS).then_inc(sm["eps"], 1)
                nc.gpsimd.memset(top.ones_bf[:, :], 1.0)
                for c in chunks:
                    nc.gpsimd.memset(expS[c][:, :, :], 0.0).then_inc(sm["zeroed"], 1)
                for s in ("s1", "s2"):
                    for c in chunks:
                        pool.wait_ge(sm[s + "_y"], done[c])
                        nc.gpsimd.tensor_tensor(X[c][:, :, :], X[c][:, :, :], y[c][:, :, :], ALU.add).then_inc(sm[s + "_x"], 1)

            @block.tensor
            def _(pe):
                def transposes(dst, src, ident, n=CT):
                    for t in range(n):
                        last = nc.tensor.transpose(dst(t), src(t), ident)
                    return last

                def mm(out, lhsT, rhs, start=True, stop=True):
                    return nc.tensor.matmul(out, lhsT, rhs, start=start, stop=stop)

                pe.wait_ge(sm["parts"], 1)
                transposes(lambda t: partsT[:, t, :], lambda t: part[:, t, :], top.ident_bf[:, :], 3)\
                    .then_inc(sm["parts_psum"], 1)
                pe.wait_ge(sm["parts_out"], 1)
                for c in chunks:
                    pe.wait_ge(sm["s1_n"], done[c])
                    transposes(lambda t: PS[c][:, t, :], lambda t: n[c][:, t, :], top.ident[:, :])\
                        .then_inc(sm["s1_nT_psum"], 1)
                for c in chunks:
                    pe.wait_ge(sm["s1_nT"], done[c])
                    for t in range(CT):
                        last = mm(PS[c][:, t, :], nT[c][:, t, :], nT[c][:, t, :])
                    last.then_inc(sm["s1_scores"], 1)
                for c in chunks:
                    pe.wait_ge(sm["s1_E"], done[c])
                    for t in range(CT):
                        last = mm(PS[c][:, t, :], expS[c][:, t, :], n[c][:, t, :])
                    last.then_inc(sm["s1_O"], 1)
                for c in chunks:
                    pe.wait_ge(sm["s2_n"], done[c])
                    transposes(lambda t: PS[c][:, t, :], lambda t: n[c][:, t, :], top.ident[:, :])\
                        .then_inc(sm["s2_nT_psum"], 1)
                for c in chunks:
                    pe.wait_ge(sm["s2_nT"], done[c])
                    for t in range(CT):
                        last = mm(PS[c][:, t, :], nT[c][:, t, :], top.hadamard[:, :])
                    last.then_inc(sm["s2_xh"], 1)
                for c in chunks:
                    pe.wait_ge(sm["s2_q"], done[c])
                    PAb = PS[c][:, 0:CT // 2, :].bitcast(BF16).rearrange("p a (b d) -> p (a b) d", b=2)
                    transposes(lambda t: PAb[:, t, :], lambda t: q[c][:, t, :], top.ident_bf[:, :])\
                        .then_inc(sm["s2_qT_psum"], 1)
                for c in chunks:
                    pe.wait_ge(sm["s2_qT"], done[c])
                    for t in range(CT):
                        for j in range(3):
                            last = mm(PS[c][:, t, :], qT[c][:, t, :], top.ternT[:, j, :], j == 0, j == 2)
                    last.then_inc(sm["s2_O"], 1)
                for c in chunks:
                    pe.wait_ge(sm["s3_n"], done[c])
                    transposes(lambda t: PS[c][:, t, :], lambda t: n[c][:, t, :], top.ident[:, :])\
                        .then_inc(sm["s3_nT_psum"], 1)
                for c in chunks:
                    if c == 0:
                        pe.wait_ge(sm["mean_w_out"], 1)
                    pe.wait_ge(sm["s3_nT"], done[c])
                    for t in range(CT):
                        last = mm(PS[c][:, t, 0:DH], nT[c][:, t, :], top.w_qmeanT[:, :])
                    last.then_inc(sm["s3_qm"], 1)
                for c in chunks:
                    pe.wait_ge(sm["s3_z"], done[c])
                    transposes(lambda t: PS[c][0:DH, t, :], lambda t: z[c][:, t, :], top.ident[:, :])\
                        .then_inc(sm["s3_zT_psum"], 1)
                for c in chunks:
                    pe.wait_ge(sm["s3_H"], done[c])
                    for a in range(2):
                        last = mm(PS[c][0:PROJ, 4 * a:4 * a + 4, :], top.w1T[:, :], HT[c][:, S * a:S * a + S])
                    last.then_inc(sm["s3_pre"], 1)
                for c in chunks:
                    pe.wait_ge(sm["s3_hidden"], done[c])
                    for a in range(2):
                        last = mm(PS[c][0:1, 4 * a:4 * a + 4, :], top.w2T[:, :], u[c][:, S * a:S * a + S])
                    last.then_inc(sm["s3_score_psum"], 1)
        ph.close()


def gated_attention_phase(nc, top, dram):
    with ExitStack() as ctx:
        ph = Phase(nc, ctx, "b_")
        sm = ph.sems(
            "scores_in top8 replaced mask_row zeroed tok_psum tok mask_bf exp_gate gate_den gate rank_psum rank_sub "
            "rank rank_rows_psum rank_rows rank_wide selT plain sel gather_psum nonsel bars gathered "
            "qk_psum qk_out qk_out_a v_psum v_out c_psum c_out yuc_psum yu_copy yu dy "
            "dots_psum diag_d diag_a dmax dmax0 centred probs em dsum den rden probs_n blocks "
            "O_psum O_out Y_psum Y")
        NQ = TILES // 16
        SC = [ph.sb(f"SC{j}", [B, S]) for j in range(3)]
        top8 = ph.sb("top8", [B, 8])
        mask_row = ph.sb("mask_row", [B, S])
        tok = ph.sb("tok", [128, 2, R, B])
        mask_bf = ph.sb("mask_bf", [128, R, B], BF16)
        egate = ph.sb("egate", [128, R, B])
        gden = ph.sb("gden", [128, R, B])
        gate = ph.sb("gate", [128, R, B])
        rank = ph.sb("rank", [128, R, B])
        rank_rows = ph.sb("rank_rows", [B, S], BF16)
        SEL = ph.sb("SEL", [128, TILES, NSEL])
        gq = ph.sb("gq", [128, B, TOP_K])
        gv = ph.sb("gv", [128, B, TOP_K])
        means = ph.sb("means", [128, 2, B])
        QK = ph.sb("QK", [128, HEADS // 2, 2, B * TOP_K])
        V = ph.sb("V", [128, NQ, HEADS * DH])
        mv_ = ph.sb("meanv", [128, HEADS // 2, 2 * B])
        ya = ph.sb("ya", [B, D])
        dY = ph.sb("dY", [B, D])
        yu = ph.sb("yu", [B, D])
        diag = [ph.sb(f"diag{Q}", [128, HEADS, TOP_K]) for Q in range(NQ)]
        dmax = [ph.sb(f"dmax{Q}", [128, HEADS]) for Q in range(NQ)]
        em = [ph.sb(f"em{Q}", [128, HEADS]) for Q in range(NQ)]
        dsum = [ph.sb(f"dsum{Q}", [128, HEADS]) for Q in range(NQ)]
        PT = [ph.sb(f"PT{Q}", [128, HEADS, 128]) for Q in range(NQ)]
        OT = ph.sb("OT", [128, HEADS // 2, 128])
        P0 = ph.ps("P0", [128, 4, 512])
        P1 = ph.ps("P1", [128, 4, 512])
        HALF = HEADS // 4
        place = lambda h: h % 2 * (HEADS // 2) + h // 2
        bcast = lambda a, n: a.rearrange("p (t o) -> p t o", o=1).broadcast_to([128, a.shape[1], n])
        with nc.Block() as block:

            @block.sync
            def _(sp):
                sp.dma_start(SC[0][:, :], dram["scores"].rearrange("a (b s) -> (a b) s", b=B))\
                    .then_inc(sm["scores_in"], 16)

            @block.gpsimd
            def _(pool):
                nc.gpsimd.memset(SEL[:, :, NSEL - 1:NSEL], 1.0).then_inc(sm["zeroed"], 1)
                for Q in range(NQ):
                    nc.gpsimd.memset(PT[Q][:, :, :], 0.0).then_inc(sm["zeroed"], 1)

            @block.vector
            def _(dve):
                dve.wait_ge(sm["scores_in"], 16)
                for t in range(TOP_K // 8):
                    src = SC[0] if t == 0 else SC[1 + (t - 1) % 2]
                    if t:
                        dve.wait_ge(sm["replaced"], t)
                    nc.vector.max(top8[:, :], src[:, :]).then_inc(sm["top8"], 1)
                    dve.wait_ge(sm["top8"], t + 1)
                    nc.vector.match_replace(SC[1 + t % 2][:, :], top8[:, :], src[:, :], LOWEST)\
                        .then_inc(sm["replaced"], 1)
                dve.wait_ge(sm["replaced"], TOP_K // 8)
                nc.vector.tensor_tensor(mask_row[:, :], SC[0][:, :], SC[1 + (TOP_K // 8 - 1) % 2][:, :],
                                        ALU.not_equal).then_inc(sm["mask_row"], 1)
                dve.wait_ge(sm["tok_psum"], 1)
                nc.vector.tensor_copy(mask_bf[:, :, :], P0[:, 0, R * B:2 * R * B].rearrange("p (r b) -> p r b", r=R))\
                    .then_inc(sm["mask_bf"], 1)
                nc.vector.tensor_copy(tok[:, :, :, :], P0[:, 0, 0:2 * R * B].rearrange("p (k r b) -> p k r b", k=2, r=R))\
                    .then_inc(sm["tok"], 1)
                dve.wait_ge(sm["exp_gate"], 1)
                nc.vector.tensor_scalar(gden[:, :, :], egate[:, :, :], 1.0, None, ALU.add).then_inc(sm["gate_den"], 1)
                dve.wait_ge(sm["gate_den"], 1)
                nc.vector.reciprocal(gate[:, :, :], gden[:, :, :]).then_inc(sm["gate"], 1)
                dve.wait_ge(sm["rank_psum"], 1)
                dve.wait_ge(sm["tok"], 1)
                nc.vector.scalar_tensor_tensor(
                    out=rank[:, :, :], in0=P1[:, 0, 0:R * B].rearrange("p (r b) -> p r b", r=R), scalar=float(TOP_K),
                    in1=tok[:, 1, :, :], op0=ALU.subtract, op1=ALU.mult).then_inc(sm["rank_sub"], 1)
                dve.wait_ge(sm["rank_sub"], 1)
                nc.vector.tensor_scalar(rank[:, :, :], rank[:, :, :], float(TOP_K), None, ALU.add)\
                    .then_inc(sm["rank"], 1)
                dve.wait_ge(sm["rank"], 1)
                sel4 = SEL[:, :, :].rearrange("p (b r) j -> p b r j", b=B)
                rank4 = rank[:, :, :].rearrange("p r (b o) -> p b r o", o=1).broadcast_to([128, B, R, TOP_K + 1])
                gate4 = gate[:, :, :].rearrange("p r (b o) -> p b r o", o=1).broadcast_to([128, B, R, TOP_K])
                for b in range(B):
                    nc.vector.tensor_tensor(
                        sel4[:, b, :, TOP_K:2 * TOP_K + 1], rank4[:, b, :, :],
                        top.iota[:, 0:TOP_K + 1].rearrange("p (o j) -> p o j", o=1).broadcast_to([128, R, TOP_K + 1]),
                        ALU.is_equal).then_inc(sm["plain"], 1)
                dve.wait_ge(sm["gate"], 1)
                for b in range(B):
                    dve.wait_ge(sm["plain"], b + 1)
                    nc.vector.tensor_tensor(sel4[:, b, :, 0:TOP_K], sel4[:, b, :, TOP_K:2 * TOP_K],
                                            gate4[:, b, :, :], ALU.mult).then_inc(sm["sel"], 1)
                dve.wait_ge(sm["rank_rows_psum"], 1)
                nc.vector.tensor_copy(rank_rows[:, :], P1[0:B, 1, :]).then_inc(sm["rank_rows"], 1)
                dve.wait_ge(sm["rank_wide"], 1)
                for Q in range(NQ):
                    nc.vector.tensor_scalar(top.selT[Q][:, :], P1[:, 2 + Q, :], top.iota_col[:, :], None,
                                            ALU.is_equal).then_inc(sm["selT"], 1)
                dve.wait_ge(sm["gather_psum"], 1)
                G = P0[:, 0:2, :].rearrange("p a (b j) -> p (a b) j", j=128)
                nc.vector.tensor_scalar(means[:, 0, :], G[:, :, NSEL - 1], 1.0 / S, None, ALU.mult)
                nc.vector.tensor_scalar(means[:, 1, :], G[:, :, NSEL - 2], 1.0 / (S - TOP_K), None, ALU.mult)\
                    .then_inc(sm["bars"], 1)
                nc.vector.tensor_copy(gq[:, :, :], G[:, :, 0:TOP_K])
                dve.wait_ge(sm["bars"], 1)
                nc.vector.tensor_tensor(gv[:, :, :], G[:, :, TOP_K:2 * TOP_K], bcast(means[:, 1, :], TOP_K),
                                        ALU.subtract).then_inc(sm["gathered"], 1)
                dve.wait_ge(sm["qk_psum"], 1)
                nc.vector.tensor_copy(QK[:, 0:HALF, :, :], P1[:, :, :].rearrange("p i (k t) -> p i k t", k=2))\
                    .then_inc(sm["qk_out"], 1)
                dve.wait_ge(sm["v_psum"], 1)
                nc.vector.tensor_copy(V[:, :, :], P1[:, :, :].rearrange("p (Q a) n -> p Q (a n)", a=2))\
                    .then_inc(sm["v_out"], 1)
                dve.wait_ge(sm["c_psum"], 1)
                nc.vector.tensor_copy(mv_[:, :, :], P0[:, 0, 0:128].rearrange("p (i c) -> p i c", i=HEADS // 2))\
                    .then_inc(sm["c_out"], 1)
                dve.wait_ge(sm["yuc_psum"], 1)
                nc.vector.tensor_copy(ya[:, :], P0[0:B, 1, 0:D]).then_inc(sm["yu_copy"], 1)
                dve.wait_ge(sm["yu_copy"], 1)
                nc.vector.tensor_tensor(yu[:, :], ya[:, :], top.b_out[:, :], ALU.add).then_inc(sm["yu"], 1)
                nc.vector.tensor_tensor(dY[:, :], P0[0:B, 1, D:2 * D], ya[:, :], ALU.subtract).then_inc(sm["dy"], 1)
                for Q in range(NQ):
                    dve.wait_ge(sm["dots_psum"], Q + 1)
                    dots = (P0, P1)[Q][:, :, :].rearrange("p a (h k) -> p (a h) k", k=128)
                    for j in range(2):
                        rows = slice(32 * j, 32 * j + 32)
                        last = nc.vector.tensor_copy(diag[Q][rows, :, :], dots[rows, :, rows])
                    last.then_inc(sm["diag_d"], 1)
                for Q in range(NQ):
                    dve.wait_ge(sm["diag_d"], Q + 1)
                    dve.wait_ge(sm["diag_a"], Q + 1)
                    nc.vector.tensor_reduce(dmax[Q][:, :], diag[Q][:, :, :], AX.X, ALU.max).then_inc(sm["dmax"], 1)
                    dve.wait_ge(sm["dmax"], Q + 1)
                    nc.vector.tensor_scalar(dmax[Q][:, :], dmax[Q][:, :], 0.0, None, ALU.max).then_inc(sm["dmax0"], 1)
                    dve.wait_ge(sm["dmax0"], Q + 1)
                    nc.vector.tensor_tensor(diag[Q][:, :, :], diag[Q][:, :, :], bcast(dmax[Q][:, :], TOP_K),
                                            ALU.subtract).then_inc(sm["centred"], 1)
                for Q in range(NQ):
                    dve.wait_ge(sm["probs"], Q + 1)
                    nc.vector.tensor_reduce(dsum[Q][:, :], diag[Q][:, :, :], AX.X, ALU.add).then_inc(sm["dsum"], 1)
                    dve.wait_ge(sm["dsum"], Q + 1)
                    nc.vector.scalar_tensor_tensor(out=dsum[Q][:, :], in0=em[Q][:, :], scalar=float(S - TOP_K),
                                                   in1=dsum[Q][:, :], op0=ALU.mult, op1=ALU.add)\
                        .then_inc(sm["den"], 1)
                    dve.wait_ge(sm["den"], Q + 1)
                    nc.vector.reciprocal(dsum[Q][:, :], dsum[Q][:, :]).then_inc(sm["rden"], 1)
                    dve.wait_ge(sm["rden"], Q + 1)
                    nc.vector.tensor_tensor(diag[Q][:, :, :], diag[Q][:, :, :], bcast(dsum[Q][:, :], TOP_K),
                                            ALU.mult).then_inc(sm["probs_n"], 1)
                    dve.wait_ge(sm["probs_n"], Q + 1)
                    dve.wait_ge(sm["zeroed"], 1 + NQ)
                    for j in range(4):
                        rows = slice(32 * j, 32 * j + 32)
                        last = nc.vector.transpose(PT[Q][rows, :, rows], diag[Q][rows, :, :])
                    last.then_inc(sm["blocks"], 1)
                for Q in range(NQ):
                    dve.wait_ge(sm["O_psum"], Q + 1)
                    nc.vector.tensor_copy(OT[:, :, :], P0[:, 0:2, :].rearrange("p a (i t) -> p (a i) t", t=128))\
                        .then_inc(sm["O_out"], 1)
                    dve.wait_ge(sm["Y_psum"], Q + 1)
                    nc.vector.tensor_copy(top.Y[Q][:, :], P0[:, 2, 0:D])
                    nc.vector.tensor_copy(top.yU[Q][:, :], P0[:, 2, D:2 * D]).then_inc(sm["Y"], 1)

            @block.scalar
            def _(act):
                act.wait_ge(sm["tok"], 1)
                nc.scalar.activation(egate[:, :, :], tok[:, 0, :, :], ACT.Exp, scale=-1.0).then_inc(sm["exp_gate"], 1)
                act.wait_ge(sm["qk_psum"], 2)
                nc.scalar.activation(QK[:, HALF:, :, :], P0[:, :, :].rearrange("p i (k t) -> p i k t", k=2), ACT.Copy)\
                    .then_inc(sm["qk_out_a"], 1)
                for Q in range(NQ):
                    act.wait_ge(sm["dots_psum"], Q + 1)
                    dots = (P0, P1)[Q][:, :, :].rearrange("p a (h k) -> p (a h) k", k=128)
                    for j in range(2, 4):
                        rows = slice(32 * j, 32 * j + 32)
                        last = nc.scalar.activation(diag[Q][rows, :, :], dots[rows, :, rows], ACT.Copy)
                    last.then_inc(sm["diag_a"], 1)
                for Q in range(NQ):
                    act.wait_ge(sm["centred"], Q + 1)
                    nc.scalar.activation(em[Q][:, :], dmax[Q][:, :], ACT.Exp, scale=-float(DH) ** -0.5)
                    nc.scalar.activation(diag[Q][:, :, :], diag[Q][:, :, :], ACT.Exp, scale=float(DH) ** -0.5)\
                        .then_inc(sm["probs"], 1)

            @block.tensor
            def _(pe):
                def mm(out, lhsT, rhs, start=True, stop=True):
                    return nc.tensor.matmul(out, lhsT, rhs, start=start, stop=stop)

                pe.wait_ge(sm["mask_row"], 1)
                for k, src in enumerate((SC[0], mask_row)):
                    by_r = src[:, :].rearrange("b (p r) -> b r p", r=R)
                    for r in range(R):
                        o = (k * R + r) * B
                        last = nc.tensor.transpose(P0[:, 0, o:o + B], by_r[:, r, :], top.ident[0:B, 0:B])
                last.then_inc(sm["tok_psum"], 1)
                pe.wait_ge(sm["mask_bf"], 1)
                mm(P1[:, 0, 0:R * B], top.lower[:, :], mask_bf[:, :, :], True, False)
                for r in range(1, R):
                    for r2 in range(r):
                        last = mm(P1[:, 0, r * B:r * B + B], top.ones_bf[:, :], mask_bf[:, r2, :], False,
                                  r == R - 1 and r2 == r - 1)
                last.then_inc(sm["rank_psum"], 1)
                pe.wait_ge(sm["rank"], 1)
                for r in range(R):
                    last = nc.tensor.transpose(P1[0:B, 1, 128 * r:128 * r + 128], rank[:, r, :], top.ident[:, :])
                last.then_inc(sm["rank_rows_psum"], 1)
                pe.wait_ge(sm["tok"], 1)
                pe.wait_ge(sm["zeroed"], 1)
                for b in range(B):
                    pe.wait_ge(sm["sel"], b + 1)
                    for r in range(R):
                        last = mm(P0[:, b // 4, 128 * (b % 4):128 * (b % 4) + NSEL], top.N3[:, R * b + r, :],
                                  SEL[:, R * b + r, :], r == 0, r == R - 1)
                last.then_inc(sm["gather_psum"], 1)
                pe.wait_ge(sm["rank_rows"], 1)
                for Q in range(NQ):
                    last = mm(P1[:, 2 + Q, :], top.batch_rows_bf[:, Q, :], rank_rows[:, :])
                last.then_inc(sm["rank_wide"], 1)
                pe.wait_ge(sm["gathered"], 1)
                pe.wait_ge(sm["selT"], NQ)
                for half in range(2):
                    for i in range(HALF):
                        for k in range(2):
                            w = k * HEADS * DH + (half * HALF + i) * 128
                            last = mm((P1, P0)[half][:, i, 256 * k:256 * k + 256], top.w_qkvT[:, w:w + 128],
                                      gq[:, :, :])
                    last.then_inc(sm["qk_psum"], 1)
                pe.wait_ge(sm["qk_out"], 1)
                for Q in range(NQ):
                    for a in range(2):
                        w = 2 * HEADS * DH + 512 * a
                        last = mm(P1[:, 2 * Q + a, :], gv[:, 4 * Q:4 * Q + 4, :], top.w_qkvT[:, w:w + 512])
                last.then_inc(sm["v_psum"], 1)
                pe.wait_ge(sm["qk_out_a"], 1)
                for i in range(HEADS // 2):
                    w = 2 * HEADS * DH + 128 * i
                    last = mm(P0[:, 0, 16 * i:16 * i + 16], top.w_qkvT[:, w:w + 128], means[:, :, :])
                last.then_inc(sm["c_psum"], 1)
                pe.wait_ge(sm["c_out"], 1)
                for k in range(2):
                    for i in range(HEADS // 2):
                        last = mm(P0[0:B, 1, D * k:D * k + D], mv_[:, i, B * k:B * k + B], top.w_outT[:, i, :],
                                  i == 0, i == HEADS // 2 - 1)
                last.then_inc(sm["yuc_psum"], 1)
                for Q in range(NQ):
                    if Q == 0:
                        pe.wait_ge(sm["dy"], 1)
                    else:
                        pe.wait_ge(sm["v_out"], 1)
                    dots = (P0, P1)[Q]
                    for h in range(HEADS):
                        rows = slice(DH * (h % 2), DH * (h % 2) + DH)
                        at = place(h)
                        last = mm(dots[:, at // 4, 128 * (at % 4):128 * (at % 4) + 128],
                                  QK[rows, h // 2, 0, 128 * Q:128 * Q + 128], QK[rows, h // 2, 1, 128 * Q:128 * Q + 128])
                    last.then_inc(sm["dots_psum"], 1)
                for Q in range(NQ):
                    pe.wait_ge(sm["blocks"], Q + 1)
                    if Q:
                        pe.wait_ge(sm["O_out"], Q)
                    for h in range(HEADS):
                        rows = slice(DH * (h % 2), DH * (h % 2) + DH)
                        last = mm(P0[rows, h // 8, 128 * (h // 2 % 4):128 * (h // 2 % 4) + 128],
                                  V[:, Q, DH * h:DH * h + DH], PT[Q][:, place(h), :])
                    last.then_inc(sm["O_psum"], 1)
                    pe.wait_ge(sm["O_out"], Q + 1)
                    if Q:
                        pe.wait_ge(sm["Y"], Q)
                    for i in range(HEADS // 2):
                        mm(P0[:, 2, 0:D], OT[:, i, :], top.w_outT[:, i, :], i == 0, False)
                    mm(P0[:, 2, 0:D], top.batch_rows[:, Q, :], dY[:, :], False, True)
                    mm(P0[:, 2, D:2 * D], top.batch_rows[:, Q, :], yu[:, :]).then_inc(sm["Y_psum"], 1)
        ph.close()


def projection_phase(nc, top, dram):
    with ExitStack() as ctx:
        ph = Phase(nc, ctx, "c_")
        sm = ph.sems("y_psum y_stats y_mv y_std y_rstd y_norm y x stats mv var2 std rstd norm nb2 a n4 aT_psum aT "
                     "q_psum k_psum v_psum q1 k1 qr kr q2 k2 q3 k3 v_ready zeroed")
        stored = [ph.sem(f"stored{c}") for c in range(2)]
        two = range(2)
        a = [ph.sb(f"a{c}", [128, CT, D]) for c in two]
        y = [ph.sb(f"y{c}", [128, CT, D]) for c in two]
        aT = [ph.sb(f"aT{c}", [128, 2, S]) for c in two]
        Qp = [ph.sb(f"Qp{c}", [128, 3, 2, S], BF16) for c in two]
        Qr = [ph.sb(f"Qr{c}", [128, 2, S]) for c in two]
        Kp = [ph.sb(f"Kp{c}", [KVD, 3, 2, S], BF16) for c in two]
        Kr = [ph.sb(f"Kr{c}", [KVD, 2, S]) for c in two]
        st = [ph.sb(f"st{c}", [128, CT, 6]) for c in two]
        mv = [ph.sb(f"mv{c}", [128, CT, 2]) for c in two]
        std = [ph.sb(f"std{c}", [128, 2, CT]) for c in two]
        rs = [ph.sb(f"rs{c}", [128, 2, CT]) for c in two]
        nb = [ph.sb(f"nb{c}", [128, 2, CT]) for c in two]
        PA = [ph.ps(f"PA{c}", [128, CT, D]) for c in two]
        PB = [ph.ps(f"PB{c}", [128, CT, D]) for c in two]
        X, N4 = top.X, top.N4
        n_stored = [0, 0]

        with nc.Block() as block:

            @block.sync
            def _(sp):
                for k in range(CHUNKS):
                    c = k % 2
                    sp.wait_ge(sm["q3"], k + 1)
                    sp.wait_ge(sm["k3"], k + 1)
                    for b in (0, 1, 1) if k == CHUNKS - 1 else (0, 1):
                        entry = 2 * k + b + (1 if n_stored[c] == 12 * (k // 2) + 12 else 0)
                        for slot, n, qpart, kpart in PAIRS:
                            sp.dma_start(dram["q_store"](entry, slot, n), Qp[c][:, qpart:qpart + n, b, :])\
                                .then_inc(stored[c], 16)
                            sp.dma_start(dram["k_store"](entry, slot, n),
                                         Kp[c][:, kpart:kpart + 1, b, :].broadcast_to([KVD, n, S]))\
                                .then_inc(stored[c], 16)
                            n_stored[c] += 2
                for c in two:
                    sp.wait_ge(stored[c], 16 * n_stored[c])

            @block.gpsimd
            def _(pool):
                nc.gpsimd.memset(top.V4[:, :, :, HD4:VW], 0.0).then_inc(sm["zeroed"], 1)
                pool.wait_ge(sm["zeroed"], 1)
                nc.gpsimd.memset(top.V4[:, :, :, HD4:HD4 + 1], 1.0).then_inc(sm["zeroed"], 1)
                for k0 in range(0, CHUNKS, 2):
                    for k in (k0, k0 + 1):
                        c = k % 2
                        tiles = slice(CT * k, CT * k + CT)
                        pool.wait_ge(sm["y"], k + 1)
                        nc.gpsimd.tensor_tensor(X[:, tiles, :], X[:, tiles, :], y[c][:, :, :], ALU.add)\
                            .then_inc(sm["x"], 1)
                    for k in (k0, k0 + 1):
                        c = k % 2
                        for dst, src, s1, s2 in ((Kp, Kr, "k2", "k3"), (Qp, Qr, "q2", "q3")):
                            pool.wait_ge(sm[s1], k + 1)
                            nc.gpsimd.tensor_tensor(dst[c][:, 2, :, :], src[c][:, :, :], dst[c][:, 1, :, :],
                                                    ALU.subtract).then_inc(sm[s2], 1)

            @block.vector
            def _(dve):
                def stats(src, c, k, s):
                    for t in range(CT):
                        last = nc.vector.bn_stats(st[c][:, t, :], src(t))
                    last.then_inc(sm[s + "stats"], 1)
                    dve.wait_ge(sm[s + "stats"], k + 1)
                    for t in range(CT):
                        last = nc.vector.bn_aggr(mv[c][:, t, :], st[c][:, t, :])
                    last.then_inc(sm[s + "mv"], 1)

                def chunk_y(k):
                    c = k % 2
                    dve.wait_ge(sm["y_psum"], k + 1)
                    stats(lambda t: PA[c][:, t, :], c, k, "y_")
                    dve.wait_ge(sm["y_std"], k + 1)
                    nc.vector.reciprocal(rs[c][:, 0, :], std[c][:, 0, :]).then_inc(sm["y_rstd"], 1)
                    dve.wait_ge(sm["y_rstd"], k + 1)
                    dve.wait_ge(sm["y_mv"], k + 1)
                    nc.vector.scalar_tensor_tensor(out=nb[c][:, 0, :], in0=mv[c][:, :, 0], scalar=-1.0,
                                                   in1=rs[c][:, 0, :], op0=ALU.mult, op1=ALU.mult)\
                        .then_inc(sm["y_norm"], 1)

                def chunk_n(k):
                    c = k % 2
                    tiles = slice(CT * k, CT * k + CT)
                    dve.wait_ge(sm["x"], k + 1)
                    stats(lambda t: X[:, CT * k + t, :], c, k, "")
                    dve.wait_ge(sm["mv"], k + 1)
                    nc.vector.tensor_scalar(nb[c][:, 0, :], mv[c][:, :, 1], LN_EPS, None, ALU.add)
                    nc.vector.tensor_scalar(nb[c][:, 1, :], mv[c][:, :, 1], 1.0 + RMS_EPS, RMS_EPS * LN_EPS,
                                            ALU.mult, ALU.add).then_inc(sm["var2"], 1)
                    dve.wait_ge(sm["std"], k + 1)
                    nc.vector.reciprocal(rs[c][:, :, :], std[c][:, :, :]).then_inc(sm["rstd"], 1)
                    dve.wait_ge(sm["rstd"], k + 1)
                    nc.vector.scalar_tensor_tensor(out=nb[c][:, 1, :], in0=mv[c][:, :, 0], scalar=-1.0,
                                                   in1=rs[c][:, 1, :], op0=ALU.mult, op1=ALU.mult)\
                        .then_inc(sm["norm"], 1)
                    for t in range(CT):
                        last = nc.vector.tensor_scalar(N4[:, CT * k + t, :], X[:, CT * k + t, :], mv[c][:, t, 0:1],
                                                       rs[c][:, 0, t:t + 1], ALU.subtract, ALU.mult)
                    last.then_inc(sm["n4"], 1)
                    dve.wait_ge(sm["aT_psum"], k + 1)
                    nc.vector.tensor_copy(aT[c][:, :, :].rearrange("c b (p r) -> c b r p", r=R),
                                          PA[c][:, :, :].rearrange("c (b r) p -> c b r p", b=2)).then_inc(sm["aT"], 1)

                def chunk_p(k):
                    c = k % 2
                    dve.wait_ge(sm["k1"], k + 1)
                    nc.vector.tensor_tensor(Kr[c][:, :, :], PA[c][0:KVD, :, :].rearrange("p (b n) t -> p b (n t)", b=2),
                                            Kp[c][:, 0, :, :], ALU.subtract).then_inc(sm["kr"], 1)
                    dve.wait_ge(sm["q1"], k + 1)
                    nc.vector.tensor_tensor(Qr[c][:, :, :], PB[c][:, :, :].rearrange("p (b n) t -> p b (n t)", b=2),
                                            Qp[c][:, 0, :, :], ALU.subtract).then_inc(sm["qr"], 1)
                    dve.wait_ge(sm["v_psum"], k + 1)
                    if k == 0:
                        dve.wait_ge(sm["zeroed"], 2)
                    nc.vector.tensor_copy(top.V4[:, CT * k:CT * k + CT, :, 0:HD4],
                                          PB[c][:, 0:2, :].rearrange("p a (t g d) -> p (a t) g d", t=4, g=KV4))\
                        .then_inc(sm["v_ready"], 1)

                for k in range(0, CHUNKS, 2):
                    for f in (chunk_y, chunk_n, chunk_p):
                        for c in two:
                            f(k + c)

            @block.scalar
            def _(act):
                for k0 in range(0, CHUNKS, 2):
                    for k in (k0, k0 + 1):
                        c = k % 2
                        act.wait_ge(sm["y_mv"], k + 1)
                        nc.scalar.activation(std[c][:, 0, :], mv[c][:, :, 1], ACT.Sqrt, bias=top.eps[:, :])\
                            .then_inc(sm["y_std"], 1)
                    for k in (k0, k0 + 1):
                        c = k % 2
                        act.wait_ge(sm["y_norm"], k + 1)
                        for t in range(CT):
                            last = nc.scalar.activation(y[c][:, t, :], PA[c][:, t, :], ACT.Identity,
                                                        bias=nb[c][:, 0, t:t + 1], scale=rs[c][:, 0, t:t + 1])
                        last.then_inc(sm["y"], 1)
                    for k in (k0, k0 + 1):
                        c = k % 2
                        act.wait_ge(sm["var2"], k + 1)
                        nc.scalar.activation(std[c][:, :, :], nb[c][:, :, :], ACT.Sqrt).then_inc(sm["std"], 1)
                        act.wait_ge(sm["norm"], k + 1)
                        for t in range(CT):
                            last = nc.scalar.activation(a[c][:, t, :], X[:, CT * k + t, :], ACT.Identity,
                                                        bias=nb[c][:, 1, t:t + 1], scale=rs[c][:, 1, t:t + 1])
                        last.then_inc(sm["a"], 1)
                    for k in (k0, k0 + 1):
                        c = k % 2
                        kp = PA[c][0:KVD, :, :].rearrange("p (b n) t -> p b (n t)", b=2)
                        qp = PB[c][:, :, :].rearrange("p (b n) t -> p b (n t)", b=2)
                        for part, rest, ps, s0, s1, sr, s2 in ((Kp, Kr, kp, "k_psum", "k1", "kr", "k2"),
                                                               (Qp, Qr, qp, "q_psum", "q1", "qr", "q2")):
                            act.wait_ge(sm[s0], k + 1)
                            if k >= 2:
                                act.wait_ge(stored[c], 16 * 12 * (k // 2))
                            nc.scalar.activation(part[c][:, 0, :, :], ps, ACT.Copy).then_inc(sm[s1], 1)
                        for part, rest, sr, s2 in ((Kp, Kr, "kr", "k2"), (Qp, Qr, "qr", "q2")):
                            act.wait_ge(sm[sr], k + 1)
                            nc.scalar.activation(part[c][:, 1, :, :], rest[c][:, :, :], ACT.Copy).then_inc(sm[s2], 1)

            @block.tensor
            def _(pe):
                def mm(out, lhsT, rhs, start=True, stop=True):
                    return nc.tensor.matmul(out, lhsT, rhs, start=start, stop=stop)

                for k0 in range(0, CHUNKS, 2):
                    for k in (k0, k0 + 1):
                        c = k % 2
                        if k >= 2:
                            pe.wait_ge(sm["kr"], k - 1)
                        for t in range(CT):
                            b, r = 2 * k + t // R, t % R
                            rows = slice(TOP_K * (b % 4), TOP_K * (b % 4) + TOP_K)
                            mm(PA[c][:, t, :], top.selT[b // 4][rows, 128 * r:128 * r + 128],
                               top.Y[b // 4][rows, :], True, False)
                            last = mm(PA[c][:, t, :], top.first_row[rows, :], top.yU[b // 4][rows, :], False, True)
                        last.then_inc(sm["y_psum"], 1)
                    for k in (k0, k0 + 1):
                        c = k % 2
                        pe.wait_ge(sm["a"], k + 1)
                        for t in range(CT):
                            last = nc.tensor.transpose(PA[c][:, t, :], a[c][:, t, :], top.ident[:, :])
                        last.then_inc(sm["aT_psum"], 1)
                    for k in (k0, k0 + 1):
                        c = k % 2
                        pe.wait_ge(sm["aT"], k + 1)
                        if k >= 2:
                            pe.wait_ge(sm["v_ready"], k - 1)
                        for b in range(2):
                            last = mm(PA[c][0:KVD, R * b:R * b + R, :], top.wk4T[:, :], aT[c][:, b, :])
                        last.then_inc(sm["k_psum"], 1)
                        for b in range(2):
                            last = mm(PB[c][:, R * b:R * b + R, :], top.wq4T[:, :], aT[c][:, b, :])
                        last.then_inc(sm["q_psum"], 1)
                    for k in (k0, k0 + 1):
                        c = k % 2
                        pe.wait_ge(sm["qr"], k + 1)
                        for t in range(CT):
                            last = mm(PB[c][:, t // 4, KVD * (t % 4):KVD * (t % 4) + KVD],
                                      aT[c][:, t // 4, 128 * (t % 4):128 * (t % 4) + 128], top.wv4T[:, :])
                        last.then_inc(sm["v_psum"], 1)
        ph.close()


def causal_attention_phase(nc, top, dram):
    with ExitStack() as ctx:
        ph = Phase(nc, ctx, "d_")
        sm = ph.sems("zeros ones ones_from max_ones S S_max part1 rest1 part2 rest2 parts mT_psum mT ST P masked PV O_sb O_T rden O_tok")
        two = range(2)
        stacks = [[ph.sem(f"stacks{c}{a}") for a in two] for c in two]
        v_in = [ph.sem(f"v_in{c}") for c in two]
        rows_stored = [ph.sem(f"rows_stored{c}") for c in two]
        rows_in = [ph.sem(f"rows_in{c}") for c in two]
        Qs = [ph.sb(f"Qs{c}", [128, HEADS // 2, S], BF16) for c in two]
        Ks = [ph.sb(f"Ks{c}", [128, KV4, S], BF16) for c in two]
        V = [ph.sb(f"V{c}", [128, QT, KV4, VW]) for c in two]
        mx = [ph.sb(f"mx{c}", [128, QT, HEADS]) for c in two]
        rest = [ph.sb(f"rest{c}", [128, 2, QT, HEADS]) for c in two]
        m3 = [ph.sb(f"m3{c}", [128, QT, 3, HEADS], BF16) for c in two]
        mT = [ph.sb(f"mT{c}", [3 * HEADS, S], BF16) for c in two]
        P = [ph.sb(f"P{k}", [128, 2, PAIRW]) for k in range(4)]
        OT = [ph.sb(f"OT{k}", [128, S]) for k in two]
        rden = ph.sb("rden", [128, QT, 2, 2])
        pS = [ph.ps(f"pS{k}", [128, 512]) for k in two]
        pT = [ph.ps(f"pT{k}", [128, 2, 512]) for k in two]
        pO = ph.ps("pO", [128, S])
        pM = ph.ps("pM", [128, S])
        NS, NT, NG = 3 * HEADS, 3 * HEADS // 2, KV4
        ROWS = SLOTS * HD4
        ALL_ROWS = 2 * ROWS
        WITH_MAX = ALL_ROWS + 6
        ORDER = [8 * a + i for i in range(HEADS // 2) for a in two]
        P_AT = (0, 512, 896, 1152)

        def wait(eng, sem, value):
            if not isinstance(value, int) or value > 0:
                eng.wait_ge(sem, value)

        def steps(eng, step):
            step(0, 0, True)
            with eng.Fori(0, B // 2 - 1) as i:
                step(2 * i + 1, i, True)
                step(2 * i + 2, i + 1, True)
            step(B - 1, B // 2 - 1, False)

        def fills(pair):
            places = [2 * (pair + LEAD) + j for j in two]
            return [(1 + k // HEADS, k % HEADS, f) for k in places for f in range(3)]

        def others(n, m, c, ahead):
            return (n + 1, m + c, 1 - c) if ahead == 1 else (n + 2, m + 1, c)

        def turn(pair, unit, at):
            g, off = divmod(3 * (pair - 2) + unit - 1 - at, 6)
            return None if off else (0 if g >= 0 else 1, g % NG)

        def turns(n, pair, unit, at):
            got = turn(pair, unit, at)
            ended = isinstance(n, int) and n == B
            if got is None or (got[0] == 0 and ended) or (got[0] == 1 and isinstance(n, int) and n == 0):
                return []
            return [(n - got[0], got[1], got[0])]

        LAST_TURNS = [(u // 3, u % 3) for u in range(7)]
        everything = [(k, f) for k in range(HEADS) for f in range(3)]
        SPLIT_AT = HEADS // 2 - LEAD
        parity = [0]

        def par(n):
            if isinstance(n, int):
                parity[0] = n % 2
            else:
                parity[0] = 1 - parity[0]
            return parity[0]

        with nc.Block() as block:

            @block.sync
            def _(sp):
                def load_stack(b, c, u):
                    for a in two:
                        rows = slice(ROWS * a, ROWS * a + ROWS)
                        sp.dma_start(Qs[c][rows, 4 * u:4 * u + 4, :], dram["q_load"](b, 8 * a + 4 * u, 4))\
                            .then_inc(stacks[c][u], 16)
                        sp.dma_start(Ks[c][rows, 2 * a + u:2 * a + u + 1, :], dram["k_load"](b, 2 * a + u, 1))\
                            .then_inc(stacks[c][u], 16)

                def load_v(b, c):
                    sp.dma_start(V[c][:, :, :, :], top.V4[:, bass.ds(b * QT, QT), :, :]).then_inc(v_in[c], 16)

                def max_rows(n, m, c):
                    sp.wait_ge(sm["mT"], n + 1)
                    sp.dma_start(dram["m_store"](c), mT[c][:, :]).then_inc(rows_stored[c], 16)
                    sp.wait_ge(rows_stored[c], 16 * m + 16)
                    for a in two:
                        at = ALL_ROWS + 3 * a
                        sp.dma_start(Qs[c][at:at + 3, :, :], dram["m_load"](c, a))\
                            .then_inc(rows_in[c], 16)

                def step(n, m, more):
                    c = par(n)
                    if more:
                        wait(sp, sm["PV"], n * NG)
                        load_v(n + 1, 1 - c)
                        if not (isinstance(n, int) and n + 2 > B):
                            sp.wait_ge(sm["ST"], n * NT + NT // 2)
                            load_stack(n + 2, c, 0)
                        max_rows(n + 1, m if c == 0 else m + 1, 1 - c)
                        sp.wait_ge(sm["ST"], n * NT + NT)
                        load_stack(n + 2, c, 1)

                sp.wait_ge(sm["zeros"], 2)
                for b in two:
                    for u in two:
                        load_stack(b, b, u)
                load_v(0, 0)
                max_rows(0, 0, 0)
                steps(sp, step)
                for a in two:
                    sp.wait_ge(stacks[0][a], 64 * (B // 2 + 1))

            @block.gpsimd
            def _(pool):
                def step(n, m, more):
                    par(n)
                    for pair in range(HEADS // 2):
                        for unit in range(3):
                            wait_alone(pool, sm["P"], n * NT + 3 * pair + unit + 1)
                            for at in ((P_AT[0],), (P_AT[1],), P_AT[2:])[unit]:
                                view = P[pair % 4][:, :, at:at + 128]
                                last = nc.gpsimd.affine_select(out=view, in_=view, compare_op=ALU.is_ge, fill=0.0,
                                                               base=0, pattern=[[0, 2], [1, 128]],
                                                               channel_multiplier=-1)
                            last.then_inc(sm["masked"], 1)

                for c in two:
                    nc.gpsimd.memset(Ks[c][0:ALL_ROWS, :, :], 0.0).then_inc(sm["zeros"], 1)
                    nc.gpsimd.memset(Ks[c][ALL_ROWS:128, :, :], 1.0).then_inc(sm["ones"], 1)
                for c in two:
                    pool.wait_ge(sm["ones"], c + 1)
                    for a in two:
                        view = Ks[c][ALL_ROWS:128, 2 * a:2 * a + 2, :]
                        nc.gpsimd.affine_select(out=view, in_=view, compare_op=ALU.is_ge, fill=0.0, base=-3 * a,
                                                pattern=[[0, 2], [0, S]], channel_multiplier=1)\
                            .then_inc(sm["ones_from"], 1)
                        pool.wait_ge(sm["ones_from"], 2 * c + a + 1)
                        nc.gpsimd.affine_select(out=view, in_=view, compare_op=ALU.is_ge, fill=0.0, base=3 * a + 2,
                                                pattern=[[0, 2], [0, S]], channel_multiplier=-1)\
                            .then_inc(sm["max_ones"], 1)
                steps(pool, step)

            @block.vector
            def _(dve):
                def maxima(n, c, some):
                    for k, f in some:
                        h, fill = ORDER[k], 3 * k + f
                        dve.wait_ge(sm["S"], n * NS + fill + 1)
                        src = pS[fill % 2]
                        if f < 2:
                            last = nc.vector.reduce_max(mx[c][:, 3 - f, h:h + 1], src[:, 0:512 - 128 * f], AX.X)
                        else:
                            nc.vector.reduce_max(mx[c][:, 1, h:h + 1], src[:, 0:256], AX.X)
                            last = nc.vector.reduce_max(mx[c][:, 0, h:h + 1], src[:, 256:384], AX.X)
                        last.then_inc(sm["S_max"], 1)

                def split(n, c):
                    dve.wait_ge(sm["S_max"], n * NS + NS)
                    nc.vector.tensor_scalar(m3[c][:, :, 0, :], mx[c][:, :, :], -1.0, None, ALU.mult)\
                        .then_inc(sm["part1"], 1)
                    dve.wait_ge(sm["part1"], n + 1)
                    nc.vector.scalar_tensor_tensor(out=rest[c][:, 0, :, :], in0=mx[c][:, :, :], scalar=-1.0,
                                                   in1=m3[c][:, :, 0, :], op0=ALU.mult, op1=ALU.subtract)\
                        .then_inc(sm["rest1"], 1)
                    dve.wait_ge(sm["rest1"], n + 1)
                    nc.vector.tensor_copy(m3[c][:, :, 1, :], rest[c][:, 0, :, :]).then_inc(sm["part2"], 1)
                    dve.wait_ge(sm["part2"], n + 1)
                    nc.vector.tensor_tensor(m3[c][:, :, 2, :], rest[c][:, 0, :, :], m3[c][:, :, 1, :], ALU.subtract)\
                        .then_inc(sm["parts"], 1)

                def divide(n, g):
                    dve.wait_ge(sm["O_T"], n * NG + g + 1)
                    o = pM[:, :].rearrange("p (q i a d) -> p q i a d", q=QT, i=2, a=2)
                    nc.vector.reciprocal(rden[:, :, :, :], o[:, :, :, :, HD4]).then_inc(sm["rden"], 1)
                    dve.wait_ge(sm["rden"], n * NG + g + 1)
                    for i in two:
                        at = HD4 * (2 * g + i)
                        last = nc.vector.tensor_tensor(
                            top.O4[:, bass.ds(n * QT, QT), :].rearrange("p q (a x) -> p q a x", a=2)
                            [:, :, :, at:at + HD4], o[:, :, i, :, 0:HD4],
                            rden[:, :, i, :].rearrange("p q (a o) -> p q a o", o=1)
                            .broadcast_to([128, QT, 2, HD4]), ALU.mult)
                    last.then_inc(sm["O_tok"], 1)

                def step(n, m, more):
                    c = par(n)
                    for pair in range(HEADS // 2):
                        if more and pair == SPLIT_AT:
                            split(n + 1, 1 - c)
                        for unit in range(3):
                            if more:
                                for ahead, k, f in fills(pair)[2 * unit:2 * unit + 2]:
                                    b, _, b_c = others(n, m, c, ahead)
                                    maxima(b, b_c, [(k, f)])
                            for b, g, _ in turns(n, pair, unit, 5):
                                divide(b, g)

                maxima(0, 0, everything)
                split(0, 0)
                maxima(1, 1, everything[:6 * LEAD])
                steps(dve, step)
                for pair, unit in LAST_TURNS:
                    for b, g, _ in turns(B, pair, unit, 5):
                        divide(b, g)

            @block.scalar
            def _(act):
                def rows(n, c):
                    act.wait_ge(sm["mT_psum"], n + 1)
                    nc.scalar.activation(mT[c][:, :], pM[0:3 * HEADS, 0:S // 2].bitcast(BF16), ACT.Copy)\
                        .then_inc(sm["mT"], 1)

                def evacuate(n, g):
                    act.wait_ge(sm["PV"], n * NG + g + 1)
                    wait(act, sm["O_T"], n * NG + g - 1)
                    nc.scalar.activation(OT[g % 2][:, :], pO[:, :], ACT.Copy).then_inc(sm["O_sb"], 1)

                def step(n, m, more):
                    c = par(n)
                    for pair in range(HEADS // 2):
                        for unit in range(3):
                            act.wait_ge(sm["ST"], n * NT + 3 * pair + unit + 1)
                            if unit == 0:
                                wait(act, sm["PV"], n * NG + pair // 2 - 1)
                            w = 512 if unit == 0 else 384
                            nc.scalar.activation(P[pair % 4][:, :, P_AT[unit]:P_AT[unit] + w],
                                                 pT[(3 * pair + unit) % 2][:, :, 0:w], ACT.Exp,
                                                 scale=float(HD4) ** -0.5).then_inc(sm["P"], 1)
                            if more and pair == SPLIT_AT and unit == 1:
                                rows(n + 1, 1 - c)
                            for b, g, _ in turns(n, pair, unit, 3):
                                evacuate(b, g)

                rows(0, 0)
                steps(act, step)
                for pair, unit in LAST_TURNS:
                    for b, g, _ in turns(B, pair, unit, 3):
                        evacuate(b, g)

            @block.tensor
            def _(pe):
                def mm(out, lhsT, rhs, start=True, stop=True):
                    return nc.tensor.matmul(out, lhsT, rhs, start=start, stop=stop)

                def first(n, m, c, some):
                    for k, f in some:
                        h, i = ORDER[k], ORDER[k] % 8
                        if k % 8 == 0 and f == 0:
                            pe.wait_ge(stacks[c][k // 8], 64 * m + 64)
                        wait(pe, sm["S_max"], n * NS + 3 * k + f - 1)
                        dst = pS[(3 * k + f) % 2]
                        for q, at in ((3, 0),) if f == 0 else ((2, 0),) if f == 1 else ((1, 0), (0, 256)):
                            w = 128 * q + 128
                            mm(dst[:, at:at + w], Qs[c][0:ALL_ROWS, i, 128 * q:128 * q + 128],
                               Ks[c][0:ALL_ROWS, h // 4, 0:w], True, False)
                            last = mm(dst[:, at + w - 128:at + w], top.ident_bf[:, :], top.mask_bf[:, :],
                                      False, True)
                        last.then_inc(sm["S"], 1)

                def second(n, m, c, pair, unit):
                    if pair == 0 and unit == 0:
                        pe.wait_ge(sm["max_ones"], 4)
                        pe.wait_ge(rows_in[c], 32 * m + 32)
                    wait(pe, sm["P"], n * NT + 3 * pair + unit - 1)
                    dst = pT[(3 * pair + unit) % 2]
                    for j in two:
                        for kt, at in ((0, 0),) if unit == 0 else ((1, 0),) if unit == 1 else ((2, 0), (3, 256)):
                            w = S - 128 * kt
                            last = mm(dst[:, j, at:at + w], Ks[c][0:WITH_MAX, 2 * j + pair // 4,
                                                                  128 * kt:128 * kt + 128],
                                      Qs[c][0:WITH_MAX, pair, 128 * kt:S])
                    last.then_inc(sm["ST"], 1)

                def values(n, m, c, g, kt):
                    if kt == 0:
                        if g == 0:
                            pe.wait_ge(v_in[c], 16 * m + 16)
                        pe.wait_ge(sm["masked"], n * NT + 6 * g + 6)
                        wait(pe, sm["O_sb"], n * NG + g)
                    w = S - 128 * kt
                    for j in range(4):
                        last = mm(pO[32 * j:32 * j + 32, 128 * kt:S], V[c][:, kt, 2 * (j % 2) + g // 2, :],
                                  P[(2 * g + j // 2) % 4][:, j % 2, P_AT[kt]:P_AT[kt] + w], kt == 0, kt == QT - 1)
                    if kt == QT - 1:
                        last.then_inc(sm["PV"], 1)

                def outputs(n, m, c, pair, unit, more):
                    for kt in range(QT):
                        for b, g, back in turns(n, pair, unit, kt):
                            values(b, m + c - 1 if back else m, 1 - c if back else c, g, kt)
                    for b, g, _ in turns(n, pair, unit, 5):
                        by_token(b, g, more)

                def by_token(n, g, more=False):
                    pe.wait_ge(sm["O_sb"], n * NG + g + 1)
                    wait(pe, sm["O_tok"], n * NG + g)
                    if more and g == 1:
                        pe.wait_ge(sm["mT"], n + 2)
                    for q in range(QT):
                        last = nc.tensor.transpose(pM[:, 128 * q:128 * q + 128],
                                                   OT[g % 2][:, 128 * q:128 * q + 128], top.ident[:, :])
                    last.then_inc(sm["O_T"], 1)

                def rows(n, c):
                    if not (isinstance(n, int) and n == 0):
                        wait_alone(pe, sm["O_tok"], (n - 1) * NG + 1)
                    wait_alone(pe, sm["parts"], n + 1)
                    for q in range(QT):
                        last = nc.tensor.transpose(pM[0:3 * HEADS, 64 * q:64 * q + 64].bitcast(BF16),
                                                   m3[c][:, q, :, :].rearrange("p k h -> p (k h)"), top.ident_bf[:, :])
                    last.then_inc(sm["mT_psum"], 1)

                def step(n, m, more):
                    c = par(n)
                    for pair in range(HEADS // 2):
                        for unit in range(3):
                            second(n, m, c, pair, unit)
                            if more:
                                for ahead, k, f in fills(pair)[2 * unit:2 * unit + 2]:
                                    first(*others(n, m, c, ahead), [(k, f)])
                                if pair == SPLIT_AT and unit == 1:
                                    rows(n + 1, 1 - c)
                            outputs(n, m, c, pair, unit, more)

                first(0, 0, 0, everything)
                rows(0, 0)
                first(1, 0, 1, everything[:6 * LEAD])
                steps(pe, step)
                for pair, unit in LAST_TURNS:
                    outputs(B, B // 2, 0, pair, unit, False)
        ph.close()


def experts_phase(nc, top, dram, out):
    with ExitStack() as ctx:
        ph = Phase(nc, ctx, "e_")
        sm = ph.sems("oT_psum oT proj h sq rms rrms hT_psum hT logits best index diff ediff wden w1 w2 picks pick1 "
                     "comb0 comb0b comb scale exp_psum scaled_d scaled_a halved summed total stats mv std rstd y out "
                     "stored")
        chunks = range(CHUNKS)
        two = range(2)
        small = lambda name, *shape, dt=FP32: [ph.sb(f"{name}{c}", [128, *shape], dt) for c in chunks]
        oT = small("oT", 2, S)
        hT = oT
        h, moe = small("h", CT, D), small("moe", CT, D)
        sq, rms, rr, rs, std = (small(name, CT) for name in ("sq", "rms", "rr", "rs", "std"))
        best, logit, index = small("best", CT, 8), small("logit", CT, NE), small("index", CT, 8, dt=mybir.dt.uint32)
        indexf, pick, comb = small("indexf", CT, 2), small("pick", 2, CT, NE), small("comb", CT, NE)
        w = small("w", 4, CT)
        st, mv = small("st", CT, 6), small("mv", CT, 2)
        T = [ph.sb(f"T{k}", [128, NE, D]) for k in range(4)]
        PA = [ph.ps(f"PA{k}", [128, CT, D]) for k in two]
        PE_ = [ph.ps(f"PE{k}", [128, NE, D]) for k in two]
        X = [top.X[:, CT * c:CT * c + CT, :] for c in chunks]
        N4 = [top.N4[:, CT * c:CT * c + CT, :] for c in chunks]
        O4 = [top.O4[:, CT * c:CT * c + CT, :] for c in chunks]
        wide = lambda a, n: a.rearrange("p (t o) -> p t o", o=1).broadcast_to([128, a.shape[1], n])
        by_batch = lambda a: a.rearrange("p (b n) t -> p b (n t)", b=2)
        LAG = 2
        PE_STEPS = {-11: "attention_by_channel", -9: "project", -7: "h_by_channel", -5: "gate"}
        DVE_STEPS = {-8: "residual", -4: "choose", -2: "weigh", 11: "total", 13: "normalise"}
        ACT_STEPS = {-10: "attention_by_channel", -7: "mean_square", -6: "h_by_channel", -3: "exp_difference",
                     12: "deviation"}
        TURNS = range(-11, TILES + 6)

        def due(u, steps):
            return [(steps[u - CT * c], c) for c in chunks if u - CT * c in steps]


        with nc.Block() as block:

            @block.sync
            def _(sp):
                for c in chunks:
                    sp.wait_ge(sm["out"], c + 1)
                    sp.dma_start(out[:, CT * c:CT * c + CT, :], moe[c][:, :, :]).then_inc(sm["stored"], 16)
                sp.wait_ge(sm["stored"], 16 * CHUNKS)

            @block.gpsimd
            def _(pool):
                def finish(c):
                    pool.wait_ge(sm["y"], c + 1)
                    nc.gpsimd.tensor_tensor(moe[c][:, :, :], h[c][:, :, :], X[c][:, :, :], ALU.add)\
                        .then_inc(sm["out"], 1)

                for u in range(TILES):
                    pool.wait_ge(sm["scaled_a" if u % 2 else "scaled_d"], u // 2 + 1)
                    nc.gpsimd.tensor_tensor(T[u % 4][:, 0:NE // 2, :], T[u % 4][:, 0:NE // 2, :],
                                            T[u % 4][:, NE // 2:NE, :], ALU.add).then_inc(sm["halved"], 1)
                    if u > CT and u % CT == 7:
                        finish(u // CT - 1)
                finish(CHUNKS - 1)

            @block.vector
            def _(dve):
                def residual(c):
                    dve.wait_ge(sm["proj"], c + 1)
                    nc.vector.tensor_tensor(h[c][:, :, :], PA[c % 2][:, :, :], N4[c][:, :, :], ALU.add)\
                        .then_inc(sm["h"], 1)

                def choose(c):
                    dve.wait_ge(sm["rms"], c + 1)
                    nc.vector.reciprocal(rr[c][:, :], rms[c][:, :]).then_inc(sm["rrms"], 1)
                    dve.wait_ge(sm["rrms"], c + 1)
                    dve.wait_ge(sm["logits"], c + 1)
                    nc.vector.tensor_tensor(logit[c][:, :, :],
                                            PA[c % 2][:, 0, 0:CT * NE].rearrange("p (t e) -> p t e", e=NE),
                                            wide(rr[c][:, :], NE), ALU.mult).then_inc(sm["scale"], 1)
                    dve.wait_ge(sm["scale"], c + 1)
                    for t in range(CT):
                        last = nc.vector.max(best[c][:, t, :], logit[c][:, t, :])
                    last.then_inc(sm["best"], 1)
                    dve.wait_ge(sm["best"], c + 1)
                    nc.vector.tensor_tensor(w[c][:, 0, :], best[c][:, :, 1], best[c][:, :, 0], ALU.subtract)\
                        .then_inc(sm["diff"], 1)
                    for t in range(CT):
                        last = nc.vector.max_index(index[c][:, t, :], best[c][:, t, :], logit[c][:, t, :])
                    last.then_inc(sm["index"], 1)
                    dve.wait_ge(sm["index"], c + 1)
                    nc.vector.tensor_copy(indexf[c][:, :, :], index[c][:, :, 0:2]).then_inc(sm["picks"], 1)
                    dve.wait_ge(sm["picks"], c + 1)
                    for j in two:
                        last = nc.vector.tensor_tensor(
                            pick[c][:, j, :, :], wide(indexf[c][:, :, j], NE),
                            top.iota[:, 0:NE].rearrange("p (o e) -> p o e", o=1).broadcast_to([128, CT, NE]),
                            ALU.is_equal)
                    last.then_inc(sm["pick1"], 1)

                def weigh(c):
                    dve.wait_ge(sm["ediff"], c + 1)
                    nc.vector.tensor_scalar(w[c][:, 2, :], w[c][:, 1, :], 1.0, None, ALU.add).then_inc(sm["wden"], 1)
                    dve.wait_ge(sm["wden"], c + 1)
                    nc.vector.reciprocal(w[c][:, 3, :], w[c][:, 2, :]).then_inc(sm["w1"], 1)
                    dve.wait_ge(sm["w1"], c + 1)
                    nc.vector.tensor_tensor(w[c][:, 2, :], w[c][:, 3, :], rr[c][:, :], ALU.mult).then_inc(sm["w2"], 1)
                    dve.wait_ge(sm["w2"], c + 1)
                    nc.vector.tensor_tensor(w[c][:, 3, :], w[c][:, 2, :], w[c][:, 1, :], ALU.mult)
                    dve.wait_ge(sm["pick1"], c + 1)
                    nc.vector.tensor_tensor(pick[c][:, 0, :, :], pick[c][:, 0, :, :], wide(w[c][:, 2, :], NE),
                                            ALU.mult).then_inc(sm["comb0"], 1)
                    dve.wait_ge(sm["comb0"], c + 1)
                    nc.vector.tensor_tensor(pick[c][:, 1, :, :], pick[c][:, 1, :, :], wide(w[c][:, 3, :], NE),
                                            ALU.mult).then_inc(sm["comb0b"], 1)
                    dve.wait_ge(sm["comb0b"], c + 1)
                    nc.vector.tensor_tensor(comb[c][:, :, :], pick[c][:, 0, :, :], pick[c][:, 1, :, :],
                                            ALU.add).then_inc(sm["comb"], 1)
                    dve.wait_ge(sm["comb"], c + 1)

                def scale_tile(u):
                    dve.wait_ge(sm["exp_psum"], u + 1)
                    if u >= 4:
                        dve.wait_ge(sm["summed"], u - 3)
                    nc.vector.tensor_tensor(T[u % 4][:, :, :], PE_[0][:, :, :], wide(comb[u // CT][:, u % CT, :], D),
                                            ALU.mult).then_inc(sm["scaled_d"], 1)

                def sum_tile(u):
                    dve.wait_ge(sm["halved"], u + 1)
                    nc.vector.tensor_reduce(moe[u // CT][:, u % CT, :],
                                            T[u % 4][:, 0:NE // 2, :].rearrange("p e d -> p d e"),
                                            AX.X, ALU.add).then_inc(sm["summed"], 1)

                def total(c):
                    dve.wait_ge(sm["summed"], c * CT + CT)
                    nc.vector.tensor_tensor(h[c][:, :, :], h[c][:, :, :], moe[c][:, :, :], ALU.add)\
                        .then_inc(sm["total"], 1)
                    dve.wait_ge(sm["total"], c + 1)
                    for t in range(CT):
                        last = nc.vector.bn_stats(st[c][:, t, :], h[c][:, t, :])
                    last.then_inc(sm["stats"], 1)
                    dve.wait_ge(sm["stats"], c + 1)
                    for t in range(CT):
                        last = nc.vector.bn_aggr(mv[c][:, t, :], st[c][:, t, :])
                    last.then_inc(sm["mv"], 1)

                def normalise(c):
                    dve.wait_ge(sm["std"], c + 1)
                    nc.vector.reciprocal(rs[c][:, :], std[c][:, :]).then_inc(sm["rstd"], 1)
                    dve.wait_ge(sm["rstd"], c + 1)
                    for t in range(CT):
                        last = nc.vector.tensor_scalar(h[c][:, t, :], h[c][:, t, :], mv[c][:, t, 0:1],
                                                       rs[c][:, t:t + 1], ALU.subtract, ALU.mult)
                    last.then_inc(sm["y"], 1)

                for u in TURNS:
                    if 0 <= u < TILES and u % 2 == 0:
                        scale_tile(u)
                    if LAG <= u < TILES + LAG:
                        sum_tile(u - LAG)
                    for step, c in due(u, DVE_STEPS):
                        if step == "residual":
                            residual(c)
                        if step == "choose":
                            choose(c)
                        if step == "weigh":
                            weigh(c)
                        if step == "total":
                            total(c)
                        if step == "normalise":
                            normalise(c)

            @block.scalar
            def _(act):
                def attention_by_channel(c):
                    act.wait_ge(sm["oT_psum"], c + 1)
                    nc.scalar.activation(oT[c][:, :, :], by_batch(PA[c % 2][:, :, :]), ACT.Copy).then_inc(sm["oT"], 1)

                def h_by_channel(c):
                    act.wait_ge(sm["hT_psum"], c + 1)
                    nc.scalar.activation(hT[c][:, :, :], by_batch(PA[c % 2][:, :, :]), ACT.Copy).then_inc(sm["hT"], 1)

                def mean_square(c):
                    act.wait_ge(sm["h"], c + 1)
                    for t in range(CT):
                        last = nc.scalar.activation(moe[c][:, t, :], h[c][:, t, :], ACT.Square,
                                                    accum_out=sq[c][:, t:t + 1])
                    last.then_inc(sm["sq"], 1)
                    act.wait_ge(sm["sq"], c + 1)
                    nc.scalar.activation(rms[c][:, :], sq[c][:, :], ACT.Sqrt, scale=1.0 / D, bias=top.eps_rms[:, :])\
                        .then_inc(sm["rms"], 1)

                def deviation(c):
                    act.wait_ge(sm["mv"], c + 1)
                    nc.scalar.activation(std[c][:, :], mv[c][:, :, 1], ACT.Sqrt, bias=top.eps[:, :])\
                        .then_inc(sm["std"], 1)

                def exp_difference(c):
                    act.wait_ge(sm["diff"], c + 1)
                    nc.scalar.activation(w[c][:, 1, :], w[c][:, 0, :], ACT.Exp).then_inc(sm["ediff"], 1)

                for u in TURNS:
                    if 0 <= u < TILES and u % 2:
                        act.wait_ge(sm["comb"], u // CT + 1)
                        act.wait_ge(sm["exp_psum"], u + 1)
                        if u >= 4:
                            act.wait_ge(sm["summed"], u - 3)
                        for e in range(NE):
                            last = nc.scalar.activation(T[u % 4][:, e, :], PE_[1][:, e, :], ACT.Copy,
                                                        scale=comb[u // CT][:, u % CT, e:e + 1])
                        last.then_inc(sm["scaled_a"], 1)
                    for step, c in due(u, ACT_STEPS):
                        if step == "attention_by_channel":
                            attention_by_channel(c)
                        if step == "h_by_channel":
                            h_by_channel(c)
                        if step == "mean_square":
                            mean_square(c)
                        if step == "exp_difference":
                            exp_difference(c)
                        if step == "deviation":
                            deviation(c)

            @block.tensor
            def _(pe):
                def mm(out_, lhsT, rhs, start=True, stop=True):
                    return nc.tensor.matmul(out_, lhsT, rhs, start=start, stop=stop)

                def attention_by_channel(c):
                    if c >= 2:
                        pe.wait_ge(sm["scale"], c - 1)
                    for t in range(CT):
                        last = nc.tensor.transpose(PA[c % 2][:, t, :], O4[c][:, t, :], top.ident[:, :])
                    last.then_inc(sm["oT_psum"], 1)

                def project(c):
                    pe.wait_ge(sm["oT"], c + 1)
                    for t in range(CT):
                        lhsT = oT[c][:, t // R, :].rearrange("d (p r) -> d r p", r=R)[:, t % R, :]
                        last = mm(PA[c % 2][:, t, :], lhsT, top.wo4T[:, :])
                    last.then_inc(sm["proj"], 1)

                def h_by_channel(c):
                    pe.wait_ge(sm["h"], c + 1)
                    for t in range(CT):
                        last = nc.tensor.transpose(PA[c % 2][:, t, :], h[c][:, t, :], top.ident[:, :])
                    last.then_inc(sm["hT_psum"], 1)

                tokens = lambda c, t: hT[c][:, t // 4, 128 * (t % 4):128 * (t % 4) + 128]

                def gate(c):
                    pe.wait_ge(sm["hT"], c + 1)
                    for t in range(CT):
                        last = mm(PA[c % 2][:, 0, NE * t:NE * t + NE], tokens(c, t), top.gate_expT[:, 0:NE])
                    last.then_inc(sm["logits"], 1)

                for u in TURNS:
                    if 0 <= u < TILES:
                        if u >= 2:
                            pe.wait_ge(sm["scaled_a" if u % 2 else "scaled_d"], u // 2)
                        for a in two:
                            last = mm(PE_[u % 2][:, 4 * a:4 * a + 4, :], tokens(u // CT, u % CT),
                                      top.gate_expT[:, NE + 512 * a:NE + 512 * a + 512])
                        last.then_inc(sm["exp_psum"], 1)
                    for step, c in due(u, PE_STEPS):
                        if step == "attention_by_channel":
                            attention_by_channel(c)
                        if step == "project":
                            project(c)
                        if step == "h_by_channel":
                            h_by_channel(c)
                        if step == "gate":
                            gate(c)
        ph.close()


def sandwich(nc, dram, out):
    with ExitStack() as ctx:
        top = Phase(nc, ctx)
        top.X = top.sb("X", [128, TILES, D])
        top.N3 = top.sb("N3", [128, TILES, D])
        top.N4 = top.N3
        top.V4 = top.sb("V4", [128, TILES, KV4, VW])
        top.O4 = top.sb("O4", [128, TILES, D])
        top.ident = top.sb("ident", [128, 128])
        top.ident_bf = top.sb("ident_bf", [128, 128], BF16)
        top.eps = top.sb("eps", [128, 1])
        top.eps_rms = top.sb("eps_rms", [128, 1])
        top.hadamard = top.sb("hadamard", [128, D])
        top.ternT = top.sb("ternT", [128, 3, D], BF16)
        top.w_qmeanT = top.sb("w_qmeanT", [128, DH])
        top.ln_gb = top.sb("ln_gb", [DH, 2])
        top.w1T = top.sb("w1T", [DH, PROJ])
        top.b1 = top.sb("b1", [PROJ, 1])
        top.w2T = top.sb("w2T", [PROJ, 1])
        top.b2 = top.sb("b2", [1, 1])
        top.w_qkvT = top.sb("w_qkvT", [128, 3 * HEADS * DH])
        top.w_outT = top.sb("w_outT", [128, HEADS // 2, D])
        top.b_out = top.sb("b_out", [B, D])
        top.iota = top.sb("iota", [128, TOP_K + 1])
        top.iota_col = top.sb("iota_col", [128, 1])
        top.batch_rows = top.sb("batch_rows", [B, 2, 128])
        top.batch_rows_bf = top.sb("batch_rows_bf", [B, 2, 128], BF16)
        top.first_row = top.sb("first_row", [128, 128])
        top.lower_f = top.sb("lower_f", [128, 128])
        top.lower = top.sb("lower", [128, 128], BF16)
        top.ones_bf = top.sb("ones_bf", [128, 128], BF16)
        top.selT = [top.sb(f"selT{Q}", [128, S]) for Q in range(2)]
        top.Y = [top.sb(f"Y{Q}", [128, D]) for Q in range(2)]
        top.yU = [top.sb(f"yU{Q}", [128, D]) for Q in range(2)]
        top.qkv4T = top.sb("qkv4T", [128, D + 2 * KVD])
        top.wq4T, top.wk4T, top.wv4T = (top.qkv4T[:, 0:D], top.qkv4T[:, D:D + KVD], top.qkv4T[:, D + KVD:D + 2 * KVD])
        top.wo4T = top.sb("wo4T", [128, D])
        top.gate_expT = top.sb("gate_expT", [128, NE + NE * D])
        top.norm_w = top.sb("norm_w", [128, 2])
        top.mask_f = top.sb("mask_f", [128, 128])
        top.mask_bf = top.sb("mask_bf", [128, 128], BF16)
        dilated_and_ternary_phase(nc, top, dram)
        gated_attention_phase(nc, top, dram)
        projection_phase(nc, top, dram)
        causal_attention_phase(nc, top, dram)
        experts_phase(nc, top, dram, out)


def kernel(**inputs):
    import numpy as np
    import concourse.bacc as bacc
    from concourse.bass_utils import run_bass_kernel_spmd

    def hadamard(size):
        h = np.array([[1.0]], dtype=np.float64)
        while h.shape[0] < size:
            h = np.block([[h, h], [h, -h]])
        return (h / np.sqrt(size)).astype(np.float32)

    a = {k: np.asarray(v) for k, v in inputs.items()}
    by_channel = lambda w: w.reshape(-1, HD4, D).transpose(1, 0, 2).reshape(-1, D)
    col = lambda v: np.ascontiguousarray(v.reshape(-1, 1))
    arrays = {
        "x": a["L0_attn_x"].reshape(B, 128, R, D).transpose(1, 0, 2, 3).reshape(128, TILES, D),
        "ffn_weight": a["L0_ffn_weight"],
        "w_qkvT": a["L1_attn_w_qkv"].T,
        "ln_gb": np.stack([a["L1_attn_ln_g"], a["L1_attn_ln_b"]], axis=1),
        "w1T": a["L1_attn_w1"].T,
        "b1": col(a["L1_attn_b1"]),
        "w2T": a["L1_attn_w2"].T,
        "b2": col(a["L1_attn_b2"]),
        "ident": np.eye(128, dtype=np.float32),
        "hadamard": hadamard(D),
        "w_outT": a["L1_attn_w_out"].T.reshape(HEADS // 2, 128, D).transpose(1, 0, 2),
        "b_out": np.broadcast_to(a["L1_attn_b_out"], (B, D)),
        "qkv4T": np.concatenate([by_channel(a["L1_ffn_wq"]), by_channel(a["L1_ffn_wk"]), a["L1_ffn_wv"]]).T,
        "wo4T": a["L1_ffn_wo"].T,
        "gate_expT": np.concatenate([a["L1_ffn_gate_w"], a["L1_ffn_expert_w"].reshape(NE * D, D)]).T,
        "norm_w": np.stack([a["L1_ffn_attn_norm_w"], a["L1_ffn_ffn_norm_w"]], axis=1),
        "iota": np.tile(np.arange(TOP_K + 1, dtype=np.float32), (128, 1)),
        "iota_col": (np.arange(128) % TOP_K).astype(np.float32).reshape(128, 1),
        "batch_rows": (np.arange(B)[:, None] == np.arange(2 * 128)[None] // TOP_K).astype(np.float32).reshape(B, 2, 128),
        "first_row": np.repeat((np.arange(128) % TOP_K == 0).astype(np.float32)[:, None], 128, axis=1),
        "lower": np.triu(np.ones((128, 128), np.float32), 1),
        "mask": np.triu(np.full((128, 128), -1e30, np.float32), 1),
    }
    nc = bacc.Bacc("TRN2", target_bir_lowering=False, num_devices=1)
    dram, send = {}, {}
    for name, v in arrays.items():
        send[f"in_{name}_dram"] = np.ascontiguousarray(v)
        dram[name] = nc.dram_tensor(f"in_{name}_dram", v.shape, mybir.dt.from_np(v.dtype), kind="ExternalInput").ap()
    dram["scores"] = nc.dram_tensor("scores", (1, B * S), FP32, kind="Internal").ap()
    q_stack = nc.dram_tensor("q_stack", (B + 1, SLOTS, HD4, HEADS, S), BF16, kind="Internal").ap()
    k_stack = nc.dram_tensor("k_stack", (B + 1, SLOTS, HD4, KV4, S), BF16, kind="Internal").ap()
    m_rows = nc.dram_tensor("m_rows", (2, 3, 2, HEADS // 2, S), BF16, kind="Internal").ap()

    def stack_load(stack):
        return lambda b, head, n: stack[bass.ds(b, 1), :, :, head:head + n, :].rearrange("o j d h t -> (o j d) h t")

    def stack_store(stack):
        return lambda b, slot, n: stack[b, slot:slot + n].rearrange("j d h t -> (d h) j t")

    dram["q_load"], dram["k_load"] = stack_load(q_stack), stack_load(k_stack)
    dram["q_store"], dram["k_store"] = stack_store(q_stack), stack_store(k_stack)
    dram["m_store"] = lambda c: m_rows[c].rearrange("k a i t -> (k a i) t")
    dram["m_load"] = lambda c, a: m_rows[c, :, a, :, :]
    out = nc.dram_tensor("out_0_dram", (128, TILES, D), FP32, kind="ExternalOutput").ap()
    sandwich(nc, dram, out)
    got = run_bass_kernel_spmd(nc, [send], core_ids=[0]).results[0]["out_0_dram"]
    return got.reshape(128, B, R, D).transpose(1, 0, 2, 3).reshape(B, S, D)
```
